# Optimizing a Trainium2 kernel written in Bass

```python
import numpy as np
import jax
import jax.numpy as jnp

def _softmax(x, axis=-1):
    return jax.nn.softmax(x, axis=axis)

def _gelu(x):
    return jax.nn.gelu(x, approximate=True)

def _silu(x):
    return jax.nn.silu(x)

def _sigmoid(x):
    return jax.nn.sigmoid(x)

def _layernorm(x, axis=-1, eps=1e-05):
    m = jnp.mean(x, axis=axis, keepdims=True)
    v = jnp.var(x, axis=axis, keepdims=True)
    return (x - m) / jnp.sqrt(v + eps)

def _scatter_add(tgt, idx, src, axis=0):
    return tgt.at[idx].add(src)

def _segment_sum(src, seg, n):
    return jax.ops.segment_sum(src, seg, n)
kernel_name = 'mk_seq_postln_d2_jaxref_r8_374d21'

def setup_inputs(seed: int=0):
    np.random.seed(seed)
    _w = jnp.asarray

    def _L0_attn_setup():
        import jax, jax.numpy as jnp
        import numpy as np
        import math
        EMBED_DIM = 128
        NUM_HEADS = 16
        HEAD_DIM = EMBED_DIM // NUM_HEADS
        key = jax.random.key(seed)
        ks = jax.random.split(key, 5)
        B, S, D = (2, 256, EMBED_DIM)
        s = 1.0 / math.sqrt(D)
        x = jax.random.normal(ks[0], (B, S, D), dtype=jnp.float32)
        W_qkv = jax.random.normal(ks[1], (3 * D, D), dtype=jnp.float32) * s
        b_qkv = jax.random.normal(ks[2], (3 * D,), dtype=jnp.float32) * 0.01
        W_out = jax.random.normal(ks[3], (D, D), dtype=jnp.float32) * s
        b_out = jax.random.normal(ks[4], (D,), dtype=jnp.float32) * 0.01
        return {'x': x, 'W_qkv': W_qkv, 'b_qkv': b_qkv, 'W_out': W_out, 'b_out': b_out}
    _L0_attn_in = _L0_attn_setup()

    def _L0_ffn_setup():
        import jax, jax.numpy as jnp
        import numpy as np
        from jax import lax
        D_MODEL = 128
        INTER = 128
        N_EXPERTS = 8
        TOP_K = 2
        ROUTE_SCALE = 1.0
        B, S = (2, 512)
        key = jax.random.key(seed)
        ks = jax.random.split(key, 16)
        sc_d = 1.0 / np.sqrt(D_MODEL)
        sc_f = 1.0 / np.sqrt(INTER)
        inp = {'x': jax.random.normal(ks[0], (B, S, D_MODEL), dtype=jnp.float32), 'gate_w': jax.random.normal(ks[1], (N_EXPERTS, D_MODEL), dtype=jnp.float32) * sc_d, 'w1': jax.random.normal(ks[2], (N_EXPERTS, D_MODEL, INTER), dtype=jnp.float32) * sc_d, 'b1': jnp.zeros((N_EXPERTS, INTER), dtype=jnp.float32), 'w2': jax.random.normal(ks[3], (N_EXPERTS, INTER, D_MODEL), dtype=jnp.float32) * sc_f, 'b2': jnp.zeros((N_EXPERTS, D_MODEL), dtype=jnp.float32), 'w3': jax.random.normal(ks[4], (N_EXPERTS, D_MODEL, INTER), dtype=jnp.float32) * sc_d, 'b3': jnp.zeros((N_EXPERTS, INTER), dtype=jnp.float32), 'sw1': jax.random.normal(ks[5], (D_MODEL, INTER), dtype=jnp.float32) * sc_d, 'sb1': jnp.zeros((INTER,), dtype=jnp.float32), 'sw2': jax.random.normal(ks[6], (INTER, D_MODEL), dtype=jnp.float32) * sc_f, 'sb2': jnp.zeros((D_MODEL,), dtype=jnp.float32), 'sw3': jax.random.normal(ks[7], (D_MODEL, INTER), dtype=jnp.float32) * sc_d, 'sb3': jnp.zeros((INTER,), dtype=jnp.float32)}
        return inp
    _L0_ffn_in = _L0_ffn_setup()

    def _L1_attn_setup():
        import jax, jax.numpy as jnp
        import numpy as np
        N_SCALES = 11
        N_TAPS = 4
        OFFSETS = [(1 << j) * tau for j in range(N_SCALES) for tau in range(N_TAPS)]

        def _shift(a, off):
            N = a.shape[2]
            return jnp.pad(a[:, :, :N - off], ((0, 0), (0, 0), (off, 0), (0, 0)))
        key = jax.random.key(seed)
        ks = jax.random.split(key, 8)
        B, N, D, H = (4, 512, 128, 16)
        w_scale = 0.02
        return {'x': jax.random.normal(ks[0], (B, N, D), jnp.float32), 'w_qkv': jax.random.normal(ks[1], (D, 3 * D), jnp.float32) * w_scale, 'b_qkv': jnp.zeros((3 * D,), jnp.float32), 'w_out': jax.random.normal(ks[2], (D, D), jnp.float32) * w_scale, 'b_out': jnp.zeros((D,), jnp.float32), 'w_gate': jax.random.normal(ks[3], (D, D), jnp.float32) * w_scale, 'b_gate': 2.0 * jnp.ones((D,), jnp.float32), 'pos_bias': jax.random.normal(ks[4], (len(OFFSETS), H), jnp.float32) * 0.1}
    _L1_attn_in = _L1_attn_setup()

    def _L1_ffn_setup():
        import jax, jax.numpy as jnp
        import numpy as np
        NUM_EXPERTS = 8
        TOP_K = 2
        N_EMBD = 128
        B, T = (4, 256)
        key = jax.random.key(seed)
        k_x, k_g, k_e = jax.random.split(key, 3)
        x = jax.random.normal(k_x, (B, T, N_EMBD), dtype=jnp.float32)
        scale = 1.0 / np.sqrt(N_EMBD)
        gate_w = jax.random.uniform(k_g, (NUM_EXPERTS, N_EMBD), dtype=jnp.float32, minval=-scale, maxval=scale)
        expert_w = jax.random.uniform(k_e, (NUM_EXPERTS, N_EMBD, N_EMBD), dtype=jnp.float32, minval=-scale, maxval=scale)
        return {'x': x, 'gate_w': gate_w, 'expert_w': expert_w}
    _L1_ffn_in = _L1_ffn_setup()
    _d = {'L0_attn_x': _L0_attn_in['x'], 'L0_attn_W_qkv': _L0_attn_in['W_qkv'], 'L0_attn_b_qkv': _L0_attn_in['b_qkv'], 'L0_attn_W_out': _L0_attn_in['W_out'], 'L0_attn_b_out': _L0_attn_in['b_out'], 'L0_ffn_gate_w': _L0_ffn_in['gate_w'], 'L0_ffn_w1': _L0_ffn_in['w1'], 'L0_ffn_b1': _L0_ffn_in['b1'], 'L0_ffn_w2': _L0_ffn_in['w2'], 'L0_ffn_b2': _L0_ffn_in['b2'], 'L0_ffn_w3': _L0_ffn_in['w3'], 'L0_ffn_b3': _L0_ffn_in['b3'], 'L0_ffn_sw1': _L0_ffn_in['sw1'], 'L0_ffn_sb1': _L0_ffn_in['sb1'], 'L0_ffn_sw2': _L0_ffn_in['sw2'], 'L0_ffn_sb2': _L0_ffn_in['sb2'], 'L0_ffn_sw3': _L0_ffn_in['sw3'], 'L0_ffn_sb3': _L0_ffn_in['sb3'], 'L1_attn_w_qkv': _L1_attn_in['w_qkv'], 'L1_attn_b_qkv': _L1_attn_in['b_qkv'], 'L1_attn_w_out': _L1_attn_in['w_out'], 'L1_attn_b_out': _L1_attn_in['b_out'], 'L1_attn_w_gate': _L1_attn_in['w_gate'], 'L1_attn_b_gate': _L1_attn_in['b_gate'], 'L1_attn_pos_bias': _L1_attn_in['pos_bias'], 'L1_ffn_gate_w': _L1_ffn_in['gate_w'], 'L1_ffn_expert_w': _L1_ffn_in['expert_w']}
    _x0 = _d['L0_attn_x']
    _d['L0_attn_x'] = jax.random.normal(jax.random.fold_in(jax.random.key(seed), 1), (32, 256, 128), dtype=_x0.dtype)
    del _x0
    return _d

def reference(L0_attn_x, L0_attn_W_qkv, L0_attn_b_qkv, L0_attn_W_out, L0_attn_b_out, L0_ffn_gate_w, L0_ffn_w1, L0_ffn_b1, L0_ffn_w2, L0_ffn_b2, L0_ffn_w3, L0_ffn_b3, L0_ffn_sw1, L0_ffn_sb1, L0_ffn_sw2, L0_ffn_sb2, L0_ffn_sw3, L0_ffn_sb3, L1_attn_w_qkv, L1_attn_b_qkv, L1_attn_w_out, L1_attn_b_out, L1_attn_w_gate, L1_attn_b_gate, L1_attn_pos_bias, L1_ffn_gate_w, L1_ffn_expert_w):

    def _L0_attn_ref(x, W_qkv, b_qkv, W_out, b_out):
        import jax, jax.numpy as jnp
        import numpy as np
        import math
        EMBED_DIM = 128
        NUM_HEADS = 16
        HEAD_DIM = EMBED_DIM // NUM_HEADS
        B, S, D = x.shape
        H, Hd = (NUM_HEADS, HEAD_DIM)
        slopes = jnp.power(2.0, 8.0 * jnp.arange(0, -H, -1, dtype=jnp.float32) / H)
        qkv = x @ W_qkv.T + b_qkv
        qkv = qkv.reshape(B, S, 3, H, Hd).transpose(2, 0, 3, 1, 4)
        q, k, v = (qkv[0], qkv[1], qkv[2])
        scores = jnp.einsum('bhqd,bhkd->bhqk', q, k) / math.sqrt(Hd)
        pos = jnp.arange(S)
        rel = jnp.abs(pos[None, :] - pos[:, None]).astype(jnp.float32)
        bias = -slopes[:, None, None] * rel
        probs = jax.nn.softmax(scores + bias[None], axis=-1)
        out = jnp.einsum('bhqk,bhkd->bhqd', probs, v)
        out = out.transpose(0, 2, 1, 3).reshape(B, S, D)
        return out @ W_out.T + b_out

    def _L0_ffn_ref(x, gate_w, w1, b1, w2, b2, w3, b3, sw1, sb1, sw2, sb2, sw3, sb3):
        import jax, jax.numpy as jnp
        import numpy as np
        from jax import lax
        D_MODEL = 128
        INTER = 128
        N_EXPERTS = 8
        TOP_K = 2
        ROUTE_SCALE = 1.0
        B, S = (2, 512)
        Bx, Sx, D = x.shape
        xt = x.reshape(-1, D)
        scores = jax.nn.softmax((xt @ gate_w.T).astype(jnp.float32), axis=-1)
        top_vals, top_idx = lax.top_k(scores, TOP_K)
        weights = (top_vals * ROUTE_SCALE).astype(x.dtype)
        combine = jnp.sum(jax.nn.one_hot(top_idx, N_EXPERTS, dtype=x.dtype) * weights[..., None], axis=1)

        def body(acc, p):
            W1, B1, W2, B2, W3, B3, c = p
            h = jax.nn.silu(xt @ W1 + B1) * (xt @ W3 + B3)
            return (acc + c[:, None] * (h @ W2 + B2), None)
        y, _ = lax.scan(body, jnp.zeros_like(xt), (w1, b1, w2, b2, w3, b3, combine.T))
        z = jax.nn.silu(xt @ sw1 + sb1) * (xt @ sw3 + sb3) @ sw2 + sb2
        return (y + z).reshape(Bx, Sx, D)

    def _L1_attn_ref(x, w_qkv, b_qkv, w_out, b_out, w_gate, b_gate, pos_bias):
        import jax, jax.numpy as jnp
        import numpy as np
        N_SCALES = 11
        N_TAPS = 4
        OFFSETS = [(1 << j) * tau for j in range(N_SCALES) for tau in range(N_TAPS)]

        def _shift(a, off):
            N = a.shape[2]
            return jnp.pad(a[:, :, :N - off], ((0, 0), (0, 0), (off, 0), (0, 0)))
        B, N, D = x.shape
        H = pos_bias.shape[1]
        HD = D // H
        scale = HD ** (-0.5)
        qkv = x @ w_qkv + b_qkv
        q, k, v = jnp.split(qkv, 3, axis=-1)
        q = q.reshape(B, N, H, HD).transpose(0, 2, 1, 3)
        k = k.reshape(B, N, H, HD).transpose(0, 2, 1, 3)
        v = v.reshape(B, N, H, HD).transpose(0, 2, 1, 3)
        scores = []
        for off in OFFSETS:
            if off == 0:
                ks_ = k
            elif off >= N:
                ks_ = jnp.zeros_like(k)
            else:
                ks_ = _shift(k, off)
            scores.append(jnp.einsum('bhnd,bhnd->bhn', q, ks_) * scale)
        scores = jnp.stack(scores, axis=-1)
        scores = scores + pos_bias.T[None, :, None, :]
        attn = jax.nn.softmax(scores, axis=-1)
        out = jnp.zeros_like(q)
        for i, off in enumerate(OFFSETS):
            if off >= N:
                continue
            vs = v if off == 0 else _shift(v, off)
            out = out + attn[..., i:i + 1] * vs
        gathered = out.transpose(0, 2, 1, 3).reshape(B, N, D)
        gate = jax.nn.sigmoid(x @ w_gate + b_gate)
        return gathered * gate @ w_out + b_out

    def _L1_ffn_ref(x, gate_w, expert_w):
        import jax, jax.numpy as jnp
        import numpy as np
        NUM_EXPERTS = 8
        TOP_K = 2
        N_EMBD = 128
        B, T = (4, 256)
        Bb, Tt, C = x.shape
        xf = x.reshape(Bb * Tt, C)
        logits = xf @ gate_w.T
        w, sel = jax.lax.top_k(logits, TOP_K)
        w = jax.nn.softmax(w.astype(jnp.float32), axis=1).astype(xf.dtype)
        n = xf.shape[0]
        w_full = jnp.zeros((n, NUM_EXPERTS), dtype=xf.dtype)
        w_full = w_full.at[jnp.arange(n)[:, None], sel].add(w)
        expert_out = jnp.einsum('nc,edc->ned', xf, expert_w)
        out = jnp.einsum('ne,ned->nd', w_full, expert_out)
        return out.reshape(Bb, Tt, C)
    x = L0_attn_x
    x = _layernorm(x + _L0_attn_ref(x, L0_attn_W_qkv, L0_attn_b_qkv, L0_attn_W_out, L0_attn_b_out), axis=-1)
    x = _layernorm(x + _L0_ffn_ref(x, L0_ffn_gate_w, L0_ffn_w1, L0_ffn_b1, L0_ffn_w2, L0_ffn_b2, L0_ffn_w3, L0_ffn_b3, L0_ffn_sw1, L0_ffn_sb1, L0_ffn_sw2, L0_ffn_sb2, L0_ffn_sw3, L0_ffn_sb3), axis=-1)
    x = _layernorm(x + _L1_attn_ref(x, L1_attn_w_qkv, L1_attn_b_qkv, L1_attn_w_out, L1_attn_b_out, L1_attn_w_gate, L1_attn_b_gate, L1_attn_pos_bias), axis=-1)
    x = _layernorm(x + _L1_ffn_ref(x, L1_ffn_gate_w, L1_ffn_expert_w), axis=-1)
    return x

_drawn_inputs = setup_inputs


def setup_inputs(seed=0):
    import zlib

    import numpy as np

    out = dict(_drawn_inputs(seed))
    spreads = {'L0_ffn_b1': (0.0, 0.1),
     'L0_ffn_b2': (0.0, 0.1),
     'L0_ffn_b3': (0.0, 0.1),
     'L0_ffn_sb1': (0.0, 0.1),
     'L0_ffn_sb2': (0.0, 0.1),
     'L0_ffn_sb3': (0.0, 0.1),
     'L1_attn_b_qkv': (0.0, 0.1),
     'L1_attn_b_out': (0.0, 0.1),
     'L1_attn_b_gate': (2.0, 0.6)}
    factors = {'L1_attn_w_gate': 8.0, 'L1_attn_pos_bias': 23.608}
    for name, (base, spread) in spreads.items():
        noise = np.random.default_rng([zlib.crc32(name.encode()), seed]).standard_normal(out[name].shape)
        drawn = base * np.exp(spread * noise) if base else spread * noise
        out[name] = jnp.asarray(drawn.astype(out[name].dtype))
    for name, factor in factors.items():
        out[name] = (out[name] * factor).astype(out[name].dtype)
    return out
```

```python
import concourse.bass as bass
from concourse import mybir
from contextlib import ExitStack
import numpy as np

B, T, D = 32, 256, 128
H, HD = 16, 8
E = 8
TT = T // 128
EPS = 1e-5

N_SCALES, N_TAPS = 11, 4
OFFSETS = [(1 << j) * tau for j in range(N_SCALES) for tau in range(N_TAPS)]
SHIFTS = sorted({o for o in OFFSETS if o < T})
PAIRS = [(SHIFTS[2 * p + 1], SHIFTS[2 * p]) for p in range(len(SHIFTS) // 2)]
NP = len(PAIRS)
NS = len(SHIFTS)
PAD = max(SHIFTS)
DUP = max(sum(o == s for o in OFFSETS) for s in SHIFTS)
OOB = [i for i, o in enumerate(OFFSETS) if o >= T]

ROW_D, ROW_M = 9 * HD, 96

LAG = {"A1": 0, "M": 1, "A2": 1, "A3": 2, "B": 2, "C1": 3, "C2": 4, "D": 5}
LAST = max(LAG.values())
LOOP_FROM = LAST + 1
SLOTS = 20


class Steps:

    def __init__(self, sem, steps):
        self.sem, self.names = sem, []
        for s in steps.split():
            name, _, n = s.partition("*")
            self.names += [(name, i) for i in range(int(n or 1))]
        self.per_run = len(self.names)
        self.at = 0

    def done(self, name, i=0):
        assert self.names[self.at] == (name, i), (self.names[self.at], name, i)
        self.at = (self.at + 1) % self.per_run
        return self.sem

    def count(self, e, name, i=0):
        return 0 if isinstance(e, int) and e < 0 else e * self.per_run + (self.names.index((name, i)) + 1)


def dma_count(e, per_run=1):
    return 0 if isinstance(e, int) and e < 0 else (e + 1) * (16 * per_run)


def network(nc, A, out):
    F, BF, H16, I32, U16 = (mybir.dt.float32, mybir.dt.bfloat16, mybir.dt.float16, mybir.dt.int32,
                            mybir.dt.uint16)
    ALU, ACT, AX = mybir.AluOpType, mybir.ActivationFunctionType, mybir.AxisListType
    ctx = ExitStack()
    with ctx:
        def sb(name, shape, dt=F):
            return ctx.enter_context(nc.sbuf_tensor(name, shape, dt))

        def bank(name):
            return ctx.enter_context(nc.psum_tensor(name, [128, 512], F))

        def sem(name):
            return ctx.enter_context(nc.semaphore(name))

        def steps(name, s):
            return Steps(sem(name), s)

        wqk0, wv0, wo0 = sb("wqk0", [128, 2, 128]), sb("wv0", [128, 128]), sb("wo0", [128, 128])
        bqk0, bv0, bo0 = sb("bqk0", [128, 2]), sb("bv0", [128, TT, 128]), sb("bo0", [128, TT, 128])
        gw0, gw1 = sb("gw0", [128, E]), sb("gw1", [128, E])
        w13, w2 = sb("w13", [128, E + 1, 2, 128]), sb("w2", [128, E + 1, 128])
        b1, b1h, b3, b2 = sb("b1", [128, E + 1]), sb("b1h", [128, E + 1]), sb("b3", [128, E + 1]), sb("b2", [128, TT, 128])
        wc, bc = sb("wc", [128, 4, 128]), sb("bc", [128, 4])
        woc, boc = sb("woc", [128, 128]), sb("boc", [128, TT, 128])
        ew = sb("ew", [128, E, 128])
        ident, identb, identh = sb("ident", [128, 128]), sb("identb", [128, 128], BF), sb("identh", [128, 128], H16)
        dist = sb("dist", [128, H, 2, 128], H16)
        onesz, hsum = sb("onesz", [128, 4, 32]), sb("hsum", [128, 2, 32])
        tri = sb("tri", [128, TT * E * E])
        posd, oobd = sb("posd", [128, 2, DUP]), sb("oobd", [128, H, len(OOB)])
        posm, poss, posE = sb("posm", [128, 2]), sb("poss", [128, 2]), sb("posE", [128, 2])
        oobm, oobs, oobE = sb("oobm", [128, H]), sb("oobs", [128, H]), sb("oobE", [128, H])

        xT = sb("xT", [128, T])
        x0, x2b = sb("x0", [128, TT, D]), sb("x2b", [128, TT, D])
        x0b = x0
        qk = sb("qk", [128, 2, T])
        rest = qk
        parts = sb("parts", [128, 2, 3, T], BF)
        stack = [sb(f"stack{i}", [ROW_M + 1, 2, H, T], BF) for i in range(2)]
        Vz = [sb(f"Vz{i}", [128, TT, 4, 160]) for i in range(2)]
        mx, mneg, mT = sb("mx", [128, TT, H]), sb("mneg", [128, TT, H], BF), sb("mT", [H, T], BF)
        P = [sb(f"P{i}", [128, TT, T]) for i in range(8)]
        rden, attnT = sb("rden", [128, T]), sb("attnT", [128, T])
        x1, x2, x3 = ([sb(f"x{n}_{i}", [128, TT, D]) for i in range(2)] for n in (1, 2, 3))
        xout = sb("xout", [128, TT, D])

        def norm_buffers(n):
            return dict(y=sb(n + "y", [128, TT, D]), st=sb(n + "st", [128, TT, 6]), mv=sb(n + "mv", [128, TT, 2]),
                        v=sb(n + "v", [128, TT]), i=sb(n + "i", [128, TT], I32), r=sb(n + "r", [128, TT]),
                        s=sb(n + "s", [128, TT]), tick=sb(n + "tick", [128, TT]))

        def gate_buffers(n):
            return dict(L=sb(n + "L", [128, TT, E]), mx=sb(n + "mx", [128, TT]), dl=sb(n + "dl", [128, TT, E]),
                        gt=sb(n + "gt", [128, TT * E * E]), eq=sb(n + "eq", [128, TT * E * E]),
                        rank=sb(n + "rank", [128, TT, E]), ge=sb(n + "ge", [128, TT, E]),
                        sel=sb(n + "sel", [128, TT, E]), sum=sb(n + "sum", [128, TT]), rec=sb(n + "rec", [128, TT]),
                        c=sb(n + "c", [128, TT, 64]), cT=sb(n + "cT", [128, 128]),
                        cb=sb(n + "cb", [128, TT, E, 128]))

        nA, nB, nC, nD = (norm_buffers("n" + n) for n in "ABCD")
        gB, gD = gate_buffers("gB"), gate_buffers("gD")
        x1T = sb("x1T", [128, T])
        th, bb, wa, ub = ([sb(f"{n}{i}", [128, T]) for i in range(2)] for n in ("th", "bb", "wa", "ub"))
        h9 = sb("h9", [128, E + 1, T])
        x2T, qC, kC = sb("x2T", [128, T]), sb("qC", [128, T]), sb("kC", [128, PAD + T])
        vC = [sb(f"vC{i}", [128, PAD + T]) for i in range(2)]
        tg = [sb(f"tg{i}", [128, T]) for i in range(2)]
        prod = sb("prod", [128, NS, T])
        ds = sb("ds", [128, TT, NS + 1, H])
        es = ds
        mC, mC2, sC, rC = (sb(n, [128, TT, H]) for n in ("mC", "mC2", "sC", "rC"))
        wn, wT = sb("wn", [128, TT, NS, H]), sb("wT", [128, 2, T])
        scs = wT
        wb = sb("wb", [128, NS, T])
        pv = wb
        gat = sb("gat", [128, T])
        x3T = sb("x3T", [128, T])
        xs = prod

        bS, bST = [bank("bS0"), bank("bS1")], [bank("bT0"), bank("bT1")]
        bPV, bAB, b6, b7 = bank("bPV"), bank("bAB"), bank("b6"), bank("b7")

        d_parts = nc.dram_tensor("d_parts", (2, 3, 128, T), BF, kind="Internal").ap()
        d_w = nc.dram_tensor("d_w", (2, 128, T), F, kind="Internal").ap()
        d_cB = nc.dram_tensor("d_cB", (TT, E, 128), F, kind="Internal").ap()
        d_cD = nc.dram_tensor("d_cD", (TT, E, 128), F, kind="Internal").ap()

        LN = "res bn*2 ag*2 ve sh mg nt*9 nm*2"
        GATE = "cp gmx sub gt eq eqt add rank sel sum rec c"
        peA1 = steps("peA1", "qk v S*16")
        peM = steps("peM", "mT")
        peA2, pePV = steps("peA2", "ST*16"), steps("pePV", "PV*4")
        peA3 = steps("peA3", "out")
        peB = steps("peB", "xT lg cT ab*9 z")
        peC1 = steps("peC1", "xT qk vg sc scT wT")
        peC2 = steps("peC2", "out")
        peD = steps("peD", "xT lg cT y")
        actA1 = steps("actA1", "q k")
        actM = steps("actM", "mT")
        actA2 = steps("actA2", "exp*16")
        actB = steps("actB", "xT ge cT ab*18")
        actC1 = steps("actC1", "xT q k v g exp wT")
        actD = steps("actD", "xT ge cT")
        dveA1 = steps("dveA1", "hi rest mid lo v max*16")
        dveM = steps("dveM", "neg")
        dveA3 = steps("dveA3", "rec num " + LN)
        dveBg = steps("dveBg", GATE)
        dveB = steps("dveB", "wu*18")
        dveBn = steps("dveBn", LN)
        dveC1 = steps("dveC1", "sc*2 mx m2 sub subo sum rec w")
        dveC2 = steps("dveC2", "pv*8")
        dveC2n = steps("dveC2n", "gt " + LN)
        dveDg = steps("dveDg", GATE)
        dveDn = steps("dveDn", LN)
        poolA3 = steps("poolA3", "xbo")
        poolB = steps("poolB", "h*9")
        poolC1 = steps("poolC1", "prod*8")
        poolC2 = steps("poolC2", "xb add*5")
        poolD = steps("poolD", "xs*4")
        ld_const, ld_xT, ld_x = sem("ld_const"), sem("ld_xT"), sem("ld_x")
        st_parts, ld_stack, ld_m = sem("st_parts"), sem("ld_stack"), sem("ld_m")
        st_cB, ld_cB, st_cD, ld_cD = sem("st_cB"), sem("ld_cB"), sem("st_cD"), sem("ld_cD")
        st_w, ld_w, st_out = sem("st_w"), sem("ld_w"), sem("st_out")
        setup_dve, setup_act = sem("setup_dve"), sem("setup_act")
        SETUP_DVE, SETUP_ACT = 18, 9
        N_STACK, N_W = 12, HD

        consts = [(wqk0, "wqk0"), (wv0, "wv0"), (wo0, "wo0"), (bqk0, "bqk0"), (gw0, "gw0"), (gw1, "gw1"),
                  (w13, "w13"), (w2, "w2"), (b1, "b1"), (b3, "b3"), (b2, "b2"), (wc, "wc"), (bc, "bc"), (woc, "woc"),
                  (ew, "ew"), (ident, "ident"), (identh, "identh"), (dist, "dist"),
                  (onesz, "onesz"), (hsum, "hsum"), (tri, "tri"), (posd, "posd"), (oobd, "oobd")]
        N_CONST = len(consts) + 1 + 3 * TT + 4

        x_rows = A["x"].rearrange("b (t p) c -> p (b t) c", p=128)
        out_rows = out.rearrange("b (t p) c -> p (b t) c", p=128)

        def head(k):
            return 4 * (k % 4) + k // 4

        def expert(n):
            return E if n == 0 else n - 1

        def shifted(x, p):
            hi, lo = PAIRS[p]
            return bass.AP(x, PAD - hi, [[PAD + T, 128], [hi - lo, 2], [1, T]])

        def stages(t):
            r = {}
            for s, lag in LAG.items():
                e = t - lag
                r[s] = None if isinstance(e, int) and not 0 <= e < B else e
            return r

        def passes(eng, one):
            for t in range(LOOP_FROM):
                one(t, t % 2, t)
            with eng.Fori(0, (B - LOOP_FROM) // 2) as r:
                for u in range(2):
                    one(r * 2 + (LOOP_FROM + u), (LOOP_FROM + u) % 2, LOOP_FROM + u)
            for t in range(B, B + LAST):
                one(t, t % 2, t)

        block = ctx.enter_context(nc.Block())

        @block.sync
        def _(sp):
            for dst, name in consts:
                sp.dma_start(dst[:], A[name]).then_inc(ld_const, 16)
            sp.dma_start(identb[:].bitcast(U16), A["identb"]).then_inc(ld_const, 16)
            for tt in range(TT):
                for dst, name in ((bv0, "bv0"), (bo0, "bo0"), (boc, "boc")):
                    sp.dma_start(dst[:, tt, :], bass.AP(A[name].tensor, 0, [[0, 128], [1, 128]])).then_inc(ld_const, 16)
            for i in range(2):
                for s in range(2):
                    n = ROW_M + s - ROW_D
                    sp.dma_start(stack[i][ROW_D:ROW_D + n, s].bitcast(U16),
                                 A["rows"][0:n, s]).then_inc(ld_const, 16)

            def one(t, par, key):
                r = stages(t)
                for g in range(SLOTS):
                    if g == 0:
                        if (e := r["A1"]) is not None:
                            sp.wait_ge(peA1.sem, peA1.count(e - 1, "v"))
                            sp.dma_start(xT[:], A["xT"][:, bass.ds(e * T, T)]).then_inc(ld_xT, 16)
                        if (e := r["A3"]) is not None:
                            sp.wait_ge(dveA3.sem, dveA3.count(e - 1, "res"))
                            sp.dma_start(x0[:], x_rows[:, bass.ds(e * TT, TT), :]).then_inc(ld_x, 16)
                        if (e := r["M"]) is not None:
                            sp.wait_ge(actM.sem, actM.count(e, "mT"))
                            sp.dma_start(stack[1 - par][ROW_M:ROW_M + 1, 0], mT[:]).then_inc(ld_m, 16)
                    if g == 2 and (e := r["A1"]) is not None:
                        sp.wait_ge(ld_stack, dma_count(e - 1, N_STACK))
                        sp.wait_ge(dveA1.sem, dveA1.count(e, "lo"))
                        for s in range(2):
                            sp.dma_start(d_parts[s].rearrange("a p n -> p a n"), parts[:, s]).then_inc(st_parts, 16)
                        sp.wait_ge(st_parts, dma_count(e, 2))
                        sp.wait_ge(peA2.sem, peA2.count(e - 2, "ST", 15))
                        for kp in range(3):
                            sp.dma_start(stack[par][24 * kp:24 * kp + 24, 0].rearrange("p h n -> p (h n)"),
                                         bass.AP(d_parts.tensor, 0, [[H * T, 24], [1, H * T]])).then_inc(ld_stack, 16)
                            for qp in range(3):
                                sp.dma_start(stack[par][24 * kp + 8 * qp:24 * kp + 8 * qp + 8, 1].rearrange("p h n -> p (h n)"),
                                             bass.AP(d_parts.tensor, (3 + kp) * 128 * T,
                                                     [[H * T, 8], [1, H * T]])).then_inc(ld_stack, 16)
                    if g == 8:
                        for st, dg, dr, st_s, ld_s, act, used in (("B", gB, d_cB, st_cB, ld_cB, actB, (dveB, "wu", 16)),
                                                                  ("D", gD, d_cD, st_cD, ld_cD, actD, (poolD, "xs", 3))):
                            if (e := r[st]) is not None:
                                sp.wait_ge(ld_s, dma_count(e - 1))
                                sp.wait_ge(act.sem, act.count(e, "cT"))
                                for tt in range(TT):
                                    sp.dma_start(dr[tt], dg["cT"][64 * tt:64 * tt + E, :]).then_inc(st_s, 16)
                        for st, dg, dr, st_s, ld_s, act, used in (("B", gB, d_cB, st_cB, ld_cB, actB, (dveB, "wu", 16)),
                                                                  ("D", gD, d_cD, st_cD, ld_cD, actD, (poolD, "xs", 3))):
                            if (e := r[st]) is not None:
                                sp.wait_ge(st_s, dma_count(e, TT))
                                sp.wait_ge(used[0].sem, used[0].count(e - 1, used[1], used[2]))
                                sp.dma_start(dg["cb"][:].rearrange("p a b n -> p (a b n)"),
                                             bass.AP(dr.tensor, 0, [[0, 128], [1, TT * E * 128]])).then_inc(ld_s, 16)
                    if g == 14 and (e := r["C1"]) is not None:
                        sp.wait_ge(ld_w, dma_count(e - 1, N_W))
                        sp.wait_ge(actC1.sem, actC1.count(e, "wT"))
                        sp.dma_start(d_w.rearrange("s p n -> p s n"), wT[:]).then_inc(st_w, 16)
                        sp.wait_ge(st_w, dma_count(e))
                        sp.wait_ge(dveC2n.sem, dveC2n.count(e - 1, "gt"))
                        for d in range(HD):
                            sp.dma_start(wb[H * d:H * d + H].rearrange("p (s j) n -> p s j n", s=2),
                                         bass.AP(d_w.tensor, 0, [[T, H], [128 * T, 2], [H * T, NP], [1, T]])
                                         ).then_inc(ld_w, 16)
                    if g == 18 and (e := r["D"]) is not None:
                        sp.wait_ge(dveDn.sem, dveDn.count(e, "nm", 1))
                        sp.dma_start(out_rows[:, bass.ds(e * TT, TT), :], xout[:]).then_inc(st_out, 16)

            passes(sp, one)
            sp.wait_ge(st_out, dma_count(B - 1))

        @block.tensor
        def _(pe):
            mm = nc.tensor.matmul
            pe.wait_ge(ld_const, 16 * N_CONST)
            pe.wait_ge(setup_dve, SETUP_DVE)
            pe.wait_ge(setup_act, SETUP_ACT)
            last = {6: None, 7: None}

            def take(bank_no, now, t):
                if last[bank_no]:
                    st, s, name, i, when = last[bank_no]
                    pe.wait_ge(s.sem, s.count(when - LAG[st], name, i))
                last[bank_no] = (*now, t)

            def one(t, par, key):
                if key == LOOP_FROM and not isinstance(t, int):
                    for b in (6, 7):
                        last[b] = (*last[b][:4], t - 1)
                if isinstance(t, int) and t == B:
                    for b in (6, 7):
                        last[b] = (*last[b][:4], B - 1)
                r = stages(t)
                odd = 1 - par
                for g in range(SLOTS):
                    if g == 0 and (e := r["M"]) is not None:
                        take(6, ("M", actM, "mT", 0), t)
                        pe.wait_ge(dveM.sem, dveM.count(e, "neg"))
                        o = b6[:].bitcast(BF)
                        for tt in range(TT):
                            i = nc.tensor.transpose(o[0:H, tt * 128:tt * 128 + 128], mneg[:, tt, :], identb[:])
                        i.then_inc(peM.done("mT"), 1)
                    if g == 1:
                        if (e := r["A1"]) is not None:
                            take(6, ("A1", actA1, "k", 0), t)
                            pe.wait_ge(ld_xT, dma_count(e))
                            mm(b6[:, 0:T], wqk0[:, 0, :], xT[:], start=True, stop=True)
                            mm(b6[:, T:2 * T], wqk0[:, 1, :], xT[:], start=True, stop=True).then_inc(peA1.done("qk"), 1)
                        if (e := r["C1"]) is not None:
                            take(7, ("C1", actC1, "xT", 0), t)
                            pe.wait_ge(dveBn.sem, dveBn.count(e, "nm", 1))
                            for tt in range(TT):
                                i = nc.tensor.transpose(b7[:, tt * 128:tt * 128 + 128], x2[odd][:, tt, :], ident[:])
                            i.then_inc(peC1.done("xT"), 1)
                        if (e := r["A3"]) is not None:
                            take(6, ("A3", dveA3, "res", 0), t)
                            pe.wait_ge(dveA3.sem, dveA3.count(e, "num"))
                            for tt in range(TT):
                                i = mm(b6[:, tt * 128:tt * 128 + 128], attnT[:, tt * 128:tt * 128 + 128], wo0[:],
                                       start=True, stop=True)
                            i.then_inc(peA3.done("out"), 1)
                    if g == 2:
                        if (e := r["C1"]) is not None:
                            take(7, ("C1", actC1, "k", 0), t)
                            pe.wait_ge(actC1.sem, actC1.count(e, "xT"))
                            mm(b7[:, 0:T], wc[:, 0, :], x2T[:], start=True, stop=True)
                            mm(b7[:, T:2 * T], wc[:, 1, :], x2T[:], start=True, stop=True).then_inc(peC1.done("qk"), 1)
                        if (e := r["A1"]) is not None:
                            take(6, ("A1", dveA1, "v", 0), t)
                            for tt in range(TT):
                                i = mm(b6[:, tt * 128:tt * 128 + 128], xT[:, tt * 128:tt * 128 + 128], wv0[:],
                                       start=True, stop=True)
                            i.then_inc(peA1.done("v"), 1)
                    if g == 3 and (e := r["C1"]) is not None:
                        take(7, ("C1", actC1, "g", 0), t)
                        mm(b7[:, 0:T], wc[:, 2, :], x2T[:], start=True, stop=True)
                        mm(b7[:, T:2 * T], wc[:, 3, :], x2T[:], start=True, stop=True).then_inc(peC1.done("vg"), 1)
                    if g == 4:
                        for st, bk, bn, s, act, src, prev in (("B", b6, 6, peB, actB, x1[par], dveA3),
                                                              ("D", b7, 7, peD, actD, x3[1 - par], dveC2n)):
                            if (e := r[st]) is not None:
                                take(bn, (st, act, "xT", 0), t)
                                pe.wait_ge(prev.sem, prev.count(e, "nm", 1))
                                for tt in range(TT):
                                    i = nc.tensor.transpose(bk[:, tt * 128:tt * 128 + 128], src[:, tt, :], ident[:])
                                i.then_inc(s.done("xT"), 1)
                    if g == 5:
                        for st, bk, bn, s, act, xt, gw, dg in (("B", b6, 6, peB, actB, x1T, gw0, dveBg),
                                                               ("D", b7, 7, peD, actD, x3T, gw1, dveDg)):
                            if (e := r[st]) is not None:
                                take(bn, (st, dg, "cp", 0), t)
                                pe.wait_ge(act.sem, act.count(e, "xT"))
                                for tt in range(TT):
                                    i = mm(bk[:, tt * E:tt * E + E], xt[:, tt * 128:tt * 128 + 128], gw[:],
                                           start=True, stop=True)
                                i.then_inc(s.done("lg"), 1)
                    if g == 8:
                        for st, bk, bn, s, act, dg, gb in (("B", b6, 6, peB, actB, dveBg, gB),
                                                           ("D", b7, 7, peD, actD, dveDg, gD)):
                            if (e := r[st]) is not None:
                                take(bn, (st, act, "cT", 0), t)
                                pe.wait_ge(dg.sem, dg.count(e, "c"))
                                nc.tensor.transpose(bk[:, 0:128], gb["c"][:].rearrange("p a b -> p (a b)"),
                                                    ident[:]).then_inc(s.done("cT"), 1)
                    if 3 <= g < 19 and (e := r["A2"]) is not None:
                        k = g - 3
                        h = head(k)
                        if k == 0:
                            pe.wait_ge(ld_m, dma_count(e))
                        if k >= 2:
                            pe.wait_ge(actA2.sem, actA2.count(e, "exp", k - 2))
                        else:
                            pe.wait_ge(actA2.sem, actA2.count(e - 1, "exp", k + 14))
                        o = bST[k % 2]
                        for kt in range(TT):
                            q = slice(kt * T, kt * T + T)
                            c = slice(kt * T + kt * 128, kt * T + kt * 128 + 128)
                            mm(o[:, q], stack[odd][0:ROW_M + 1, 1, h, kt * 128:kt * 128 + 128],
                               stack[odd][0:ROW_M + 1, 0, h, :], start=True, stop=False)
                            last_part = h % 2 == 0
                            i = mm(o[:, c], identh[:], dist[:, h, 0, :], start=False, stop=last_part)
                            if not last_part:
                                i = mm(o[:, c], identh[:], dist[:, h, 1, :], start=False, stop=True)
                        i.then_inc(peA2.done("ST", k), 1)
                    if g % 4 == 3 and g >= 7 and (e := r["A2"]) is not None:
                        rr = (g - 7) // 4
                        pe.wait_ge(actA2.sem, actA2.count(e, "exp", 4 * rr + 3))
                        if rr == 0:
                            pe.wait_ge(dveA3.sem, dveA3.count(e - 1, "num"))
                            pe.wait_ge(dveA1.sem, dveA1.count(e, "v"))
                        for kt in range(TT):
                            for den in range(2):
                                for j in range(4):
                                    k = 4 * rr + j
                                    lhs = onesz[:, rr, :] if den else Vz[odd][:, kt, j, 32 * rr:32 * rr + 32]
                                    i = mm(bPV[32 * j:32 * j + 32, den * T:den * T + T], lhs, P[k % 8][:, kt, :],
                                           start=(rr == 0 and kt == 0 and den == 0), stop=(rr == 3 and kt == 1),
                                           skip_group_check=True)
                        i.then_inc(pePV.done("PV", rr), 1)
                    if g >= 5 and (e := r["A1"]) is not None:
                        for k in ((0, 1) if g == 5 else (g - 4,)):
                            if k == 0:
                                pe.wait_ge(ld_stack, dma_count(e, N_STACK))
                            if k >= 2:
                                pe.wait_ge(dveA1.sem, dveA1.count(e, "max", k - 2))
                            else:
                                pe.wait_ge(dveA1.sem, dveA1.count(e - 1, "max", k + 14))
                            o = bS[k % 2]
                            h = k
                            for qt in range(TT):
                                mm(o[:, qt * T:qt * T + T], stack[par][0:ROW_M, 0, h, qt * 128:qt * 128 + 128],
                                   stack[par][0:ROW_M, 1, h, :], start=True, stop=False)
                                c = slice(qt * T + qt * 128, qt * T + qt * 128 + 128)
                                i = mm(o[:, c], identh[:], dist[:, h, 0, :], start=False, stop=True)
                            i.then_inc(peA1.done("S", k), 1)
                    if 9 <= g < 18 and (e := r["B"]) is not None:
                        n = g - 9
                        x = expert(n)
                        if n:
                            pe.wait_ge(actB.sem, actB.count(e, "ab", 2 * n - 1))
                            pe.wait_ge(dveB.sem, dveB.count(e, "wu", 2 * n - 2))
                        else:
                            pe.wait_ge(actB.sem, actB.count(e - 1, "ab", 17))
                            pe.wait_ge(dveB.sem, dveB.count(e - 1, "wu", 16))
                        mm(bAB[:, 0:T], w13[:, x, 0, :], x1T[:], start=True, stop=True)
                        mm(bAB[:, T:2 * T], w13[:, x, 1, :], x1T[:], start=True, stop=True).then_inc(peB.done("ab", n), 1)
                    if g == 9 and (e := r["C1"]) is not None:
                        take(7, ("C1", dveC1, "sc", 1), t)
                        pe.wait_ge(poolC1.sem, poolC1.count(e, "prod", 7))
                        for s in range(2):
                            for o2 in range(2):
                                for j in range(4):
                                    i = mm(b7[32 * j:32 * j + 32, s * T:s * T + T], hsum[:, o2, :],
                                           prod[:, 2 * (4 * s + j) + o2, :], start=(s == 0 and o2 == 0), stop=o2 == 1,
                                           skip_group_check=True)
                        i.then_inc(peC1.done("sc"), 1)
                    if g == 10 and (e := r["C1"]) is not None:
                        take(7, ("C1", dveC1, "sub", 0), t)
                        for tt in range(TT):
                            for s in range(2):
                                i = nc.tensor.transpose(b7[:, tt * T + s * 128:tt * T + s * 128 + 128],
                                                        scs[:, s, tt * 128:tt * 128 + 128], ident[:])
                        i.then_inc(peC1.done("scT"), 1)
                    if g == 12 and (e := r["C2"]) is not None:
                        take(7, ("C2", dveC2n, "res", 0), t)
                        pe.wait_ge(dveC2n.sem, dveC2n.count(e, "gt"))
                        for tt in range(TT):
                            i = mm(b7[:, tt * 128:tt * 128 + 128], gat[:, tt * 128:tt * 128 + 128], woc[:],
                                   start=True, stop=True)
                        i.then_inc(peC2.done("out"), 1)
                    if g == 13 and (e := r["C1"]) is not None:
                        take(7, ("C1", actC1, "wT", 0), t)
                        pe.wait_ge(dveC1.sem, dveC1.count(e, "w"))
                        wv = wn[:].rearrange("p t a h -> p t (a h)")
                        for s in range(2):
                            for tt in range(TT):
                                i = nc.tensor.transpose(b7[:, s * T + tt * 128:s * T + tt * 128 + 128],
                                                        wv[:, tt, s * 128:s * 128 + 128], ident[:])
                        i.then_inc(peC1.done("wT"), 1)
                    if g == 15 and (e := r["D"]) is not None:
                        take(7, ("D", dveDn, "res", 0), t)
                        for tt in range(TT):
                            for x in range(E):
                                if tt == 0 and x % 2 == 0:
                                    pe.wait_ge(poolD.sem, poolD.count(e, "xs", x // 2))
                                i = mm(b7[:, tt * 128:tt * 128 + 128], xs[:, x, tt * 128:tt * 128 + 128], ew[:, x, :],
                                       start=(x == 0), stop=(x == E - 1))
                        i.then_inc(peD.done("y"), 1)
                    if g == 18 and (e := r["B"]) is not None:
                        take(6, ("B", dveBn, "res", 0), t)
                        pe.wait_ge(actB.sem, actB.count(e, "cT"))
                        for tt in range(TT):
                            mm(b6[:, tt * 128:tt * 128 + 128], gB["cT"][:], b2[:, tt, :], start=True, stop=False)
                            for n in range(E + 1):
                                if tt == 0:
                                    pe.wait_ge(poolB.sem, poolB.count(e, "h", n))
                                i = mm(b6[:, tt * 128:tt * 128 + 128], h9[:, n, tt * 128:tt * 128 + 128],
                                       w2[:, expert(n), :], start=False, stop=(n == E))
                        i.then_inc(peB.done("z"), 1)

            passes(pe, one)

        @block.scalar
        def _(act):
            act.wait_ge(ld_const, 16 * N_CONST)
            q_scale = HD ** -0.5
            nc.scalar.mul(bqk0[:, 0:1], bqk0[:, 0:1], q_scale).then_inc(setup_act, 1)
            nc.scalar.mul(b3[:], b3[:], 0.5).then_inc(setup_act, 1)
            nc.scalar.mul(bc[:, 0:1], bc[:, 0:1], q_scale).then_inc(setup_act, 1)
            nc.scalar.mul(bc[:, 3:4], bc[:, 3:4], 0.5).then_inc(setup_act, 1)
            nc.scalar.mul(woc[:], woc[:], 0.5).then_inc(setup_act, 1)
            act.wait_ge(setup_dve, 14)
            nc.scalar.activation(posd[:], posd[:], ACT.Exp).then_inc(setup_act, 1)
            nc.scalar.activation(oobd[:], oobd[:], ACT.Exp).then_inc(setup_act, 1)
            act.wait_ge(setup_dve, 16)
            nc.scalar.activation(posE[:], poss[:], ACT.Ln).then_inc(setup_act, 1)
            nc.scalar.activation(oobE[:], oobs[:], ACT.Ln).then_inc(setup_act, 1)
            act.wait_ge(setup_act, SETUP_ACT)
            act.wait_ge(setup_dve, SETUP_DVE)

            def one(t, par, key):
                r = stages(t)
                odd = 1 - par
                act_f = nc.scalar.activation
                for g in range(SLOTS):
                    if g == 0 and (e := r["M"]) is not None:
                        act.wait_ge(peM.sem, peM.count(e, "mT"))
                        act.wait_ge(ld_m, dma_count(e - 1))
                        nc.scalar.copy(mT[:], b6[:].bitcast(BF)[0:H, 0:T]).then_inc(actM.done("mT"), 1)
                    if g == 1:
                        if (e := r["A1"]) is not None:
                            act.wait_ge(peA1.sem, peA1.count(e, "qk"))
                            act.wait_ge(dveA1.sem, dveA1.count(e - 1, "lo"))
                            act_f(qk[:, 0, :], b6[:, 0:T], ACT.Identity, bias=bqk0[:, 0:1],
                                  scale=q_scale).then_inc(actA1.done("q"), 1)
                            act_f(qk[:, 1, :], b6[:, T:2 * T], ACT.Identity, bias=bqk0[:, 1:2]).then_inc(actA1.done("k"), 1)
                        if (e := r["C1"]) is not None:
                            act.wait_ge(peC1.sem, peC1.count(e, "xT"))
                            nc.scalar.copy(x2T[:], b7[:, 0:T]).then_inc(actC1.done("xT"), 1)
                    if g == 2 and (e := r["C1"]) is not None:
                        act.wait_ge(peC1.sem, peC1.count(e, "qk"))
                        act.wait_ge(poolC1.sem, poolC1.count(e - 1, "prod", 7))
                        act_f(qC[:], b7[:, 0:T], ACT.Identity, bias=bc[:, 0:1], scale=q_scale).then_inc(actC1.done("q"), 1)
                        act_f(kC[:, PAD:], b7[:, T:2 * T], ACT.Identity, bias=bc[:, 1:2]).then_inc(actC1.done("k"), 1)
                    if g == 3 and (e := r["C1"]) is not None:
                        act.wait_ge(peC1.sem, peC1.count(e, "vg"))
                        act.wait_ge(dveC2.sem, dveC2.count(e - 2, "pv", 7))
                        act.wait_ge(dveC2n.sem, dveC2n.count(e - 2, "gt"))
                        act_f(vC[odd][:, PAD:], b7[:, 0:T], ACT.Identity, bias=bc[:, 2:3]).then_inc(actC1.done("v"), 1)
                        act_f(tg[odd][:], b7[:, T:2 * T], ACT.Tanh, bias=bc[:, 3:4], scale=0.5).then_inc(actC1.done("g"), 1)
                    if g == 4:
                        if (e := r["B"]) is not None:
                            act.wait_ge(peB.sem, peB.count(e, "xT"))
                            act.wait_ge(peB.sem, peB.count(e - 1, "ab", 8))
                            nc.scalar.copy(x1T[:], b6[:, 0:T]).then_inc(actB.done("xT"), 1)
                        if (e := r["D"]) is not None:
                            act.wait_ge(peD.sem, peD.count(e, "xT"))
                            act.wait_ge(poolD.sem, poolD.count(e - 1, "xs", 3))
                            nc.scalar.copy(x3T[:], b7[:, 0:T]).then_inc(actD.done("xT"), 1)
                    if g == 6:
                        for st, s, dg, gb in (("B", actB, dveBg, gB), ("D", actD, dveDg, gD)):
                            if (e := r[st]) is not None:
                                act.wait_ge(dg.sem, dg.count(e, "sub"))
                                act.wait_ge(dg.sem, dg.count(e - 1, "sum"))
                                act_f(gb["ge"][:], gb["dl"][:], ACT.Exp).then_inc(s.done("ge"), 1)
                    if g == 8:
                        for st, s, p, gb, bk, used in (("B", actB, peB, gB, b6, (peB, "z")), ("D", actD, peD, gD, b7, None)):
                            if (e := r[st]) is not None:
                                act.wait_ge(p.sem, p.count(e, "cT"))
                                act.wait_ge(st_cB if st == "B" else st_cD, dma_count(e - 1, TT))
                                if used:
                                    act.wait_ge(used[0].sem, used[0].count(e - 1, used[1]))
                                nc.scalar.copy(gb["cT"][:], bk[:, 0:128]).then_inc(s.done("cT"), 1)
                    if 3 <= g < 19 and (e := r["A2"]) is not None:
                        k = g - 3
                        act.wait_ge(peA2.sem, peA2.count(e, "ST", k))
                        if k >= 8:
                            act.wait_ge(pePV.sem, pePV.count(e, "PV", (k - 8) // 4))
                        else:
                            act.wait_ge(pePV.sem, pePV.count(e - 1, "PV", (k + 8) // 4))
                        act_f(P[k % 8][:].rearrange("p a b -> p (a b)"), bST[k % 2][:], ACT.Exp).then_inc(actA2.done("exp", k), 1)
                    if 9 <= g < 18 and (e := r["B"]) is not None:
                        n = g - 9
                        x = expert(n)
                        act.wait_ge(peB.sem, peB.count(e, "ab", n))
                        if n >= 2:
                            act.wait_ge(dveB.sem, dveB.count(e, "wu", 2 * n - 3))
                        else:
                            act.wait_ge(dveB.sem, dveB.count(e - 1, "wu", 17))
                        act_f(th[n % 2][:], bAB[:, 0:T], ACT.Tanh, bias=b1h[:, x:x + 1], scale=0.5).then_inc(actB.done("ab", 2 * n), 1)
                        act_f(bb[n % 2][:], bAB[:, T:2 * T], ACT.Identity, bias=b3[:, x:x + 1],
                              scale=0.5).then_inc(actB.done("ab", 2 * n + 1), 1)
                    if g == 11 and (e := r["C1"]) is not None:
                        act.wait_ge(dveC1.sem, dveC1.count(e, "subo"))
                        act_f(es[:], ds[:], ACT.Exp).then_inc(actC1.done("exp"), 1)
                    if g == 13 and (e := r["C1"]) is not None:
                        act.wait_ge(peC1.sem, peC1.count(e, "wT"))
                        act.wait_ge(st_w, dma_count(e - 1))
                        nc.scalar.copy(wT[:].rearrange("p a b -> p (a b)"), b7[:]).then_inc(actC1.done("wT"), 1)

            passes(act, one)

        @block.vector
        def _(dve):
            v = nc.vector
            for i in range(2):
                v.memset(Vz[i][:], 0.0).then_inc(setup_dve, 1)
            for z in (kC[:, 0:PAD], vC[0][:, 0:PAD], vC[1][:, 0:PAD]):
                v.memset(z, 0.0).then_inc(setup_dve, 1)
            for gb in (gB, gD):
                v.memset(gb["c"][:, :, E + 1:], 0.0).then_inc(setup_dve, 1)
                v.memset(gb["c"][:, :, E:E + 1], 1.0).then_inc(setup_dve, 1)
            dve.wait_ge(ld_const, 16 * N_CONST)
            v.tensor_scalar(b1h[:], b1[:], 0.5, None, ALU.mult).then_inc(setup_dve, 1)
            v.tensor_reduce(posm[:], posd[:], op=ALU.max, axis=AX.X).then_inc(setup_dve, 1)
            v.tensor_reduce(oobm[:], oobd[:], op=ALU.max, axis=AX.X).then_inc(setup_dve, 1)
            dve.wait_ge(setup_dve, 12)
            v.tensor_tensor(posd[:], posd[:], posm[:].unsqueeze(2).to_broadcast([128, 2, DUP]),
                            ALU.subtract).then_inc(setup_dve, 1)
            v.tensor_tensor(oobd[:], oobd[:], oobm[:].unsqueeze(2).to_broadcast([128, H, len(OOB)]),
                            ALU.subtract).then_inc(setup_dve, 1)
            dve.wait_ge(setup_act, 7)
            v.tensor_reduce(poss[:], posd[:], op=ALU.add, axis=AX.X).then_inc(setup_dve, 1)
            v.tensor_reduce(oobs[:], oobd[:], op=ALU.add, axis=AX.X).then_inc(setup_dve, 1)
            dve.wait_ge(setup_act, 9)
            v.tensor_tensor(posE[:], posE[:], posm[:], ALU.add).then_inc(setup_dve, 1)
            v.tensor_tensor(oobE[:], oobE[:], oobm[:], ALU.add).then_inc(setup_dve, 1)
            dve.wait_ge(setup_dve, SETUP_DVE)

            def norm(s, e, nb, x, out_x):
                dve.wait_ge(s.sem, s.count(e, "res"))
                for tt in range(TT):
                    v.bn_stats(nb["st"][:, tt, :], nb["y"][:, tt, :]).then_inc(s.done("bn", tt), 1)
                for tt in range(TT):
                    dve.wait_ge(s.sem, s.count(e, "bn", tt))
                    v.memset(nb["tick"][:, tt:tt + 1], 0.0)
                    v.bn_aggr(nb["mv"][:, tt, :], nb["st"][:, tt, :]).then_inc(s.done("ag", tt), 1)
                dve.wait_ge(s.sem, s.count(e, "ag", 1))
                v.tensor_scalar(nb["v"][:], nb["mv"][:, :, 1], EPS, None, ALU.add).then_inc(s.done("ve"), 1)
                dve.wait_ge(s.sem, s.count(e, "ve"))
                v.tensor_scalar(nb["i"][:], nb["v"][:].bitcast(I32), 1, None,
                                ALU.logical_shift_right).then_inc(s.done("sh"), 1)
                dve.wait_ge(s.sem, s.count(e, "sh"))
                v.tensor_scalar(nb["r"][:].bitcast(I32), nb["i"][:], -1.0, float(0x5F3759DF), ALU.mult,
                                ALU.add).then_inc(s.done("mg"), 1)
                dve.wait_ge(s.sem, s.count(e, "mg"))
                for n in range(3):
                    if n:
                        dve.wait_ge(s.sem, s.count(e, "nt", 3 * n - 1))
                    v.tensor_tensor(nb["s"][:], nb["r"][:], nb["r"][:], ALU.mult).then_inc(s.done("nt", 3 * n), 1)
                    dve.wait_ge(s.sem, s.count(e, "nt", 3 * n))
                    v.scalar_tensor_tensor(nb["s"][:], nb["s"][:], -0.5, nb["v"][:], ALU.mult,
                                           ALU.mult).then_inc(s.done("nt", 3 * n + 1), 1)
                    dve.wait_ge(s.sem, s.count(e, "nt", 3 * n + 1))
                    v.scalar_tensor_tensor(nb["r"][:], nb["s"][:], 1.5, nb["r"][:], ALU.add,
                                           ALU.mult).then_inc(s.done("nt", 3 * n + 2), 1)
                dve.wait_ge(s.sem, s.count(e, "nt", 8))
                for tt in range(TT):
                    v.tensor_scalar(out_x[:, tt, :], nb["y"][:, tt, :], nb["mv"][:, tt, 0:1], nb["r"][:, tt:tt + 1],
                                    ALU.subtract, ALU.mult).then_inc(s.done("nm", tt), 1)

            def gates_rank(both):
                for s, e, gb, bk, p in both:
                    dve.wait_ge(p.sem, p.count(e, "lg"))
                    dve.wait_ge(s.sem, s.count(e - 1, "c"))
                    v.tensor_copy(gb["L"][:].rearrange("p t x -> p (t x)"), bk[:, 0:TT * E]).then_inc(s.done("cp"), 1)
                for s, e, gb, bk, p in both:
                    dve.wait_ge(s.sem, s.count(e, "cp"))
                    v.tensor_reduce(gb["mx"][:], gb["L"][:], op=ALU.max, axis=AX.X).then_inc(s.done("gmx"), 1)
                for s, e, gb, bk, p in both:
                    dve.wait_ge(s.sem, s.count(e, "gmx"))
                    v.tensor_tensor(gb["dl"][:], gb["L"][:], gb["mx"][:].unsqueeze(2).to_broadcast([128, TT, E]),
                                    ALU.subtract).then_inc(s.done("sub"), 1)
                for s, e, gb, bk, p in both:
                    lj = gb["L"][:].unsqueeze(2).to_broadcast([128, TT, E, E])
                    li = gb["L"][:].unsqueeze(3).to_broadcast([128, TT, E, E])
                    o = [gb[x][:].rearrange("p (t i j) -> p t i j", t=TT, i=E) for x in ("gt", "eq")]
                    v.tensor_tensor(o[0], lj, li, ALU.is_gt).then_inc(s.done("gt"), 1)
                    v.tensor_tensor(o[1], lj, li, ALU.is_equal).then_inc(s.done("eq"), 1)
                for s, e, gb, bk, p in both:
                    dve.wait_ge(s.sem, s.count(e, "eq"))
                    v.tensor_tensor(gb["eq"][:], gb["eq"][:], tri[:], ALU.mult).then_inc(s.done("eqt"), 1)
                for s, e, gb, bk, p in both:
                    dve.wait_ge(s.sem, s.count(e, "eqt"))
                    v.tensor_tensor(gb["gt"][:], gb["gt"][:], gb["eq"][:], ALU.add).then_inc(s.done("add"), 1)
                for s, e, gb, bk, p in both:
                    dve.wait_ge(s.sem, s.count(e, "add"))
                    v.tensor_reduce(gb["rank"][:].rearrange("p t x -> p (t x)"),
                                    gb["gt"][:].rearrange("p (a j) -> p a j", j=E), op=ALU.add,
                                    axis=AX.X).then_inc(s.done("rank"), 1)

            def gates_weigh(both):
                for s, e, gb, acts, peS, over in both:
                    dve.wait_ge(acts.sem, acts.count(e, "ge"))
                    dve.wait_ge(s.sem, s.count(e, "rank"))
                    v.scalar_tensor_tensor(gb["sel"][:], gb["rank"][:], 1.5, gb["ge"][:], ALU.is_lt,
                                           ALU.mult).then_inc(s.done("sel"), 1)
                for s, e, gb, acts, peS, over in both:
                    dve.wait_ge(s.sem, s.count(e, "sel"))
                    v.tensor_reduce(gb["sum"][:], gb[over][:], op=ALU.add, axis=AX.X).then_inc(s.done("sum"), 1)
                for s, e, gb, acts, peS, over in both:
                    dve.wait_ge(s.sem, s.count(e, "sum"))
                    v.reciprocal(gb["rec"][:], gb["sum"][:]).then_inc(s.done("rec"), 1)
                for s, e, gb, acts, peS, over in both:
                    dve.wait_ge(s.sem, s.count(e, "rec"))
                    dve.wait_ge(peS.sem, peS.count(e - 1, "cT"))
                    v.tensor_tensor(gb["c"][:, :, 0:E], gb["sel"][:], gb["rec"][:].unsqueeze(2).to_broadcast([128, TT, E]),
                                    ALU.mult).then_inc(s.done("c"), 1)

            def one(t, par, key):
                r = stages(t)
                odd = 1 - par
                for g in range(SLOTS):
                    if g == 0 and (e := r["M"]) is not None:
                        dve.wait_ge(dveA1.sem, dveA1.count(e, "max", 15))
                        dve.wait_ge(peM.sem, peM.count(e - 1, "mT"))
                        v.tensor_scalar(mneg[:], mx[:], -1.0, None, ALU.mult).then_inc(dveM.done("neg"), 1)
                    if g == 1:
                        if (e := r["A3"]) is not None:
                            dve.wait_ge(pePV.sem, pePV.count(e, "PV", 3))
                            dve.wait_ge(peA3.sem, peA3.count(e - 1, "out"))
                            v.reciprocal(rden[:], bPV[:, T:2 * T]).then_inc(dveA3.done("rec"), 1)
                            dve.wait_ge(dveA3.sem, dveA3.count(e, "rec"))
                            v.tensor_tensor(attnT[:], bPV[:, 0:T], rden[:], ALU.mult).then_inc(dveA3.done("num"), 1)
                        if (e := r["A1"]) is not None:
                            dve.wait_ge(actA1.sem, actA1.count(e, "k"))
                            dve.wait_ge(st_parts, dma_count(e - 1, 2))
                            v.tensor_copy(parts[:, :, 0, :], qk[:]).then_inc(dveA1.done("hi"), 1)
                            dve.wait_ge(dveA1.sem, dveA1.count(e, "hi"))
                            v.tensor_tensor(rest[:], qk[:], parts[:, :, 0, :], ALU.subtract).then_inc(dveA1.done("rest"), 1)
                            dve.wait_ge(dveA1.sem, dveA1.count(e, "rest"))
                            v.tensor_copy(parts[:, :, 1, :], rest[:]).then_inc(dveA1.done("mid"), 1)
                            dve.wait_ge(dveA1.sem, dveA1.count(e, "mid"))
                            v.tensor_tensor(parts[:, :, 2, :], rest[:], parts[:, :, 1, :],
                                            ALU.subtract).then_inc(dveA1.done("lo"), 1)
                    if g == 2:
                        if (e := r["A3"]) is not None:
                            dve.wait_ge(peA3.sem, peA3.count(e, "out"))
                            dve.wait_ge(poolA3.sem, poolA3.count(e, "xbo"))
                            dve.wait_ge(dveA3.sem, dveA3.count(e - 1, "nm", 1))
                            v.tensor_tensor(nA["y"][:].rearrange("p t c -> p (t c)"), b6[:, 0:T],
                                            x0b[:].rearrange("p t c -> p (t c)"), ALU.add).then_inc(dveA3.done("res"), 1)
                        if (e := r["A1"]) is not None:
                            dve.wait_ge(peA1.sem, peA1.count(e, "v"))
                            dve.wait_ge(pePV.sem, pePV.count(e - 2, "PV", 3))
                            o = bass.AP(Vz[par], 0, [[TT * 4 * 160, 128], [160, TT * 4], [40, 4], [1, HD]])
                            v.tensor_tensor(o, b6[:, 0:T].rearrange("p (a r d) -> p a r d", r=4, d=HD),
                                            bv0[:].rearrange("p t c -> p (t c)").rearrange("p (a r d) -> p a r d", r=4, d=HD),
                                            ALU.add).then_inc(dveA1.done("v"), 1)
                        if (e := r["A3"]) is not None:
                            norm(dveA3, e, nA, None, x1[par])
                    if g <= 3 and (e := r["C2"]) is not None:
                        if g == 0:
                            dve.wait_ge(ld_w, dma_count(e, N_W))
                            dve.wait_ge(actC1.sem, actC1.count(e, "v"))
                            dve.wait_ge(dveC2n.sem, dveC2n.count(e - 1, "gt"))
                        for p in (2 * g, 2 * g + 1):
                            v.tensor_tensor(pv[:, 2 * p:2 * p + 2, :], wb[:, 2 * p:2 * p + 2, :], shifted(vC[par], p),
                                            ALU.mult).then_inc(dveC2.done("pv", p), 1)
                    if g == 6:
                        both = [(s, r[st], gb, bk, p) for st, s, gb, bk, p in
                                (("B", dveBg, gB, b6, peB), ("D", dveDg, gD, b7, peD)) if r[st] is not None]
                        gates_rank(both)
                    if g == 7:
                        both = [(s, r[st], gb, a, p, over) for st, s, gb, a, p, over in
                                (("B", dveBg, gB, actB, peB, "ge"), ("D", dveDg, gD, actD, peD, "sel"))
                                if r[st] is not None]
                        gates_weigh(both)
                    if g >= 5 and (e := r["A1"]) is not None:
                        for k in ((0, 1) if g == 5 else (g - 4,)):
                            dve.wait_ge(peA1.sem, peA1.count(e, "S", k))
                            if k == 0:
                                dve.wait_ge(dveM.sem, dveM.count(e - 1, "neg"))
                            v.tensor_reduce(mx[:, :, k], bS[k % 2][:].rearrange("p (a b) -> p a b", a=TT), op=ALU.max,
                                            axis=AX.X).then_inc(dveA1.done("max", k), 1)
                    if 9 <= g < 18 and (e := r["B"]) is not None:
                        n = g - 9
                        x = expert(n)
                        dve.wait_ge(actB.sem, actB.count(e, "ab", 2 * n + 1))
                        if n >= 2:
                            dve.wait_ge(poolB.sem, poolB.count(e, "h", n - 2))
                        else:
                            dve.wait_ge(poolB.sem, poolB.count(e - 1, "h", n + 7))
                        if n == 1:
                            dve.wait_ge(ld_cB, dma_count(e))
                        if n == 0:
                            i = v.tensor_scalar(wa[0][:], bAB[:, 0:T], b1[:, x:x + 1], None, ALU.add)
                        else:
                            i = v.scalar_tensor_tensor(wa[n % 2][:].rearrange("p (t n) -> p t n", t=TT),
                                                       bAB[:, 0:T].rearrange("p (t n) -> p t n", t=TT), b1[:, x:x + 1],
                                                       gB["cb"][:, :, x, :], ALU.add, ALU.mult)
                        i.then_inc(dveB.done("wu", 2 * n), 1)
                        v.scalar_tensor_tensor(ub[n % 2][:], th[n % 2][:], 1.0, bb[n % 2][:], ALU.add,
                                               ALU.mult).then_inc(dveB.done("wu", 2 * n + 1), 1)
                    if g == 9 and (e := r["C1"]) is not None:
                        dve.wait_ge(peC1.sem, peC1.count(e, "sc"))
                        dve.wait_ge(peC1.sem, peC1.count(e - 1, "scT"))
                        for s in range(2):
                            v.tensor_scalar(scs[:, s, :], b7[:, s * T:s * T + T], posE[:, s:s + 1], None,
                                            ALU.add).then_inc(dveC1.done("sc", s), 1)
                    if g == 11 and (e := r["C1"]) is not None:
                        dve.wait_ge(peC1.sem, peC1.count(e, "scT"))
                        sc_ = b7[:].rearrange("p (t a h) -> p t a h", t=TT, h=H)
                        v.tensor_reduce(mC[:], sc_.rearrange("p t a h -> p t h a"), op=ALU.max,
                                        axis=AX.X).then_inc(dveC1.done("mx"), 1)
                        dve.wait_ge(dveC1.sem, dveC1.count(e, "mx"))
                        ob = oobE[:].unsqueeze(1).to_broadcast([128, TT, H])
                        v.tensor_tensor(mC2[:], mC[:], ob, ALU.max).then_inc(dveC1.done("m2"), 1)
                        dve.wait_ge(dveC1.sem, dveC1.count(e, "m2"))
                        dve.wait_ge(actC1.sem, actC1.count(e - 1, "exp"))
                        v.tensor_tensor(ds[:, :, 0:NS, :], sc_, mC2[:].unsqueeze(2).to_broadcast([128, TT, NS, H]),
                                        ALU.subtract).then_inc(dveC1.done("sub"), 1)
                        v.tensor_tensor(ds[:, :, NS, :], ob, mC2[:], ALU.subtract).then_inc(dveC1.done("subo"), 1)
                    if g == 12 and (e := r["C1"]) is not None:
                        dve.wait_ge(actC1.sem, actC1.count(e, "exp"))
                        v.tensor_reduce(sC[:], es[:].rearrange("p t a h -> p t h a"), op=ALU.add,
                                        axis=AX.X).then_inc(dveC1.done("sum"), 1)
                        dve.wait_ge(dveC1.sem, dveC1.count(e, "sum"))
                        v.reciprocal(rC[:], sC[:]).then_inc(dveC1.done("rec"), 1)
                        dve.wait_ge(dveC1.sem, dveC1.count(e, "rec"))
                        dve.wait_ge(peC1.sem, peC1.count(e - 1, "wT"))
                        v.tensor_tensor(wn[:], es[:, :, 0:NS, :], rC[:].unsqueeze(2).to_broadcast([128, TT, NS, H]),
                                        ALU.mult).then_inc(dveC1.done("w"), 1)
                    if g == 11 and (e := r["C2"]) is not None:
                        dve.wait_ge(poolC2.sem, poolC2.count(e, "add", 4))
                        dve.wait_ge(actC1.sem, actC1.count(e, "g"))
                        dve.wait_ge(peC2.sem, peC2.count(e - 1, "out"))
                        v.scalar_tensor_tensor(gat[:], tg[par][:], 1.0, pv[:, 0, :], ALU.add,
                                               ALU.mult).then_inc(dveC2n.done("gt"), 1)
                    if g == 13 and (e := r["C2"]) is not None:
                        dve.wait_ge(peC2.sem, peC2.count(e, "out"))
                        dve.wait_ge(poolC2.sem, poolC2.count(e, "xb"))
                        dve.wait_ge(dveC2n.sem, dveC2n.count(e - 1, "nm", 1))
                        v.tensor_tensor(nC["y"][:].rearrange("p t c -> p (t c)"), b7[:, 0:T],
                                        x2b[:].rearrange("p t c -> p (t c)"), ALU.add).then_inc(dveC2n.done("res"), 1)
                        norm(dveC2n, e, nC, None, x3[par])
                    if g == 16 and (e := r["D"]) is not None:
                        dve.wait_ge(peD.sem, peD.count(e, "y"))
                        dve.wait_ge(dveDn.sem, dveDn.count(e - 1, "nm", 1))
                        dve.wait_ge(st_out, dma_count(e - 1))
                        v.tensor_tensor(nD["y"][:].rearrange("p t c -> p (t c)"), b7[:, 0:T],
                                        x3[odd][:].rearrange("p t c -> p (t c)"), ALU.add).then_inc(dveDn.done("res"), 1)
                        norm(dveDn, e, nD, None, xout)
                    if g == 19 and (e := r["B"]) is not None:
                        dve.wait_ge(peB.sem, peB.count(e, "z"))
                        dve.wait_ge(dveBn.sem, dveBn.count(e - 1, "nm", 1))
                        dve.wait_ge(poolC2.sem, poolC2.count(e - 2, "xb"))
                        dve.wait_ge(peC1.sem, peC1.count(e - 1, "xT"))
                        v.tensor_tensor(nB["y"][:].rearrange("p t c -> p (t c)"), b6[:, 0:T],
                                        x1[par][:].rearrange("p t c -> p (t c)"), ALU.add).then_inc(dveBn.done("res"), 1)
                        norm(dveBn, e, nB, None, x2[par])

            passes(dve, one)

        @block.gpsimd
        def _(pool):
            tt_ = nc.gpsimd.tensor_tensor
            pool.wait_ge(ld_const, 16 * N_CONST)
            pool.wait_ge(setup_dve, SETUP_DVE)

            def one(t, par, key):
                r = stages(t)
                odd = 1 - par
                for g in range(SLOTS):
                    if g == 0:
                        if (e := r["A3"]) is not None:
                            pool.wait_ge(ld_x, dma_count(e))
                            pool.wait_ge(dveA3.sem, dveA3.count(e - 1, "res"))
                            tt_(x0b[:], x0[:], bo0[:], ALU.add).then_inc(poolA3.done("xbo"), 1)
                        if (e := r["C2"]) is not None:
                            pool.wait_ge(dveC2n.sem, dveC2n.count(e - 1, "res"))
                            pool.wait_ge(dveBn.sem, dveBn.count(e, "nm", 1))
                            tt_(x2b[:], x2[par][:], boc[:], ALU.add).then_inc(poolC2.done("xb"), 1)
                    if 2 <= g < 6 and (e := r["C1"]) is not None:
                        if g == 2:
                            pool.wait_ge(actC1.sem, actC1.count(e, "k"))
                            pool.wait_ge(peC1.sem, peC1.count(e - 1, "sc"))
                            pool.wait_ge(peD.sem, peD.count(e + LAG["C1"] - LAG["D"] - 1, "y"))
                        for p in (2 * (g - 2), 2 * (g - 2) + 1):
                            tt_(prod[:, 2 * p:2 * p + 2, :], shifted(kC, p), qC[:].unsqueeze(1).to_broadcast([128, 2, T]),
                                ALU.mult).then_inc(poolC1.done("prod", p), 1)
                    if g == 6 and (e := r["C2"]) is not None:
                        pool.wait_ge(dveC2.sem, dveC2.count(e, "pv", 7))
                        for n, (a, b, w) in enumerate(((0, 8, 4), (4, 12, 4), (0, 4, 4), (0, 2, 2), (0, 1, 1))):
                            if n >= 2:
                                pool.wait_ge(poolC2.sem, poolC2.count(e, "add", n - 1))
                            tt_(pv[:, a:a + w, :], pv[:, a:a + w, :], pv[:, b:b + w, :],
                                ALU.add).then_inc(poolC2.done("add", n), 1)
                    if 10 <= g < 14 and (e := r["D"]) is not None:
                        i = g - 10
                        if i == 0:
                            pool.wait_ge(ld_cD, dma_count(e))
                            pool.wait_ge(actD.sem, actD.count(e, "xT"))
                            pool.wait_ge(peD.sem, peD.count(e - 1, "y"))
                            if (c1 := r["C1"]) is not None:
                                pool.wait_ge(peC1.sem, peC1.count(c1, "sc"))
                        tt_(xs[:, 2 * i:2 * i + 2, :].rearrange("p x (t n) -> p x t n", t=TT),
                            gD["cb"][:, :, 2 * i:2 * i + 2, :].rearrange("p t x n -> p x t n"),
                            x3T[:].rearrange("p (t n) -> p t n", t=TT).unsqueeze(1).to_broadcast([128, 2, TT, 128]),
                            ALU.mult).then_inc(poolD.done("xs", i), 1)
                    if 9 <= g < 18 and (e := r["B"]) is not None:
                        n = g - 9
                        pool.wait_ge(dveB.sem, dveB.count(e, "wu", 2 * n + 1))
                        if n == 0:
                            pool.wait_ge(peB.sem, peB.count(e - 1, "z"))
                        tt_(h9[:, n, :], wa[n % 2][:], ub[n % 2][:], ALU.mult).then_inc(poolB.done("h", n), 1)

            passes(pool, one)


def distance_tables():
    slopes = np.power(np.float32(2.0), np.float32(8.0) * np.arange(0, -H, -1, dtype=np.float32) / np.float32(H))
    i = np.arange(128)
    d = -slopes[:, None, None].astype(np.float64) * np.abs(i[:, None] - i[None, :])
    hi = d.astype(np.float16)
    lo = (d - hi.astype(np.float64)).astype(np.float16)
    dist = np.stack([hi, lo], 1).transpose(2, 0, 1, 3)

    def bf16(a):
        u = np.asarray(a, np.float32).view(np.uint32)
        u = ((u + 0x7FFF + ((u >> 16) & 1)) >> 16).astype(np.uint32)
        return u.astype(np.uint16), (u << 16).view(np.float32)

    def three(a):
        out, left = [], np.asarray(a, np.float64)
        for _ in range(3):
            bits, val = bf16(left.astype(np.float32))
            out.append(bits)
            left = left - val
        return out

    one = bf16(np.ones(1))[0][0]
    t = np.arange(T)
    first, second = t < 128, t >= 128
    rows = np.zeros((ROW_M + 1 - ROW_D, 2, H, T), np.uint16)
    far = slopes[:, None].astype(np.float64) * np.abs(t - 128)
    for n, part in enumerate(three(-far)):
        rows[n, 0] = np.where(first, one, 0)
        rows[n, 1] = np.where(second, part, 0)
        rows[3 + n, 0] = np.where(first, part, 0)
        rows[3 + n, 1] = np.where(second, one, 0)
        rows[6 + n, 0] = np.where(second, one, 0)
        rows[6 + n, 1] = np.where(first, part, 0)
        rows[9 + n, 0] = np.where(second, part, 0)
        rows[9 + n, 1] = np.where(first, one, 0)
    rows[ROW_M - ROW_D, 1] = one
    identb = np.zeros((128, 128), np.uint16)
    identb[i, i] = one
    return np.ascontiguousarray(dist), rows, identb


def kernel(**inputs):
    from concourse import bacc
    from concourse.bass_utils import run_bass_kernel_spmd

    a = {k: np.asarray(v) for k, v in inputs.items()}
    dh = np.arange(D).reshape(H, HD).T.reshape(-1)
    w, b = a["L0_attn_W_qkv"], a["L0_attn_b_qkv"]
    cw, cb = a["L1_attn_w_qkv"], a["L1_attn_b_qkv"]
    pos = a["L1_attn_pos_bias"]
    posd = np.full((128, 2, DUP), -1e30, pos.dtype)
    for p, pair in enumerate(PAIRS):
        for o2, shift in enumerate(pair):
            for n, i in enumerate(i for i, o in enumerate(OFFSETS) if o == shift):
                row = 32 * (p % 4) + 16 * o2
                posd[row:row + H, p // 4, n] = pos[i]
    dist, rows, identb = distance_tables()
    onesz = np.zeros((128, 4, 32), np.float32)
    hsum = np.zeros((128, 2, 32), np.float32)
    for r in range(4):
        onesz[:, r, HD * r:HD * r + HD] = 1
    for o2 in range(2):
        for p in range(128):
            hsum[p, o2, 16 * o2 + p % H] = 1
    b2 = np.zeros((128, TT, D), np.float32)
    for tt in range(TT):
        b2[64 * tt:64 * tt + E, tt] = a["L0_ffn_b2"]
        b2[64 * tt + E, tt] = a["L0_ffn_sb2"]
    ii = np.arange(E)
    arrays = {
        "x": a["L0_attn_x"],
        "xT": a["L0_attn_x"].reshape(B * T, D).T,
        "wqk0": np.stack([w[:D][dh].T, w[D:2 * D][dh].T], 1),
        "wv0": w[2 * D:].T,
        "wo0": a["L0_attn_W_out"].T,
        "bqk0": np.stack([b[:D][dh], b[D:2 * D][dh]], 1),
        "bv0": b[None, 2 * D:],
        "bo0": a["L0_attn_b_out"][None],
        "gw0": a["L0_ffn_gate_w"].T,
        "w13": np.stack([np.concatenate([a["L0_ffn_w1"], a["L0_ffn_sw1"][None]]),
                         np.concatenate([a["L0_ffn_w3"], a["L0_ffn_sw3"][None]])], 1).transpose(2, 0, 1, 3),
        "w2": np.concatenate([a["L0_ffn_w2"], a["L0_ffn_sw2"][None]]).transpose(1, 0, 2),
        "b1": np.concatenate([a["L0_ffn_b1"], a["L0_ffn_sb1"][None]]).T,
        "b3": np.concatenate([a["L0_ffn_b3"], a["L0_ffn_sb3"][None]]).T,
        "b2": b2,
        "wc": np.stack([cw[:, :D][:, dh], cw[:, D:2 * D][:, dh], cw[:, 2 * D:][:, dh],
                        a["L1_attn_w_gate"][:, dh]], 1),
        "bc": np.stack([cb[:D][dh], cb[D:2 * D][dh], cb[2 * D:][dh], a["L1_attn_b_gate"][dh]], 1),
        "woc": a["L1_attn_w_out"][dh],
        "boc": a["L1_attn_b_out"][None],
        "gw1": a["L1_ffn_gate_w"].T,
        "ew": a["L1_ffn_expert_w"].transpose(2, 0, 1),
        "posd": posd,
        "oobd": np.broadcast_to(pos[OOB].T, (128, H, len(OOB))),
        "ident": np.eye(128, dtype=np.float32),
        "identh": np.eye(128, dtype=np.float16),
        "identb": identb,
        "dist": dist,
        "rows": rows,
        "onesz": onesz,
        "hsum": hsum,
        "tri": np.broadcast_to((ii[None, :] < ii[:, None]).astype(np.float32).reshape(1, 1, -1),
                               (128, TT, E * E)).reshape(128, -1),
    }
    nc = bacc.Bacc("TRN2", target_bir_lowering=False, num_devices=1)
    feeds, aps = {}, {}
    for name, x in arrays.items():
        x = np.ascontiguousarray(x)
        feeds[f"in_{name}"] = x
        aps[name] = nc.dram_tensor(f"in_{name}", x.shape, mybir.dt.from_np(x.dtype), kind="ExternalInput").ap()
    out = nc.dram_tensor("out_x", (B, T, D), mybir.dt.float32, kind="ExternalOutput").ap()
    network(nc, aps, out)
    return run_bass_kernel_spmd(nc, [feeds], core_ids=[0]).results[0]["out_x"]
```

```python
import concourse.bass as bass
from concourse import mybir
from contextlib import ExitStack
import numpy as np

B, T, D = 32, 256, 128
H, HD = 16, 8
E = 8
TT = T // 128
EPS = 1e-5

N_SCALES, N_TAPS = 11, 4
OFFSETS = [(1 << j) * tau for j in range(N_SCALES) for tau in range(N_TAPS)]
SHIFTS = sorted({o for o in OFFSETS if o < T})
PAIRS = [(SHIFTS[2 * p + 1], SHIFTS[2 * p]) for p in range(len(SHIFTS) // 2)]
NP = len(PAIRS)
NS = len(SHIFTS)
PAD = max(SHIFTS)
DUP = max(sum(o == s for o in OFFSETS) for s in SHIFTS)
OOB = [i for i, o in enumerate(OFFSETS) if o >= T]

ROW_D, ROW_M = 9 * HD, 96

LAG = {"A1": 0, "M": 1, "A2": 1, "A3": 2, "B": 2, "B2": 3, "C1": 3, "C2": 4, "D": 4, "D2": 5}
NORMS = ("A3", "B2", "C2", "D2")
LAST = max(LAG.values())
LOOP_FROM = LAST + 1
SLOTS = 20
AB_SLOT = {9: 0, 12: 1, 13: 2, 14: 3, 15: 4, 16: 5, 17: 6, 18: 7, 19: 8}
PV_ORDER = (0, 1, 4, 5, 2, 3, 6, 7)
PV_SLOT = {17: (0,), 18: (1,), 19: (2, 3), 0: (4, 5, 6, 7)}


class Steps:

    def __init__(self, sem, steps):
        self.sem, self.names = sem, []
        for s in steps.split():
            name, _, n = s.partition("*")
            self.names += [(name, i) for i in range(int(n or 1))]
        self.per_run = len(self.names)
        self.at = 0

    def done(self, name, i=0):
        assert self.names[self.at] == (name, i), (self.names[self.at], name, i)
        self.at = (self.at + 1) % self.per_run
        return self.sem

    def count(self, e, name, i=0):
        return 0 if isinstance(e, int) and e < 0 else e * self.per_run + (self.names.index((name, i)) + 1)


def dma_count(e, per_run=1):
    return 0 if isinstance(e, int) and e < 0 else (e + 1) * (16 * per_run)


def network(nc, A, out):
    F, BF, H16, I32, U16 = (mybir.dt.float32, mybir.dt.bfloat16, mybir.dt.float16, mybir.dt.int32,
                            mybir.dt.uint16)
    ALU, ACT, AX = mybir.AluOpType, mybir.ActivationFunctionType, mybir.AxisListType
    ctx = ExitStack()
    with ctx:
        def sb(name, shape, dt=F):
            return ctx.enter_context(nc.sbuf_tensor(name, shape, dt))

        def bank(name):
            return ctx.enter_context(nc.psum_tensor(name, [128, 512], F))

        def sem(name):
            return ctx.enter_context(nc.semaphore(name))

        def steps(name, s):
            return Steps(sem(name), s)

        wqk0, wv0, wo0 = sb("wqk0", [128, 2, 128]), sb("wv0", [128, 128]), sb("wo0", [128, 128])
        bqk0, bv0, bo0 = sb("bqk0", [128, 2]), sb("bv0", [128, TT, 128]), sb("bo0", [128, TT, 128])
        gw0, gw1 = sb("gw0", [128, E]), sb("gw1", [128, E])
        w13, w2 = sb("w13", [128, E + 1, 2, 128]), sb("w2", [128, E + 1, 128])
        b1, b1h, b3, b2 = sb("b1", [128, E + 1]), sb("b1h", [128, E + 1]), sb("b3", [128, E + 1]), sb("b2", [128, TT, 128])
        wc, bc = sb("wc", [128, 4, 128]), sb("bc", [128, 4])
        woc, boc = sb("woc", [128, 128]), sb("boc", [128, TT, 128])
        ew = sb("ew", [128, E, 128])
        ident, identb, identh = sb("ident", [128, 128]), sb("identb", [128, 128], BF), sb("identh", [128, 128], H16)
        dist = sb("dist", [128, H, 2, 128], H16)
        onesz, hsum = sb("onesz", [128, 4, 32]), sb("hsum", [128, 2, 32])
        tri = sb("tri", [128, TT * E * E])
        posd, oobd = sb("posd", [128, 2, DUP]), sb("oobd", [128, H, len(OOB)])
        posm, poss, posE = sb("posm", [128, 2]), sb("poss", [128, 2]), sb("posE", [128, 2])
        oobm, oobs, oobE = sb("oobm", [128, H]), sb("oobs", [128, H]), sb("oobE", [128, H])

        xT = sb("xT", [128, T])
        x0, x2b = sb("x0", [128, TT, D]), sb("x2b", [128, TT, D])
        x0b = x0
        qk = sb("qk", [128, 2, T])
        rest = qk
        parts = sb("parts", [128, 2, 3, T], BF)
        stack = [sb(f"stack{i}", [ROW_M + 1, 2, H, T], BF) for i in range(2)]
        Vz = [sb(f"Vz{i}", [128, TT, 4, 160]) for i in range(2)]
        mx, mneg, mT = sb("mx", [128, TT, H]), sb("mneg", [128, TT, H], BF), sb("mT", [H, T], BF)
        P = [sb(f"P{i}", [128, TT, T]) for i in range(8)]
        rden, attnT = sb("rden", [128, T]), sb("attnT", [128, T])
        x1, x2, x3 = (sb(f"x{n}", [128, TT, D]) for n in (1, 2, 3))
        xout = sb("xout", [128, TT, D])

        def norm_buffers(n):
            return dict(y=sb(n + "y", [128, TT, D]), st=sb(n + "st", [128, TT, 6]), tick=sb(n + "tick", [128, TT]),
                        row="ABCD".index(n[1]))

        def gate_buffers(n):
            return dict(L=sb(n + "L", [128, TT, E]), mx=sb(n + "mx", [128, TT]), dl=sb(n + "dl", [128, TT, E]),
                        gt=sb(n + "gt", [128, TT * E * E]), eq=sb(n + "eq", [128, TT * E * E]),
                        rank=sb(n + "rank", [128, TT, E]), ge=sb(n + "ge", [128, TT, E]),
                        sel=sb(n + "sel", [128, TT, E]), sum=sb(n + "sum", [128, TT]), rec=sb(n + "rec", [128, TT]),
                        c=sb(n + "c", [128, TT, 64]), cT=sb(n + "cT", [128, 128]),
                        cb=sb(n + "cb", [128, TT, E, 128]))

        nA, nB, nC, nD = (norm_buffers("n" + n) for n in "ABCD")
        n_mv, n_v, n_i = sb("n_mv", [128, 4, TT, 2]), sb("n_v", [128, 4, TT]), sb("n_i", [128, 4, TT], I32)
        n_r, n_s = sb("n_r", [128, 4, TT]), sb("n_s", [128, 4, TT])
        gB, gD = gate_buffers("gB"), gate_buffers("gD")
        x1T = sb("x1T", [128, T])
        th, bb, wa, ub = ([sb(f"{n}{i}", [128, T]) for i in range(2)] for n in ("th", "bb", "wa", "ub"))
        h9 = sb("h9", [128, E + 1, T])
        x2T, qC, kC = sb("x2T", [128, T]), sb("qC", [128, T]), sb("kC", [128, PAD + T])
        vC, tg = sb("vC", [128, PAD + T]), sb("tg", [128, T])
        prod = sb("prod", [128, NS, T])
        ds = sb("ds", [128, TT, NS + 1, H])
        es = ds
        mC, mC2, sC, rC = (sb(n, [128, TT, H]) for n in ("mC", "mC2", "sC", "rC"))
        wn, wT = sb("wn", [128, TT, NS, H]), sb("wT", [128, 2, T])
        scs = wT
        wb = sb("wb", [128, NS, T])
        pv = wb
        gat = sb("gat", [128, T])
        x3T = sb("x3T", [128, T])
        xs = prod

        bS, bTU = [bank("bS0"), bank("bS1")], [bank("bTU0"), bank("bTU1"), bank("bTU2")]
        bPV, b6, b7 = bank("bPV"), bank("b6"), bank("b7")
        turn = []
        for g in range(SLOTS):
            turn += [("ST", g - 3)] * (3 <= g < 19) + [("ab", AB_SLOT.get(g))] * (g in AB_SLOT)

        def turn_bank(what, n):
            return turn.index((what, n)) % 3

        d_parts = nc.dram_tensor("d_parts", (2, 3, 128, T), BF, kind="Internal").ap()
        d_w = nc.dram_tensor("d_w", (2, 128, T), F, kind="Internal").ap()
        d_cB = nc.dram_tensor("d_cB", (TT, E, 128), F, kind="Internal").ap()
        d_cD = nc.dram_tensor("d_cD", (TT, E, 128), F, kind="Internal").ap()

        LN = "res bn*2 ag*2 nm*2"
        GATE = "cp gmx sub gt eq eqt add rank sel sum rec c"
        peA1 = steps("peA1", "qk v S*16")
        peM = steps("peM", "mT")
        peA2, pePV = steps("peA2", "ST*16"), steps("pePV", "PV*4")
        peA3 = steps("peA3", "out")
        peB = steps("peB", "xT lg cT ab*9 z")
        peC1 = steps("peC1", "xT qk vg sc scT wT")
        peC2 = steps("peC2", "out")
        peD = steps("peD", "xT lg cT y")
        actA1 = steps("actA1", "q k")
        actM = steps("actM", "mT")
        actA2 = steps("actA2", "exp*16")
        actB = steps("actB", "xT ge cT ab*18")
        actC1 = steps("actC1", "xT q k v g exp wT")
        actD = steps("actD", "xT ge cT")
        dveA1 = steps("dveA1", "hi rest mid lo v max*16")
        dveM = steps("dveM", "neg")
        dveA3 = steps("dveA3", "rec num " + LN)
        dveBg = steps("dveBg", GATE)
        dveB = steps("dveB", "wu*18")
        dveBn = steps("dveBn", LN)
        dveC1 = steps("dveC1", "sc*2 mx m2 sub subo sum rec w")
        dveC2 = steps("dveC2", "pv*8")
        dveC2n = steps("dveC2n", "add*2 gt " + LN)
        dveN = steps("dveN", "ve sh mg nt*9")
        dveDg = steps("dveDg", GATE)
        dveDn = steps("dveDn", LN)
        poolA3 = steps("poolA3", "xbo")
        poolB = steps("poolB", "h*9")
        poolC1 = steps("poolC1", "prod*8")
        poolC2 = steps("poolC2", "xb add*3")
        poolD = steps("poolD", "xs*4")
        ld_const, ld_xT, ld_x = sem("ld_const"), sem("ld_xT"), sem("ld_x")
        st_parts, ld_stack, ld_m = sem("st_parts"), sem("ld_stack"), sem("ld_m")
        st_cB, ld_cB, st_cD, ld_cD = sem("st_cB"), sem("ld_cB"), sem("st_cD"), sem("ld_cD")
        st_w, ld_w, st_out = sem("st_w"), sem("ld_w"), sem("st_out")
        setup_dve, setup_act = sem("setup_dve"), sem("setup_act")
        SETUP_DVE, SETUP_ACT = 17, 9
        N_STACK, N_W = 12, HD

        consts = [(wqk0, "wqk0"), (wv0, "wv0"), (wo0, "wo0"), (bqk0, "bqk0"), (gw0, "gw0"), (gw1, "gw1"),
                  (w13, "w13"), (w2, "w2"), (b1, "b1"), (b3, "b3"), (b2, "b2"), (wc, "wc"), (bc, "bc"), (woc, "woc"),
                  (ew, "ew"), (ident, "ident"), (identh, "identh"), (dist, "dist"),
                  (onesz, "onesz"), (hsum, "hsum"), (tri, "tri"), (posd, "posd"), (oobd, "oobd")]
        N_CONST = len(consts) + 1 + 3 * TT + 4

        x_rows = A["x"].rearrange("b (t p) c -> p (b t) c", p=128)
        out_rows = out.rearrange("b (t p) c -> p (b t) c", p=128)

        def head(k):
            return 4 * (k % 4) + k // 4

        def expert(n):
            return E if n == 0 else n - 1

        def shifted(x, p):
            hi, lo = PAIRS[p]
            return bass.AP(x, PAD - hi, [[PAD + T, 128], [hi - lo, 2], [1, T]])

        def stages(t):
            r = {}
            for s, lag in LAG.items():
                e = t - lag
                r[s] = None if isinstance(e, int) and not 0 <= e < B else e
            return r

        def passes(eng, one):
            for t in range(LOOP_FROM):
                one(t, t % 2, t)
            with eng.Fori(0, (B - LOOP_FROM) // 2) as r:
                for u in range(2):
                    one(r * 2 + (LOOP_FROM + u), (LOOP_FROM + u) % 2, LOOP_FROM + u)
            for t in range(B, B + LAST):
                one(t, t % 2, t)

        block = ctx.enter_context(nc.Block())

        @block.sync
        def _(sp):
            for dst, name in consts:
                sp.dma_start(dst[:], A[name]).then_inc(ld_const, 16)
            sp.dma_start(identb[:].bitcast(U16), A["identb"]).then_inc(ld_const, 16)
            for tt in range(TT):
                for dst, name in ((bv0, "bv0"), (bo0, "bo0"), (boc, "boc")):
                    sp.dma_start(dst[:, tt, :], bass.AP(A[name].tensor, 0, [[0, 128], [1, 128]])).then_inc(ld_const, 16)
            for i in range(2):
                for s in range(2):
                    n = ROW_M + s - ROW_D
                    sp.dma_start(stack[i][ROW_D:ROW_D + n, s].bitcast(U16),
                                 A["rows"][0:n, s]).then_inc(ld_const, 16)

            def one(t, par, key):
                r = stages(t)
                for g in range(SLOTS):
                    if g == 0:
                        if (e := r["A1"]) is not None:
                            sp.wait_ge(peA1.sem, peA1.count(e - 1, "v"))
                            sp.dma_start(xT[:], A["xT"][:, bass.ds(e * T, T)]).then_inc(ld_xT, 16)
                        if (e := r["A3"]) is not None:
                            sp.wait_ge(dveA3.sem, dveA3.count(e - 1, "res"))
                            sp.dma_start(x0[:], x_rows[:, bass.ds(e * TT, TT), :]).then_inc(ld_x, 16)
                        if (e := r["M"]) is not None:
                            sp.wait_ge(actM.sem, actM.count(e, "mT"))
                            sp.dma_start(stack[1 - par][ROW_M:ROW_M + 1, 0], mT[:]).then_inc(ld_m, 16)
                    if g == 2 and (e := r["A1"]) is not None:
                        sp.wait_ge(ld_stack, dma_count(e - 1, N_STACK))
                        sp.wait_ge(dveA1.sem, dveA1.count(e, "lo"))
                        for s in range(2):
                            sp.dma_start(d_parts[s].rearrange("a p n -> p a n"), parts[:, s]).then_inc(st_parts, 16)
                        sp.wait_ge(st_parts, dma_count(e, 2))
                        sp.wait_ge(peA2.sem, peA2.count(e - 2, "ST", 15))
                        for kp in range(3):
                            sp.dma_start(stack[par][24 * kp:24 * kp + 24, 0].rearrange("p h n -> p (h n)"),
                                         bass.AP(d_parts.tensor, 0, [[H * T, 24], [1, H * T]])).then_inc(ld_stack, 16)
                            for qp in range(3):
                                sp.dma_start(stack[par][24 * kp + 8 * qp:24 * kp + 8 * qp + 8, 1].rearrange("p h n -> p (h n)"),
                                             bass.AP(d_parts.tensor, (3 + kp) * 128 * T,
                                                     [[H * T, 8], [1, H * T]])).then_inc(ld_stack, 16)
                    if g == 8:
                        for st, dg, dr, st_s, ld_s, act, used in (("B", gB, d_cB, st_cB, ld_cB, actB, (dveB, "wu", 16)),
                                                                  ("D", gD, d_cD, st_cD, ld_cD, actD, (poolD, "xs", 3))):
                            if (e := r[st]) is not None:
                                sp.wait_ge(ld_s, dma_count(e - 1))
                                sp.wait_ge(act.sem, act.count(e, "cT"))
                                for tt in range(TT):
                                    sp.dma_start(dr[tt], dg["cT"][64 * tt:64 * tt + E, :]).then_inc(st_s, 16)
                        for st, dg, dr, st_s, ld_s, act, used in (("B", gB, d_cB, st_cB, ld_cB, actB, (dveB, "wu", 16)),
                                                                  ("D", gD, d_cD, st_cD, ld_cD, actD, (poolD, "xs", 3))):
                            if (e := r[st]) is not None:
                                sp.wait_ge(st_s, dma_count(e, TT))
                                sp.wait_ge(used[0].sem, used[0].count(e - 1, used[1], used[2]))
                                sp.dma_start(dg["cb"][:].rearrange("p a b n -> p (a b n)"),
                                             bass.AP(dr.tensor, 0, [[0, 128], [1, TT * E * 128]])).then_inc(ld_s, 16)
                    if g == 14 and (e := r["C1"]) is not None:
                        sp.wait_ge(ld_w, dma_count(e - 1, N_W))
                        sp.wait_ge(actC1.sem, actC1.count(e, "wT"))
                        sp.dma_start(d_w.rearrange("s p n -> p s n"), wT[:]).then_inc(st_w, 16)
                        sp.wait_ge(st_w, dma_count(e))
                        sp.wait_ge(dveC2n.sem, dveC2n.count(e - 1, "gt"))
                        for d in range(HD):
                            sp.dma_start(wb[H * d:H * d + H].rearrange("p (s j) n -> p s j n", s=2),
                                         bass.AP(d_w.tensor, 0, [[T, H], [128 * T, 2], [H * T, NP], [1, T]])
                                         ).then_inc(ld_w, 16)
                    if g == 6 and (e := r["D2"]) is not None:
                        sp.wait_ge(dveDn.sem, dveDn.count(e, "nm", 1))
                        sp.dma_start(out_rows[:, bass.ds(e * TT, TT), :], xout[:]).then_inc(st_out, 16)

            passes(sp, one)
            sp.wait_ge(st_out, dma_count(B - 1))

        @block.tensor
        def _(pe):
            mm = nc.tensor.matmul
            pe.wait_ge(ld_const, 16 * N_CONST)
            pe.wait_ge(setup_dve, SETUP_DVE)
            pe.wait_ge(setup_act, SETUP_ACT)
            last = {b: None for b in (0, 1, 2, 6, 7)}

            def take(bank_no, now, t):
                if last[bank_no]:
                    st, s, name, i, when = last[bank_no]
                    pe.wait_ge(s.sem, s.count(when - LAG[st], name, i))
                last[bank_no] = (*now, t)

            def one(t, par, key):
                if key == LOOP_FROM and not isinstance(t, int):
                    for b in last:
                        last[b] = (*last[b][:4], t - 1)
                if isinstance(t, int) and t == B:
                    for b in last:
                        last[b] = (*last[b][:4], B - 1)
                r = stages(t)
                odd = 1 - par
                for g in range(SLOTS):
                    if g == 0 and (e := r["A1"]) is not None:
                        take(6, ("A1", actA1, "k", 0), t)
                        pe.wait_ge(ld_xT, dma_count(e))
                        mm(b6[:, 0:T], wqk0[:, 0, :], xT[:], start=True, stop=True)
                        mm(b6[:, T:2 * T], wqk0[:, 1, :], xT[:], start=True, stop=True).then_inc(peA1.done("qk"), 1)
                    if g in (0, 7, 11, 15) and (e := r["A2" if g else "A3"]) is not None:
                        rr = (g - 7) // 4 if g else 3
                        pe.wait_ge(actA2.sem, actA2.count(e, "exp", 4 * rr + 3))
                        if rr == 0:
                            pe.wait_ge(dveA3.sem, dveA3.count(e - 1, "num"))
                            pe.wait_ge(dveA1.sem, dveA1.count(e, "v"))
                        vz = Vz[odd if g else par]
                        for kt in range(TT):
                            for den in range(2):
                                for j in range(4):
                                    k = 4 * rr + j
                                    lhs = onesz[:, rr, :] if den else vz[:, kt, j, 32 * rr:32 * rr + 32]
                                    i = mm(bPV[32 * j:32 * j + 32, den * T:den * T + T], lhs, P[k % 8][:, kt, :],
                                           start=(rr == 0 and kt == 0 and den == 0), stop=(rr == 3 and kt == 1),
                                           skip_group_check=True)
                        i.then_inc(pePV.done("PV", rr), 1)
                    if g == 0 and (e := r["M"]) is not None:
                        take(7, ("M", actM, "mT", 0), t)
                        pe.wait_ge(dveM.sem, dveM.count(e, "neg"))
                        o = b7[:].bitcast(BF)
                        for tt in range(TT):
                            i = nc.tensor.transpose(o[0:H, tt * 128:tt * 128 + 128], mneg[:, tt, :], identb[:])
                        i.then_inc(peM.done("mT"), 1)
                    if g == 1 and (e := r["D2"]) is not None:
                        take(7, ("D2", dveDn, "res", 0), t)
                        for tt in range(TT):
                            for x in range(E):
                                if tt == 0 and x % 2 == 0:
                                    pe.wait_ge(poolD.sem, poolD.count(e, "xs", x // 2))
                                i = mm(b7[:, tt * 128:tt * 128 + 128], xs[:, x, tt * 128:tt * 128 + 128], ew[:, x, :],
                                       start=(x == 0), stop=(x == E - 1))
                        i.then_inc(peD.done("y"), 1)
                    if g == 2:
                        if (e := r["A3"]) is not None:
                            take(6, ("A3", dveA3, "res", 0), t)
                            pe.wait_ge(dveA3.sem, dveA3.count(e, "num"))
                            for tt in range(TT):
                                i = mm(b6[:, tt * 128:tt * 128 + 128], attnT[:, tt * 128:tt * 128 + 128], wo0[:],
                                       start=True, stop=True)
                            i.then_inc(peA3.done("out"), 1)
                        if (e := r["B2"]) is not None:
                            take(6, ("B2", dveBn, "res", 0), t)
                            pe.wait_ge(actB.sem, actB.count(e, "cT"))
                            for tt in range(TT):
                                mm(b6[:, tt * 128:tt * 128 + 128], gB["cT"][:], b2[:, tt, :], start=True, stop=False)
                                for n in range(E + 1):
                                    if tt == 0:
                                        pe.wait_ge(poolB.sem, poolB.count(e, "h", n))
                                    i = mm(b6[:, tt * 128:tt * 128 + 128], h9[:, n, tt * 128:tt * 128 + 128],
                                           w2[:, expert(n), :], start=False, stop=(n == E))
                            i.then_inc(peB.done("z"), 1)
                    if g == 0 and (e := r["A1"]) is not None:
                        take(6, ("A1", dveA1, "v", 0), t)
                        for tt in range(TT):
                            i = mm(b6[:, tt * 128:tt * 128 + 128], xT[:, tt * 128:tt * 128 + 128], wv0[:],
                                   start=True, stop=True)
                        i.then_inc(peA1.done("v"), 1)
                    if g == 4 and (e := r["C2"]) is not None:
                        take(7, ("C2", dveC2n, "res", 0), t)
                        pe.wait_ge(dveC2n.sem, dveC2n.count(e, "gt"))
                        for tt in range(TT):
                            i = mm(b7[:, tt * 128:tt * 128 + 128], gat[:, tt * 128:tt * 128 + 128], woc[:],
                                   start=True, stop=True)
                        i.then_inc(peC2.done("out"), 1)
                    if g == 6:
                        for st, bk, bn, s, act, src, prev in (("C1", b7, 7, peC1, actC1, x2, dveBn),
                                                              ("B", b6, 6, peB, actB, x1, dveA3),
                                                              ("D", b6, 6, peD, actD, x3, dveC2n)):
                            if (e := r[st]) is not None:
                                take(bn, (st, act, "xT", 0), t)
                                pe.wait_ge(prev.sem, prev.count(e, "nm", 1))
                                for tt in range(TT):
                                    i = nc.tensor.transpose(bk[:, tt * 128:tt * 128 + 128], src[:, tt, :], ident[:])
                                i.then_inc(s.done("xT"), 1)
                            if st == "B" and (e := r["C1"]) is not None:
                                take(7, ("C1", actC1, "k", 0), t)
                                pe.wait_ge(actC1.sem, actC1.count(e, "xT"))
                                mm(b7[:, 0:T], wc[:, 0, :], x2T[:], start=True, stop=True)
                                mm(b7[:, T:2 * T], wc[:, 1, :], x2T[:], start=True,
                                   stop=True).then_inc(peC1.done("qk"), 1)
                    if g == 7:
                        for st, bk, bn, s, act, xt, gw, dg in (("B", b6, 6, peB, actB, x1T, gw0, dveBg),
                                                               ("D", b6, 6, peD, actD, x3T, gw1, dveDg)):
                            if (e := r[st]) is not None:
                                take(bn, (st, dg, "cp", 0), t)
                                pe.wait_ge(act.sem, act.count(e, "xT"))
                                for tt in range(TT):
                                    i = mm(bk[:, tt * E:tt * E + E], xt[:, tt * 128:tt * 128 + 128], gw[:],
                                           start=True, stop=True)
                                i.then_inc(s.done("lg"), 1)
                            if st == "B" and (e := r["C1"]) is not None:
                                take(7, ("C1", actC1, "g", 0), t)
                                mm(b7[:, 0:T], wc[:, 2, :], x2T[:], start=True, stop=True)
                                mm(b7[:, T:2 * T], wc[:, 3, :], x2T[:], start=True,
                                   stop=True).then_inc(peC1.done("vg"), 1)
                    if g == 9:
                        for st, bk, bn, s, act, dg, gb in (("B", b6, 6, peB, actB, dveBg, gB),
                                                           ("D", b7, 7, peD, actD, dveDg, gD)):
                            if (e := r[st]) is not None:
                                take(bn, (st, act, "cT", 0), t)
                                pe.wait_ge(dg.sem, dg.count(e, "c"))
                                nc.tensor.transpose(bk[:, 0:128], gb["c"][:].rearrange("p a b -> p (a b)"),
                                                    ident[:]).then_inc(s.done("cT"), 1)
                    if 3 <= g < 19 and (e := r["A2"]) is not None:
                        k = g - 3
                        h = head(k)
                        if k == 0:
                            pe.wait_ge(ld_m, dma_count(e))
                        take(turn_bank("ST", k), ("A2", actA2, "exp", k), t)
                        o = bTU[turn_bank("ST", k)]
                        for kt in range(TT):
                            q = slice(kt * T, kt * T + T)
                            c = slice(kt * T + kt * 128, kt * T + kt * 128 + 128)
                            mm(o[:, q], stack[odd][0:ROW_M + 1, 1, h, kt * 128:kt * 128 + 128],
                               stack[odd][0:ROW_M + 1, 0, h, :], start=True, stop=False)
                            last_part = h % 2 == 0
                            i = mm(o[:, c], identh[:], dist[:, h, 0, :], start=False, stop=last_part)
                            if not last_part:
                                i = mm(o[:, c], identh[:], dist[:, h, 1, :], start=False, stop=True)
                        i.then_inc(peA2.done("ST", k), 1)
                    if g >= 5 and (e := r["A1"]) is not None:
                        for k in ((0, 1) if g == 5 else (g - 4,)):
                            if k == 0:
                                pe.wait_ge(ld_stack, dma_count(e, N_STACK))
                            if k >= 2:
                                pe.wait_ge(dveA1.sem, dveA1.count(e, "max", k - 2))
                            else:
                                pe.wait_ge(dveA1.sem, dveA1.count(e - 1, "max", k + 14))
                            o = bS[k % 2]
                            h = k
                            for qt in range(TT):
                                mm(o[:, qt * T:qt * T + T], stack[par][0:ROW_M, 0, h, qt * 128:qt * 128 + 128],
                                   stack[par][0:ROW_M, 1, h, :], start=True, stop=False)
                                c = slice(qt * T + qt * 128, qt * T + qt * 128 + 128)
                                i = mm(o[:, c], identh[:], dist[:, h, 0, :], start=False, stop=True)
                            i.then_inc(peA1.done("S", k), 1)
                    if g in AB_SLOT and (e := r["B"]) is not None:
                        n = AB_SLOT[g]
                        x = expert(n)
                        take(turn_bank("ab", n), ("B", dveB, "wu", 2 * n), t)
                        bAB = bTU[turn_bank("ab", n)]
                        mm(bAB[:, 0:T], w13[:, x, 0, :], x1T[:], start=True, stop=True)
                        mm(bAB[:, T:2 * T], w13[:, x, 1, :], x1T[:], start=True, stop=True).then_inc(peB.done("ab", n), 1)
                    if g == 11 and (e := r["C1"]) is not None:
                        take(7, ("C1", dveC1, "sc", 1), t)
                        pe.wait_ge(poolC1.sem, poolC1.count(e, "prod", 7))
                        for s in range(2):
                            for o2 in range(2):
                                for j in range(4):
                                    i = mm(b7[32 * j:32 * j + 32, s * T:s * T + T], hsum[:, o2, :],
                                           prod[:, 2 * (4 * s + j) + o2, :], start=(s == 0 and o2 == 0), stop=o2 == 1,
                                           skip_group_check=True)
                        i.then_inc(peC1.done("sc"), 1)
                    if g == 12 and (e := r["C1"]) is not None:
                        take(7, ("C1", dveC1, "sub", 0), t)
                        for tt in range(TT):
                            for s in range(2):
                                i = nc.tensor.transpose(b7[:, tt * T + s * 128:tt * T + s * 128 + 128],
                                                        scs[:, s, tt * 128:tt * 128 + 128], ident[:])
                        i.then_inc(peC1.done("scT"), 1)
                    if g == 14 and (e := r["C1"]) is not None:
                        take(7, ("C1", actC1, "wT", 0), t)
                        pe.wait_ge(dveC1.sem, dveC1.count(e, "w"))
                        wv = wn[:].rearrange("p t a h -> p t (a h)")
                        for s in range(2):
                            for tt in range(TT):
                                i = nc.tensor.transpose(b7[:, s * T + tt * 128:s * T + tt * 128 + 128],
                                                        wv[:, tt, s * 128:s * 128 + 128], ident[:])
                        i.then_inc(peC1.done("wT"), 1)

            passes(pe, one)

        @block.scalar
        def _(act):
            act.wait_ge(ld_const, 16 * N_CONST)
            q_scale = HD ** -0.5
            nc.scalar.mul(bqk0[:, 0:1], bqk0[:, 0:1], q_scale).then_inc(setup_act, 1)
            nc.scalar.mul(b3[:], b3[:], 0.5).then_inc(setup_act, 1)
            nc.scalar.mul(bc[:, 0:1], bc[:, 0:1], q_scale).then_inc(setup_act, 1)
            nc.scalar.mul(bc[:, 3:4], bc[:, 3:4], 0.5).then_inc(setup_act, 1)
            nc.scalar.mul(woc[:], woc[:], 0.5).then_inc(setup_act, 1)
            act.wait_ge(setup_dve, 13)
            nc.scalar.activation(posd[:], posd[:], ACT.Exp).then_inc(setup_act, 1)
            nc.scalar.activation(oobd[:], oobd[:], ACT.Exp).then_inc(setup_act, 1)
            act.wait_ge(setup_dve, 15)
            nc.scalar.activation(posE[:], poss[:], ACT.Ln).then_inc(setup_act, 1)
            nc.scalar.activation(oobE[:], oobs[:], ACT.Ln).then_inc(setup_act, 1)
            act.wait_ge(setup_act, SETUP_ACT)
            act.wait_ge(setup_dve, SETUP_DVE)

            def one(t, par, key):
                r = stages(t)
                odd = 1 - par
                act_f = nc.scalar.activation
                for g in range(SLOTS):
                    if g == 0 and (e := r["A1"]) is not None:
                        act.wait_ge(peA1.sem, peA1.count(e, "qk"))
                        act.wait_ge(dveA1.sem, dveA1.count(e - 1, "lo"))
                        act_f(qk[:, 0, :], b6[:, 0:T], ACT.Identity, bias=bqk0[:, 0:1],
                              scale=q_scale).then_inc(actA1.done("q"), 1)
                        act_f(qk[:, 1, :], b6[:, T:2 * T], ACT.Identity, bias=bqk0[:, 1:2]).then_inc(actA1.done("k"), 1)
                    if g == 0 and (e := r["M"]) is not None:
                        act.wait_ge(peM.sem, peM.count(e, "mT"))
                        act.wait_ge(ld_m, dma_count(e - 1))
                        nc.scalar.copy(mT[:], b7[:].bitcast(BF)[0:H, 0:T]).then_inc(actM.done("mT"), 1)
                    if g == 6:
                        if (e := r["C1"]) is not None:
                            act.wait_ge(peC1.sem, peC1.count(e, "xT"))
                            nc.scalar.copy(x2T[:], b7[:, 0:T]).then_inc(actC1.done("xT"), 1)
                        if (e := r["B"]) is not None:
                            act.wait_ge(peB.sem, peB.count(e, "xT"))
                            act.wait_ge(peB.sem, peB.count(e - 1, "ab", 8))
                            nc.scalar.copy(x1T[:], b6[:, 0:T]).then_inc(actB.done("xT"), 1)
                        if (e := r["C1"]) is not None:
                            act.wait_ge(peC1.sem, peC1.count(e, "qk"))
                            act.wait_ge(poolC1.sem, poolC1.count(e - 1, "prod", 7))
                            act_f(qC[:], b7[:, 0:T], ACT.Identity, bias=bc[:, 0:1], scale=q_scale).then_inc(actC1.done("q"), 1)
                            act_f(kC[:, PAD:], b7[:, T:2 * T], ACT.Identity, bias=bc[:, 1:2]).then_inc(actC1.done("k"), 1)
                        if (e := r["D"]) is not None:
                            act.wait_ge(peD.sem, peD.count(e, "xT"))
                            act.wait_ge(poolD.sem, poolD.count(e - 1, "xs", 3))
                            nc.scalar.copy(x3T[:], b6[:, 0:T]).then_inc(actD.done("xT"), 1)
                    if g == 7 and (e := r["C1"]) is not None:
                        act.wait_ge(peC1.sem, peC1.count(e, "vg"))
                        act.wait_ge(dveC2.sem, dveC2.count(e - 1, "pv", 7))
                        act.wait_ge(dveC2n.sem, dveC2n.count(e - 1, "gt"))
                        act_f(vC[:, PAD:], b7[:, 0:T], ACT.Identity, bias=bc[:, 2:3]).then_inc(actC1.done("v"), 1)
                        act_f(tg[:], b7[:, T:2 * T], ACT.Tanh, bias=bc[:, 3:4], scale=0.5).then_inc(actC1.done("g"), 1)
                    if g == 8:
                        for st, s, dg, gb in (("B", actB, dveBg, gB), ("D", actD, dveDg, gD)):
                            if (e := r[st]) is not None:
                                act.wait_ge(dg.sem, dg.count(e, "sub"))
                                act.wait_ge(dg.sem, dg.count(e - 1, "sum"))
                                act_f(gb["ge"][:], gb["dl"][:], ACT.Exp).then_inc(s.done("ge"), 1)
                    if g == 9:
                        for st, s, p, gb, bk, used in (("B", actB, peB, gB, b6, (peB, "z")), ("D", actD, peD, gD, b7, None)):
                            if (e := r[st]) is not None:
                                act.wait_ge(p.sem, p.count(e, "cT"))
                                act.wait_ge(st_cB if st == "B" else st_cD, dma_count(e - 1, TT))
                                if used:
                                    act.wait_ge(used[0].sem, used[0].count(e - 1, used[1]))
                                nc.scalar.copy(gb["cT"][:], bk[:, 0:128]).then_inc(s.done("cT"), 1)
                    if 3 <= g < 19 and (e := r["A2"]) is not None:
                        k = g - 3
                        act.wait_ge(peA2.sem, peA2.count(e, "ST", k))
                        if k >= 8:
                            act.wait_ge(pePV.sem, pePV.count(e, "PV", (k - 8) // 4))
                        else:
                            act.wait_ge(pePV.sem, pePV.count(e - 1, "PV", (k + 8) // 4))
                        act_f(P[k % 8][:].rearrange("p a b -> p (a b)"), bTU[turn_bank("ST", k)][:], ACT.Exp).then_inc(actA2.done("exp", k), 1)
                    if g in AB_SLOT and (e := r["B"]) is not None:
                        n = AB_SLOT[g]
                        x = expert(n)
                        act.wait_ge(peB.sem, peB.count(e, "ab", n))
                        if n >= 2:
                            act.wait_ge(dveB.sem, dveB.count(e, "wu", 2 * n - 3))
                        else:
                            act.wait_ge(dveB.sem, dveB.count(e - 1, "wu", 17))
                        bAB = bTU[turn_bank("ab", n)]
                        act_f(th[n % 2][:], bAB[:, 0:T], ACT.Tanh, bias=b1h[:, x:x + 1], scale=0.5).then_inc(actB.done("ab", 2 * n), 1)
                        act_f(bb[n % 2][:], bAB[:, T:2 * T], ACT.Identity, bias=b3[:, x:x + 1],
                              scale=0.5).then_inc(actB.done("ab", 2 * n + 1), 1)
                    if g == 13 and (e := r["C1"]) is not None:
                        act.wait_ge(dveC1.sem, dveC1.count(e, "subo"))
                        act_f(es[:], ds[:], ACT.Exp).then_inc(actC1.done("exp"), 1)
                    if g == 14 and (e := r["C1"]) is not None:
                        act.wait_ge(peC1.sem, peC1.count(e, "wT"))
                        act.wait_ge(st_w, dma_count(e - 1))
                        nc.scalar.copy(wT[:].rearrange("p a b -> p (a b)"), b7[:]).then_inc(actC1.done("wT"), 1)

            passes(act, one)

        @block.vector
        def _(dve):
            v = nc.vector
            for i in range(2):
                v.memset(Vz[i][:], 0.0).then_inc(setup_dve, 1)
            for z in (kC[:, 0:PAD], vC[:, 0:PAD]):
                v.memset(z, 0.0).then_inc(setup_dve, 1)
            for gb in (gB, gD):
                v.memset(gb["c"][:, :, E + 1:], 0.0).then_inc(setup_dve, 1)
                v.memset(gb["c"][:, :, E:E + 1], 1.0).then_inc(setup_dve, 1)
            dve.wait_ge(ld_const, 16 * N_CONST)
            v.tensor_scalar(b1h[:], b1[:], 0.5, None, ALU.mult).then_inc(setup_dve, 1)
            v.tensor_reduce(posm[:], posd[:], op=ALU.max, axis=AX.X).then_inc(setup_dve, 1)
            v.tensor_reduce(oobm[:], oobd[:], op=ALU.max, axis=AX.X).then_inc(setup_dve, 1)
            dve.wait_ge(setup_dve, 11)
            v.tensor_tensor(posd[:], posd[:], posm[:].unsqueeze(2).to_broadcast([128, 2, DUP]),
                            ALU.subtract).then_inc(setup_dve, 1)
            v.tensor_tensor(oobd[:], oobd[:], oobm[:].unsqueeze(2).to_broadcast([128, H, len(OOB)]),
                            ALU.subtract).then_inc(setup_dve, 1)
            dve.wait_ge(setup_act, 7)
            v.tensor_reduce(poss[:], posd[:], op=ALU.add, axis=AX.X).then_inc(setup_dve, 1)
            v.tensor_reduce(oobs[:], oobd[:], op=ALU.add, axis=AX.X).then_inc(setup_dve, 1)
            dve.wait_ge(setup_act, 9)
            v.tensor_tensor(posE[:], posE[:], posm[:], ALU.add).then_inc(setup_dve, 1)
            v.tensor_tensor(oobE[:], oobE[:], oobm[:], ALU.add).then_inc(setup_dve, 1)
            dve.wait_ge(setup_dve, SETUP_DVE)

            def moments(s, e, nb):
                dve.wait_ge(s.sem, s.count(e, "res"))
                for tt in range(TT):
                    v.bn_stats(nb["st"][:, tt, :], nb["y"][:, tt, :]).then_inc(s.done("bn", tt), 1)
                for tt in range(TT):
                    dve.wait_ge(s.sem, s.count(e, "bn", tt))
                    v.memset(nb["tick"][:, tt:tt + 1], 0.0)
                    v.bn_aggr(n_mv[:, nb["row"], tt, :], nb["st"][:, tt, :]).then_inc(s.done("ag", tt), 1)

            def inverse_roots(e, rows, parts):
                nv, ni, nr, ns = n_v[:, rows, :], n_i[:, rows, :], n_r[:, rows, :], n_s[:, rows, :]
                if 0 in parts:
                    v.tensor_scalar(nv, n_mv[:, rows, :, 1], EPS, None, ALU.add).then_inc(dveN.done("ve"), 1)
                    dve.wait_ge(dveN.sem, dveN.count(e, "ve"))
                    v.tensor_scalar(ni, nv.bitcast(I32), 1, None, ALU.logical_shift_right).then_inc(dveN.done("sh"), 1)
                    dve.wait_ge(dveN.sem, dveN.count(e, "sh"))
                    v.tensor_scalar(nr.bitcast(I32), ni, -1.0, float(0x5F3759DF), ALU.mult,
                                    ALU.add).then_inc(dveN.done("mg"), 1)
                for n in range(3):
                    if n + 1 in parts:
                        dve.wait_ge(dveN.sem, dveN.count(e, "nt", 3 * n - 1) if n else dveN.count(e, "mg"))
                        v.tensor_tensor(ns, nr, nr, ALU.mult).then_inc(dveN.done("nt", 3 * n), 1)
                        dve.wait_ge(dveN.sem, dveN.count(e, "nt", 3 * n))
                        v.scalar_tensor_tensor(ns, ns, -0.5, nv, ALU.mult, ALU.mult).then_inc(dveN.done("nt", 3 * n + 1), 1)
                        dve.wait_ge(dveN.sem, dveN.count(e, "nt", 3 * n + 1))
                        v.scalar_tensor_tensor(nr, ns, 1.5, nr, ALU.add, ALU.mult).then_inc(dveN.done("nt", 3 * n + 2), 1)

            def normed(s, nb, out_x):
                for tt in range(TT):
                    v.tensor_scalar(out_x[:, tt, :], nb["y"][:, tt, :], n_mv[:, nb["row"], tt, 0:1],
                                    n_r[:, nb["row"], tt:tt + 1], ALU.subtract, ALU.mult).then_inc(s.done("nm", tt), 1)

            def gates_rank(both):
                for s, e, gb, bk, p in both:
                    dve.wait_ge(p.sem, p.count(e, "lg"))
                    dve.wait_ge(s.sem, s.count(e - 1, "c"))
                    v.tensor_copy(gb["L"][:].rearrange("p t x -> p (t x)"), bk[:, 0:TT * E]).then_inc(s.done("cp"), 1)
                for s, e, gb, bk, p in both:
                    dve.wait_ge(s.sem, s.count(e, "cp"))
                    v.tensor_reduce(gb["mx"][:], gb["L"][:], op=ALU.max, axis=AX.X).then_inc(s.done("gmx"), 1)
                for s, e, gb, bk, p in both:
                    dve.wait_ge(s.sem, s.count(e, "gmx"))
                    v.tensor_tensor(gb["dl"][:], gb["L"][:], gb["mx"][:].unsqueeze(2).to_broadcast([128, TT, E]),
                                    ALU.subtract).then_inc(s.done("sub"), 1)
                for s, e, gb, bk, p in both:
                    lj = gb["L"][:].unsqueeze(2).to_broadcast([128, TT, E, E])
                    li = gb["L"][:].unsqueeze(3).to_broadcast([128, TT, E, E])
                    o = [gb[x][:].rearrange("p (t i j) -> p t i j", t=TT, i=E) for x in ("gt", "eq")]
                    v.tensor_tensor(o[0], lj, li, ALU.is_gt).then_inc(s.done("gt"), 1)
                    v.tensor_tensor(o[1], lj, li, ALU.is_equal).then_inc(s.done("eq"), 1)
                for s, e, gb, bk, p in both:
                    dve.wait_ge(s.sem, s.count(e, "eq"))
                    v.tensor_tensor(gb["eq"][:], gb["eq"][:], tri[:], ALU.mult).then_inc(s.done("eqt"), 1)
                for s, e, gb, bk, p in both:
                    dve.wait_ge(s.sem, s.count(e, "eqt"))
                    v.tensor_tensor(gb["gt"][:], gb["gt"][:], gb["eq"][:], ALU.add).then_inc(s.done("add"), 1)
                for s, e, gb, bk, p in both:
                    dve.wait_ge(s.sem, s.count(e, "add"))
                    v.tensor_reduce(gb["rank"][:].rearrange("p t x -> p (t x)"),
                                    gb["gt"][:].rearrange("p (a j) -> p a j", j=E), op=ALU.add,
                                    axis=AX.X).then_inc(s.done("rank"), 1)

            def gates_weigh(both):
                for s, e, gb, acts, peS, over in both:
                    dve.wait_ge(acts.sem, acts.count(e, "ge"))
                    dve.wait_ge(s.sem, s.count(e, "rank"))
                    v.scalar_tensor_tensor(gb["sel"][:], gb["rank"][:], 1.5, gb["ge"][:], ALU.is_lt,
                                           ALU.mult).then_inc(s.done("sel"), 1)
                for s, e, gb, acts, peS, over in both:
                    dve.wait_ge(s.sem, s.count(e, "sel"))
                    v.tensor_reduce(gb["sum"][:], gb[over][:], op=ALU.add, axis=AX.X).then_inc(s.done("sum"), 1)
                for s, e, gb, acts, peS, over in both:
                    dve.wait_ge(s.sem, s.count(e, "sum"))
                    v.reciprocal(gb["rec"][:], gb["sum"][:]).then_inc(s.done("rec"), 1)
                for s, e, gb, acts, peS, over in both:
                    dve.wait_ge(s.sem, s.count(e, "rec"))
                    dve.wait_ge(peS.sem, peS.count(e - 1, "cT"))
                    v.tensor_tensor(gb["c"][:, :, 0:E], gb["sel"][:], gb["rec"][:].unsqueeze(2).to_broadcast([128, TT, E]),
                                    ALU.mult).then_inc(s.done("c"), 1)

            def one(t, par, key):
                r = stages(t)
                odd = 1 - par
                for g in range(SLOTS):
                    if g == 0 and (e := r["M"]) is not None:
                        dve.wait_ge(dveA1.sem, dveA1.count(e, "max", 15))
                        dve.wait_ge(peM.sem, peM.count(e - 1, "mT"))
                        v.tensor_scalar(mneg[:], mx[:], -1.0, None, ALU.mult).then_inc(dveM.done("neg"), 1)
                    if g in PV_SLOT and (e := r["C1" if g else "C2"]) is not None:
                        for n in PV_SLOT[g]:
                            if n == 0:
                                dve.wait_ge(ld_w, dma_count(e, N_W))
                                dve.wait_ge(actC1.sem, actC1.count(e, "v"))
                            p = PV_ORDER[n]
                            v.tensor_tensor(pv[:, 2 * p:2 * p + 2, :], wb[:, 2 * p:2 * p + 2, :], shifted(vC, p),
                                            ALU.mult).then_inc(dveC2.done("pv", n), 1)
                    if g == 0 and (e := r["A1"]) is not None:
                        dve.wait_ge(actA1.sem, actA1.count(e, "k"))
                        dve.wait_ge(st_parts, dma_count(e - 1, 2))
                        v.tensor_copy(parts[:, :, 0, :], qk[:]).then_inc(dveA1.done("hi"), 1)
                        dve.wait_ge(dveA1.sem, dveA1.count(e, "hi"))
                        v.tensor_tensor(rest[:], qk[:], parts[:, :, 0, :], ALU.subtract).then_inc(dveA1.done("rest"), 1)
                    if g == 0 and (e := r["A3"]) is not None:
                        dve.wait_ge(pePV.sem, pePV.count(e, "PV", 3))
                        dve.wait_ge(peA3.sem, peA3.count(e - 1, "out"))
                        v.reciprocal(rden[:], bPV[:, T:2 * T]).then_inc(dveA3.done("rec"), 1)
                    if g == 0 and (e := r["A1"]) is not None:
                        dve.wait_ge(dveA1.sem, dveA1.count(e, "rest"))
                        v.tensor_copy(parts[:, :, 1, :], rest[:]).then_inc(dveA1.done("mid"), 1)
                    if g == 0 and (e := r["A3"]) is not None:
                        dve.wait_ge(dveA3.sem, dveA3.count(e, "rec"))
                        v.tensor_tensor(attnT[:], bPV[:, 0:T], rden[:], ALU.mult).then_inc(dveA3.done("num"), 1)
                    if g == 0 and (e := r["A1"]) is not None:
                        dve.wait_ge(dveA1.sem, dveA1.count(e, "mid"))
                        v.tensor_tensor(parts[:, :, 2, :], rest[:], parts[:, :, 1, :],
                                        ALU.subtract).then_inc(dveA1.done("lo"), 1)
                        dve.wait_ge(peA1.sem, peA1.count(e, "v"))
                        dve.wait_ge(pePV.sem, pePV.count(e - 2, "PV", 3))
                        o = bass.AP(Vz[par], 0, [[TT * 4 * 160, 128], [160, TT * 4], [40, 4], [1, HD]])
                        v.tensor_tensor(o, b6[:, 0:T].rearrange("p (a r d) -> p a r d", r=4, d=HD),
                                        bv0[:].rearrange("p t c -> p (t c)").rearrange("p (a r d) -> p a r d", r=4, d=HD),
                                        ALU.add).then_inc(dveA1.done("v"), 1)
                    if g == 2 and (e := r["A3"]) is not None:
                        dve.wait_ge(peA3.sem, peA3.count(e, "out"))
                        dve.wait_ge(poolA3.sem, poolA3.count(e, "xbo"))
                        dve.wait_ge(dveA3.sem, dveA3.count(e - 1, "nm", 1))
                        v.tensor_tensor(nA["y"][:].rearrange("p t c -> p (t c)"), b6[:, 0:T],
                                        x0b[:].rearrange("p t c -> p (t c)"), ALU.add).then_inc(dveA3.done("res"), 1)
                    if g == 2 and (e := r["D2"]) is not None:
                        dve.wait_ge(peD.sem, peD.count(e, "y"))
                        dve.wait_ge(dveDn.sem, dveDn.count(e - 1, "nm", 1))
                        v.tensor_tensor(nD["y"][:].rearrange("p t c -> p (t c)"), b7[:, 0:T],
                                        x3[:].rearrange("p t c -> p (t c)"), ALU.add).then_inc(dveDn.done("res"), 1)
                    if g == 2:
                        for st, s, nb in (("A3", dveA3, nA), ("D2", dveDn, nD)):
                            if (e := r[st]) is not None:
                                moments(s, e, nb)
                    if g == 3 and (e := r["C2"]) is not None:
                        dve.wait_ge(poolC2.sem, poolC2.count(e, "add", 2))
                        v.tensor_tensor(pv[:, 0:2, :], pv[:, 0:2, :], pv[:, 2:4, :], ALU.add).then_inc(dveC2n.done("add", 0), 1)
                        dve.wait_ge(dveC2n.sem, dveC2n.count(e, "add", 0))
                        v.tensor_tensor(pv[:, 0, :], pv[:, 0, :], pv[:, 1, :], ALU.add).then_inc(dveC2n.done("add", 1), 1)
                        dve.wait_ge(dveC2n.sem, dveC2n.count(e, "add", 1))
                        dve.wait_ge(actC1.sem, actC1.count(e, "g"))
                        dve.wait_ge(peC2.sem, peC2.count(e - 1, "out"))
                        v.scalar_tensor_tensor(gat[:], tg[:], 1.0, pv[:, 0, :], ALU.add,
                                               ALU.mult).then_inc(dveC2n.done("gt"), 1)
                    if g == 3 and (e := r["B2"]) is not None:
                        dve.wait_ge(peB.sem, peB.count(e, "z"))
                        dve.wait_ge(dveBn.sem, dveBn.count(e - 1, "nm", 1))
                        v.tensor_tensor(nB["y"][:].rearrange("p t c -> p (t c)"), b6[:, 0:T],
                                        x1[:].rearrange("p t c -> p (t c)"), ALU.add).then_inc(dveBn.done("res"), 1)
                        moments(dveBn, e, nB)
                    if g == 4 and (e := r["C2"]) is not None:
                        dve.wait_ge(peC2.sem, peC2.count(e, "out"))
                        dve.wait_ge(poolC2.sem, poolC2.count(e, "xb"))
                        dve.wait_ge(dveC2n.sem, dveC2n.count(e - 1, "nm", 1))
                        v.tensor_tensor(nC["y"][:].rearrange("p t c -> p (t c)"), b7[:, 0:T],
                                        x2b[:].rearrange("p t c -> p (t c)"), ALU.add).then_inc(dveC2n.done("res"), 1)
                        moments(dveC2n, e, nC)
                    if g == 4 and (present := [n for n, st in enumerate(NORMS) if r[st] is not None]):
                        rows = slice(present[0], present[-1] + 1)
                        eN = t - LAG["A3"]
                        for n, s in enumerate((dveA3, dveBn, dveC2n, dveDn)):
                            if n in present:
                                dve.wait_ge(s.sem, s.count(r[NORMS[n]], "ag", 1))
                        inverse_roots(eN, rows, range(4))
                        dve.wait_ge(dveN.sem, dveN.count(eN, "nt", 8))
                        if (e := r["B2"]) is not None:
                            dve.wait_ge(poolC2.sem, poolC2.count(e - 1, "xb"))
                            dve.wait_ge(peC1.sem, peC1.count(e - 1, "xT"))
                            normed(dveBn, nB, x2)
                        if (e := r["A3"]) is not None:
                            dve.wait_ge(peB.sem, peB.count(e - 1, "xT"))
                            normed(dveA3, nA, x1)
                        if (e := r["C2"]) is not None:
                            dve.wait_ge(peD.sem, peD.count(e - 1, "xT"))
                            normed(dveC2n, nC, x3)
                        if (e := r["D2"]) is not None:
                            dve.wait_ge(st_out, dma_count(e - 1))
                            normed(dveDn, nD, xout)
                    if g == 7:
                        both = [(s, r[st], gb, bk, p) for st, s, gb, bk, p in
                                (("B", dveBg, gB, b6, peB), ("D", dveDg, gD, b6, peD)) if r[st] is not None]
                        gates_rank(both)
                    if g == 8:
                        both = [(s, r[st], gb, a, p, over) for st, s, gb, a, p, over in
                                (("B", dveBg, gB, actB, peB, "ge"), ("D", dveDg, gD, actD, peD, "sel"))
                                if r[st] is not None]
                        gates_weigh(both)
                    if g >= 5 and (e := r["A1"]) is not None:
                        for k in ((0, 1) if g == 5 else (g - 4,)):
                            dve.wait_ge(peA1.sem, peA1.count(e, "S", k))
                            if k == 0:
                                dve.wait_ge(dveM.sem, dveM.count(e - 1, "neg"))
                            v.tensor_reduce(mx[:, :, k], bS[k % 2][:].rearrange("p (a b) -> p a b", a=TT), op=ALU.max,
                                            axis=AX.X).then_inc(dveA1.done("max", k), 1)
                    if g in AB_SLOT and (e := r["B"]) is not None:
                        n = AB_SLOT[g]
                        x = expert(n)
                        dve.wait_ge(actB.sem, actB.count(e, "ab", 2 * n + 1))
                        if n >= 2:
                            dve.wait_ge(poolB.sem, poolB.count(e, "h", n - 2))
                        else:
                            dve.wait_ge(poolB.sem, poolB.count(e - 1, "h", n + 7))
                        bAB = bTU[turn_bank("ab", n)]
                        if n == 1:
                            dve.wait_ge(ld_cB, dma_count(e))
                        if n == 0:
                            i = v.tensor_scalar(wa[0][:], bAB[:, 0:T], b1[:, x:x + 1], None, ALU.add)
                        else:
                            i = v.scalar_tensor_tensor(wa[n % 2][:].rearrange("p (t n) -> p t n", t=TT),
                                                       bAB[:, 0:T].rearrange("p (t n) -> p t n", t=TT), b1[:, x:x + 1],
                                                       gB["cb"][:, :, x, :], ALU.add, ALU.mult)
                        i.then_inc(dveB.done("wu", 2 * n), 1)
                        v.scalar_tensor_tensor(ub[n % 2][:], th[n % 2][:], 1.0, bb[n % 2][:], ALU.add,
                                               ALU.mult).then_inc(dveB.done("wu", 2 * n + 1), 1)
                    if g == 11 and (e := r["C1"]) is not None:
                        dve.wait_ge(peC1.sem, peC1.count(e, "sc"))
                        dve.wait_ge(peC1.sem, peC1.count(e - 1, "scT"))
                        for s in range(2):
                            v.tensor_scalar(scs[:, s, :], b7[:, s * T:s * T + T], posE[:, s:s + 1], None,
                                            ALU.add).then_inc(dveC1.done("sc", s), 1)
                    if g == 12 and (e := r["C1"]) is not None:
                        dve.wait_ge(peC1.sem, peC1.count(e, "scT"))
                        sc_ = b7[:].rearrange("p (t a h) -> p t a h", t=TT, h=H)
                        v.tensor_reduce(mC[:], sc_.rearrange("p t a h -> p t h a"), op=ALU.max,
                                        axis=AX.X).then_inc(dveC1.done("mx"), 1)
                        dve.wait_ge(dveC1.sem, dveC1.count(e, "mx"))
                        ob = oobE[:].unsqueeze(1).to_broadcast([128, TT, H])
                        v.tensor_tensor(mC2[:], mC[:], ob, ALU.max).then_inc(dveC1.done("m2"), 1)
                        dve.wait_ge(dveC1.sem, dveC1.count(e, "m2"))
                        dve.wait_ge(actC1.sem, actC1.count(e - 1, "exp"))
                        v.tensor_tensor(ds[:, :, 0:NS, :], sc_, mC2[:].unsqueeze(2).to_broadcast([128, TT, NS, H]),
                                        ALU.subtract).then_inc(dveC1.done("sub"), 1)
                        v.tensor_tensor(ds[:, :, NS, :], ob, mC2[:], ALU.subtract).then_inc(dveC1.done("subo"), 1)
                    if g == 13 and (e := r["C1"]) is not None:
                        dve.wait_ge(actC1.sem, actC1.count(e, "exp"))
                        v.tensor_reduce(sC[:], es[:].rearrange("p t a h -> p t h a"), op=ALU.add,
                                        axis=AX.X).then_inc(dveC1.done("sum"), 1)
                        dve.wait_ge(dveC1.sem, dveC1.count(e, "sum"))
                        v.reciprocal(rC[:], sC[:]).then_inc(dveC1.done("rec"), 1)
                        dve.wait_ge(dveC1.sem, dveC1.count(e, "rec"))
                        dve.wait_ge(peC1.sem, peC1.count(e - 1, "wT"))
                        v.tensor_tensor(wn[:], es[:, :, 0:NS, :], rC[:].unsqueeze(2).to_broadcast([128, TT, NS, H]),
                                        ALU.mult).then_inc(dveC1.done("w"), 1)

            passes(dve, one)

        @block.gpsimd
        def _(pool):
            tt_ = nc.gpsimd.tensor_tensor
            pool.wait_ge(ld_const, 16 * N_CONST)
            pool.wait_ge(setup_dve, SETUP_DVE)

            def one(t, par, key):
                r = stages(t)
                odd = 1 - par
                for g in range(SLOTS):
                    if g == 0:
                        if (e := r["A3"]) is not None:
                            pool.wait_ge(ld_x, dma_count(e))
                            pool.wait_ge(dveA3.sem, dveA3.count(e - 1, "res"))
                            tt_(x0b[:], x0[:], bo0[:], ALU.add).then_inc(poolA3.done("xbo"), 1)
                    if g == 0 and (e := r["C2"]) is not None:
                        for n, (a, b, w) in enumerate(((0, 8, 4), (4, 12, 4), (0, 4, 4))):
                            if n < 2:
                                pool.wait_ge(dveC2.sem, dveC2.count(e, "pv", 4 * n + 3))
                            else:
                                pool.wait_ge(poolC2.sem, poolC2.count(e, "add", 1))
                            tt_(pv[:, a:a + w, :], pv[:, a:a + w, :], pv[:, b:b + w, :],
                                ALU.add).then_inc(poolC2.done("add", n), 1)
                    if 7 <= g < 11 and (e := r["C1"]) is not None:
                        if g == 7:
                            pool.wait_ge(actC1.sem, actC1.count(e, "k"))
                            pool.wait_ge(peC1.sem, peC1.count(e - 1, "sc"))
                            pool.wait_ge(peD.sem, peD.count(e + LAG["C1"] - LAG["D2"], "y"))
                        for p in (2 * (g - 7), 2 * (g - 7) + 1):
                            tt_(prod[:, 2 * p:2 * p + 2, :], shifted(kC, p), qC[:].unsqueeze(1).to_broadcast([128, 2, T]),
                                ALU.mult).then_inc(poolC1.done("prod", p), 1)
                    if g == 12 and (e := r["C1"]) is not None:
                        pool.wait_ge(dveC2n.sem, dveC2n.count(e - 1, "res"))
                        pool.wait_ge(dveBn.sem, dveBn.count(e, "nm", 1))
                        tt_(x2b[:], x2[:], boc[:], ALU.add).then_inc(poolC2.done("xb"), 1)
                    if g in AB_SLOT and (e := r["B"]) is not None:
                        n = AB_SLOT[g]
                        pool.wait_ge(dveB.sem, dveB.count(e, "wu", 2 * n + 1))
                        if n == 0:
                            pool.wait_ge(peB.sem, peB.count(e - 1, "z"))
                        tt_(h9[:, n, :], wa[n % 2][:], ub[n % 2][:], ALU.mult).then_inc(poolB.done("h", n), 1)
                    if g in (13, 15, 17, 19) and (e := r["D"]) is not None:
                        i = (g - 13) // 2
                        if i == 0:
                            pool.wait_ge(ld_cD, dma_count(e))
                            pool.wait_ge(actD.sem, actD.count(e, "xT"))
                            pool.wait_ge(peD.sem, peD.count(e - 1, "y"))
                            if (c1 := r["C1"]) is not None:
                                pool.wait_ge(peC1.sem, peC1.count(c1, "sc"))
                        tt_(xs[:, 2 * i:2 * i + 2, :].rearrange("p x (t n) -> p x t n", t=TT),
                            gD["cb"][:, :, 2 * i:2 * i + 2, :].rearrange("p t x n -> p x t n"),
                            x3T[:].rearrange("p (t n) -> p t n", t=TT).unsqueeze(1).to_broadcast([128, 2, TT, 128]),
                            ALU.mult).then_inc(poolD.done("xs", i), 1)

            passes(pool, one)


def distance_tables():
    slopes = np.power(np.float32(2.0), np.float32(8.0) * np.arange(0, -H, -1, dtype=np.float32) / np.float32(H))
    i = np.arange(128)
    d = -slopes[:, None, None].astype(np.float64) * np.abs(i[:, None] - i[None, :])
    hi = d.astype(np.float16)
    lo = (d - hi.astype(np.float64)).astype(np.float16)
    dist = np.stack([hi, lo], 1).transpose(2, 0, 1, 3)

    def bf16(a):
        u = np.asarray(a, np.float32).view(np.uint32)
        u = ((u + 0x7FFF + ((u >> 16) & 1)) >> 16).astype(np.uint32)
        return u.astype(np.uint16), (u << 16).view(np.float32)

    def three(a):
        out, left = [], np.asarray(a, np.float64)
        for _ in range(3):
            bits, val = bf16(left.astype(np.float32))
            out.append(bits)
            left = left - val
        return out

    one = bf16(np.ones(1))[0][0]
    t = np.arange(T)
    first, second = t < 128, t >= 128
    rows = np.zeros((ROW_M + 1 - ROW_D, 2, H, T), np.uint16)
    far = slopes[:, None].astype(np.float64) * np.abs(t - 128)
    for n, part in enumerate(three(-far)):
        rows[n, 0] = np.where(first, one, 0)
        rows[n, 1] = np.where(second, part, 0)
        rows[3 + n, 0] = np.where(first, part, 0)
        rows[3 + n, 1] = np.where(second, one, 0)
        rows[6 + n, 0] = np.where(second, one, 0)
        rows[6 + n, 1] = np.where(first, part, 0)
        rows[9 + n, 0] = np.where(second, part, 0)
        rows[9 + n, 1] = np.where(first, one, 0)
    rows[ROW_M - ROW_D, 1] = one
    identb = np.zeros((128, 128), np.uint16)
    identb[i, i] = one
    return np.ascontiguousarray(dist), rows, identb


def kernel(**inputs):
    from concourse import bacc
    from concourse.bass_utils import run_bass_kernel_spmd

    a = {k: np.asarray(v) for k, v in inputs.items()}
    dh = np.arange(D).reshape(H, HD).T.reshape(-1)
    w, b = a["L0_attn_W_qkv"], a["L0_attn_b_qkv"]
    cw, cb = a["L1_attn_w_qkv"], a["L1_attn_b_qkv"]
    pos = a["L1_attn_pos_bias"]
    posd = np.full((128, 2, DUP), -1e30, pos.dtype)
    for p, pair in enumerate(PAIRS):
        for o2, shift in enumerate(pair):
            for n, i in enumerate(i for i, o in enumerate(OFFSETS) if o == shift):
                row = 32 * (p % 4) + 16 * o2
                posd[row:row + H, p // 4, n] = pos[i]
    dist, rows, identb = distance_tables()
    onesz = np.zeros((128, 4, 32), np.float32)
    hsum = np.zeros((128, 2, 32), np.float32)
    for r in range(4):
        onesz[:, r, HD * r:HD * r + HD] = 1
    for o2 in range(2):
        for p in range(128):
            hsum[p, o2, 16 * o2 + p % H] = 1
    b2 = np.zeros((128, TT, D), np.float32)
    for tt in range(TT):
        b2[64 * tt:64 * tt + E, tt] = a["L0_ffn_b2"]
        b2[64 * tt + E, tt] = a["L0_ffn_sb2"]
    ii = np.arange(E)
    arrays = {
        "x": a["L0_attn_x"],
        "xT": a["L0_attn_x"].reshape(B * T, D).T,
        "wqk0": np.stack([w[:D][dh].T, w[D:2 * D][dh].T], 1),
        "wv0": w[2 * D:].T,
        "wo0": a["L0_attn_W_out"].T,
        "bqk0": np.stack([b[:D][dh], b[D:2 * D][dh]], 1),
        "bv0": b[None, 2 * D:],
        "bo0": a["L0_attn_b_out"][None],
        "gw0": a["L0_ffn_gate_w"].T,
        "w13": np.stack([np.concatenate([a["L0_ffn_w1"], a["L0_ffn_sw1"][None]]),
                         np.concatenate([a["L0_ffn_w3"], a["L0_ffn_sw3"][None]])], 1).transpose(2, 0, 1, 3),
        "w2": np.concatenate([a["L0_ffn_w2"], a["L0_ffn_sw2"][None]]).transpose(1, 0, 2),
        "b1": np.concatenate([a["L0_ffn_b1"], a["L0_ffn_sb1"][None]]).T,
        "b3": np.concatenate([a["L0_ffn_b3"], a["L0_ffn_sb3"][None]]).T,
        "b2": b2,
        "wc": np.stack([cw[:, :D][:, dh], cw[:, D:2 * D][:, dh], cw[:, 2 * D:][:, dh],
                        a["L1_attn_w_gate"][:, dh]], 1),
        "bc": np.stack([cb[:D][dh], cb[D:2 * D][dh], cb[2 * D:][dh], a["L1_attn_b_gate"][dh]], 1),
        "woc": a["L1_attn_w_out"][dh],
        "boc": a["L1_attn_b_out"][None],
        "gw1": a["L1_ffn_gate_w"].T,
        "ew": a["L1_ffn_expert_w"].transpose(2, 0, 1),
        "posd": posd,
        "oobd": np.broadcast_to(pos[OOB].T, (128, H, len(OOB))),
        "ident": np.eye(128, dtype=np.float32),
        "identh": np.eye(128, dtype=np.float16),
        "identb": identb,
        "dist": dist,
        "rows": rows,
        "onesz": onesz,
        "hsum": hsum,
        "tri": np.broadcast_to((ii[None, :] < ii[:, None]).astype(np.float32).reshape(1, 1, -1),
                               (128, TT, E * E)).reshape(128, -1),
    }
    nc = bacc.Bacc("TRN2", target_bir_lowering=False, num_devices=1)
    feeds, aps = {}, {}
    for name, x in arrays.items():
        x = np.ascontiguousarray(x)
        feeds[f"in_{name}"] = x
        aps[name] = nc.dram_tensor(f"in_{name}", x.shape, mybir.dt.from_np(x.dtype), kind="ExternalInput").ap()
    out = nc.dram_tensor("out_x", (B, T, D), mybir.dt.float32, kind="ExternalOutput").ap()
    network(nc, aps, out)
    return run_bass_kernel_spmd(nc, [feeds], core_ids=[0]).results[0]["out_x"]
```

```python
import concourse.bass as bass
from concourse import mybir
from contextlib import ExitStack
import numpy as np

B, T, D = 32, 256, 128
H, HD = 16, 8
E = 8
TT = T // 128
EPS = 1e-5

N_SCALES, N_TAPS = 11, 4
OFFSETS = [(1 << j) * tau for j in range(N_SCALES) for tau in range(N_TAPS)]
SHIFTS = sorted({o for o in OFFSETS if o < T})
PAIRS = [(SHIFTS[2 * p + 1], SHIFTS[2 * p]) for p in range(len(SHIFTS) // 2)]
NP = len(PAIRS)
NS = len(SHIFTS)
PAD = max(SHIFTS)
DUP = max(sum(o == s for o in OFFSETS) for s in SHIFTS)
OOB = [i for i, o in enumerate(OFFSETS) if o >= T]

ROW_D, ROW_M = 9 * HD, 96

LAG = {"X": -1, "A1": 0, "M": 0, "A2": 1, "A3": 1, "A3n": 2, "B": 2, "B2": 3, "C1": 3, "C2": 4, "C2n": 5,
       "D": 5, "D2": 6}
NORMS = ("A3n", "B2", "C2n", "D2")
LAST = max(LAG.values())
LOOP_FROM = LAST + 1
LOOP_TO = LOOP_FROM + (B - 1 - LOOP_FROM) // 2 * 2
Z_FIRST = 6
PV_ORDER = (0, 1, 4, 5, 2, 3, 6, 7)

ORDER = {
    "pe": """
        A1.qk A1.v A2.ST.0 A2.ST.1 D2.y.0 A2.ST.2 B2.z D2.y.1 A2.ST.3 A2.ST.4 A2.ST.5 A2.ST.6 A2.ST.7 A2.ST.8
        A2.PV.0 A1.S.0 A1.S.1 B.xT A2.ST.9 C1.xT A2.ST.10 C1.qk A1.S.2 D.xT A1.S.3 B.lg C2.out A1.S.4 A2.PV.1
        C1.vg D.lg A2.ST.11 A2.ST.12 A1.S.5 A1.S.6 A2.PV.2 A1.S.7 A2.ST.13 A2.ST.14 A1.S.8 B.cT D.cT A2.ST.15
        C1.sc A2.PV.3 A1.S.9 A1.S.10 A3.pT A1.S.11 C1.scT A1.S.12 A3.aT B.ab.0 A1.S.13 B.ab.1 B.ab.2 A1.S.14
        B.ab.3 A3.out A1.S.15 C1.wT B.ab.4 B.ab.5 M.mT B.ab.6 B.ab.7 B.z B.ab.8""",
    "act": """
        A1.qk A2.exp.0 A2.exp.1 A2.exp.2 A2.exp.3 A2.exp.4 A2.exp.5 A2.exp.6 A2.exp.7 A2.exp.8 A3n.nm B2.nm
        B.xT C1.xT C2n.nm D2.nm C1.qk D.xT A2.exp.9 A2.exp.10 B.ge C1.vg A2.exp.11 A2.exp.12 D.ge A2.exp.13
        A2.exp.14 B.cT D.cT A2.exp.15 C1.sc A3.cp B.ab.0 C1.exp A3.aT B.ab.1 B.ab.2 C1.wT B.ab.3 B.ab.4 B.ab.5
        M.mT B.ab.6 B.ab.7 B.ab.8""",
    "dve": """
        A1.rest A1.v A1.mid C2.pv.0 C2.pv.1 A1.lo C2.pv.2 C2.pv.3 C2.pv.4 C2.pv.5 C2.pv.6 C2.pv.7 B2.res
        D2.res C2.add.0 N.root.0 N.root.1 N.root.2 N.root.3 C2.add.1 C2.add.2 C2.gt A1.max.0 A1.max.1 A1.max.2
        A1.max.3 C2.res A1.max.4 G.rank A1.max.5 A1.max.6 G.weigh A1.max.7 A1.max.8 A1.max.9 A1.max.10 A3.rec
        A3.num A1.max.11 A1.max.12 C1.mx B.wu.0 C1.sum B.wu.1 A1.max.13 A1.max.14 A3.res B.wu.2 A1.max.15
        M.neg B.wu.3 B.wu.4 B.wu.5 B.wu.6 B.wu.7 B.wu.8""",
    "pool": """
        A3.xbo C2.add.0 C2.add.1 C1.prod.0 C1.prod.1 C1.prod.2 C1.prod.3 C1.prod.4 C1.prod.5 C1.prod.6
        C1.prod.7 C2.xb D.xs.0 D.xs.1 B.h.0 B.h.1 B.h.2 D.xs.2 D.xs.3 B.h.3 B.h.4 B.h.5 B.h.6 B.h.7 B.h.8""",
    "sp": """
        X.xT A3.x A1.part.0 A1.part.1 A1.rows.0 A1.part.2 A1.rows.1 A1.rows.2 D2.out B.cT D.cT B.cb D.cb C1.w
        M.m""",
}
ORDER = {engine: [(".".join(step.split(".")[:2]), int((step.split(".") + [0])[2])) for step in order.split()]
         for engine, order in ORDER.items()}


class Steps:

    def __init__(self, sem, steps):
        self.sem, self.names = sem, []
        for s in steps.split():
            name, _, n = s.partition("*")
            self.names += [(name, i) for i in range(int(n or 1))]
        self.per_run = len(self.names)
        self.at = 0

    def done(self, name, i=0):
        assert self.names[self.at] == (name, i), (self.names[self.at], name, i)
        self.at = (self.at + 1) % self.per_run
        return self.sem

    def count(self, e, name, i=0):
        return 0 if isinstance(e, int) and e < 0 else e * self.per_run + (self.names.index((name, i)) + 1)


def dma_count(e, per_run=1):
    return 0 if isinstance(e, int) and e < 0 else (e + 1) * (16 * per_run)


def network(nc, A, out):
    F, BF, H16, I32, U16 = (mybir.dt.float32, mybir.dt.bfloat16, mybir.dt.float16, mybir.dt.int32,
                            mybir.dt.uint16)
    ALU, ACT, AX = mybir.AluOpType, mybir.ActivationFunctionType, mybir.AxisListType
    ctx = ExitStack()
    with ctx:
        def sb(name, shape, dt=F):
            return ctx.enter_context(nc.sbuf_tensor(name, shape, dt))

        def bank(name):
            return ctx.enter_context(nc.psum_tensor(name, [128, 512], F))

        def sem(name):
            return ctx.enter_context(nc.semaphore(name))

        def steps(name, s):
            return Steps(sem(name), s)

        wqk0, wv0, wo0 = sb("wqk0", [128, 2, 128]), sb("wv0", [128, 128]), sb("wo0", [128, 128])
        bqk0, bv0, bo0 = sb("bqk0", [128, 2]), sb("bv0", [128, TT, 128]), sb("bo0", [128, TT, 128])
        gw0, gw1 = sb("gw0", [128, E]), sb("gw1", [128, E])
        w13, w2 = sb("w13", [128, E + 1, 2, 128]), sb("w2", [128, E + 1, 128])
        b1, b1h, b3, b2 = sb("b1", [128, E + 1]), sb("b1h", [128, E + 1]), sb("b3", [128, E + 1]), sb("b2", [128, TT, 128])
        wc, bc = sb("wc", [128, 4, 128]), sb("bc", [128, 4])
        woc, boc = sb("woc", [128, 128]), sb("boc", [128, TT, 128])
        ew = sb("ew", [128, E, 128])
        ident, identb, identh = sb("ident", [128, 128]), sb("identb", [128, 128], BF), sb("identh", [128, 128], H16)
        dist = sb("dist", [128, H, 2, 128], H16)
        hsum = sb("hsum", [128, 2, 32])
        tri = sb("tri", [128, TT * E * E])
        posd, oobd = sb("posd", [128, 2, DUP]), sb("oobd", [128, H, len(OOB)])
        posm, poss, posE = sb("posm", [128, 2]), sb("poss", [128, 2]), sb("posE", [128, 2])
        oobm, oobs, oobE = sb("oobm", [128, H]), sb("oobs", [128, H]), sb("oobE", [128, H])

        xT = sb("xT", [128, T])
        x0, x2b = sb("x0", [128, TT, D]), sb("x2b", [128, TT, D])
        x0b = x0
        qk = sb("qk", [128, 2, T])
        rest = qk
        parts = sb("parts", [128, 2, 3, T], BF)
        stack = [sb(f"stack{i}", [ROW_M + 1, 2, H, T], BF) for i in range(2)]
        Vz = [sb(f"Vz{i}", [128, TT, H, 32]) for i in range(2)]
        mx, mneg, mT = sb("mx", [128, TT, H]), sb("mneg", [128, TT, H], BF), sb("mT", [H, T], BF)
        P = [sb(f"P{i}", [128, TT, T]) for i in range(8)]
        sums, attnT = sb("sums", [128, 2, T]), sb("attnT", [128, T])
        rden, attn = sb("rden", [128, 2 * TT, 4, 2]), sb("attn", [128, TT, D])
        x1, x2, x3 = (sb(f"x{n}", [128, TT, D]) for n in (1, 2, 3))
        xout = sb("xout", [128, TT, D])

        def norm_buffers(n):
            return dict(y=sb(n + "y", [128, TT, D]), st=sb(n + "st", [128, TT, 6]), tick=sb(n + "tick", [128, TT]),
                        row="ABCD".index(n[1]))

        def gate_buffers(n):
            return dict(L=sb(n + "L", [128, TT, E]), mx=sb(n + "mx", [128, TT]), dl=sb(n + "dl", [128, TT, E]),
                        gt=sb(n + "gt", [128, TT * E * E]), eq=sb(n + "eq", [128, TT * E * E]),
                        rank=sb(n + "rank", [128, TT, E]), ge=sb(n + "ge", [128, TT, E]),
                        sel=sb(n + "sel", [128, TT, E]), sum=sb(n + "sum", [128, TT]), rec=sb(n + "rec", [128, TT]),
                        c=sb(n + "c", [128, TT, 64]), cT=sb(n + "cT", [128, 128]),
                        cb=sb(n + "cb", [128, TT, E, 128]))

        nA, nB, nC, nD = (norm_buffers("n" + n) for n in "ABCD")
        n_mv, n_v, n_i = sb("n_mv", [128, 4, TT, 2]), sb("n_v", [128, 4, TT]), sb("n_i", [128, 4, TT], I32)
        n_r, n_s, n_b = sb("n_r", [128, 4, TT]), sb("n_s", [128, 4, TT]), sb("n_b", [128, 4, TT])
        gB, gD = gate_buffers("gB"), gate_buffers("gD")
        x1T = sb("x1T", [128, T])
        th, bb, wa, ub = ([sb(f"{n}{i}", [128, T]) for i in range(2)] for n in ("th", "bb", "wa", "ub"))
        h9 = sb("h9", [128, E + 1, T])
        x2T, qC, kC = sb("x2T", [128, T]), sb("qC", [128, T]), sb("kC", [128, PAD + T])
        vC, tg = sb("vC", [128, PAD + T]), sb("tg", [128, T])
        prod = sb("prod", [128, NS, T])
        ds = sb("ds", [128, TT, NS + 1, H])
        es = ds
        mC, mC2, sC, rC = (sb(n, [128, TT, H]) for n in ("mC", "mC2", "sC", "rC"))
        wn, wT = sb("wn", [128, TT, NS, H]), sb("wT", [128, 2, T])
        scs = wT
        wb = sb("wb", [128, NS, T])
        pv = wb
        gat = sb("gat", [128, T])
        x3T = sb("x3T", [128, T])
        xs = prod

        bS, bTU = [bank("bS0"), bank("bS1")], [bank("bTU0"), bank("bTU1"), bank("bTU2")]
        bPV, b6, b7 = bank("bPV"), bank("b6"), bank("b7")
        turn = [(what[-2:], n) for what, n in ORDER["pe"] if what in ("A2.ST", "B.ab")]

        def turn_bank(what, n):
            return turn.index((what, n)) % 3

        d_parts = nc.dram_tensor("d_parts", (2, 3, 128, T), BF, kind="Internal").ap()
        d_w = nc.dram_tensor("d_w", (2, 128, T), F, kind="Internal").ap()
        d_cB = nc.dram_tensor("d_cB", (TT, E, 128), F, kind="Internal").ap()
        d_cD = nc.dram_tensor("d_cD", (TT, E, 128), F, kind="Internal").ap()

        LN = "res bn*2 ag*2"
        GATE = "cp gmx sub gt eq eqt add rank sel sum rec c"
        peA1 = steps("peA1", "qk v S*16")
        peM = steps("peM", "mT")
        peA2, pePV = steps("peA2", "ST*16"), steps("pePV", "PV*4")
        peA3 = steps("peA3", "pT aT out")
        peB = steps("peB", "xT lg cT ab*9")
        peZ = steps("peZ", "z*2")
        peC1 = steps("peC1", "xT qk vg sc scT wT")
        peC2 = steps("peC2", "out")
        peD = steps("peD", "xT lg cT y*2")
        actA1 = steps("actA1", "q k hi*2")
        actM = steps("actM", "mT")
        actA2 = steps("actA2", "exp*16")
        actA3 = steps("actA3", "cp aT")
        actNA, actNB, actNC, actND = (steps("actN" + x, "nm*2") for x in "ABCD")
        actB = steps("actB", "xT ge cT ab*18")
        actC1 = steps("actC1", "xT q k v g sc*2 exp wT")
        actD = steps("actD", "xT ge cT")
        dveA1 = steps("dveA1", "rest v mid lo max*16")
        dveM = steps("dveM", "neg")
        dveA3 = steps("dveA3", "rec num*2 " + LN)
        dveBg = steps("dveBg", GATE)
        dveB = steps("dveB", "wu*18")
        dveBn = steps("dveBn", LN)
        dveC1 = steps("dveC1", "mx m2 sub subo sum rec w")
        dveC2 = steps("dveC2", "pv*8 add*3 gt")
        dveC2n = steps("dveC2n", LN)
        dveN = steps("dveN", "ve sh mg nt*9 nb")
        dveDg = steps("dveDg", GATE)
        dveDn = steps("dveDn", LN)
        poolA3 = steps("poolA3", "xbo")
        poolB = steps("poolB", "h*9")
        poolC1 = steps("poolC1", "prod*8")
        poolC2 = steps("poolC2", "xb add*2")
        poolD = steps("poolD", "xs*4")
        ld_const, ld_score, ld_expert = sem("ld_const"), sem("ld_score"), sem("ld_expert")
        ld_xT, ld_x = sem("ld_xT"), sem("ld_x")
        st_part, ld_stack, ld_m = [sem(f"st_part{n}") for n in range(3)], sem("ld_stack"), sem("ld_m")
        st_cB, ld_cB, st_cD, ld_cD = sem("st_cB"), sem("ld_cB"), sem("st_cD"), sem("ld_cD")
        st_w, ld_w, st_out = sem("st_w"), sem("ld_w"), sem("st_out")
        setup_dve, setup_act = sem("setup_dve"), sem("setup_act")
        SETUP_DVE, SETUP_ACT = 19, 9
        N_STACK, N_W = 12, HD

        consts = [(wqk0, "wqk0"), (bqk0, "bqk0"), (wv0, "wv0"), (wo0, "wo0"), (gw0, "gw0"), (gw1, "gw1"),
                  (b1, "b1"), (b3, "b3"), (b2, "b2"), (wc, "wc"), (bc, "bc"), (woc, "woc"), (ident, "ident"),
                  (hsum, "hsum"), (tri, "tri"), (posd, "posd"), (oobd, "oobd")]
        score_consts = [(identh, "identh"), (dist, "dist")]
        expert_consts = [(w13, "w13"), (w2, "w2"), (ew, "ew")]
        N_CONST, N_SCORE, N_EXPERT = len(consts) + 1 + 3 * TT, len(score_consts) + 4, len(expert_consts)

        x_rows = A["x"].rearrange("b (t p) c -> p (b t) c", p=128)
        out_rows = out.rearrange("b (t p) c -> p (b t) c", p=128)

        def head(k):
            return 4 * (k % 4) + k // 4

        def expert(n):
            return E if n == 0 else n - 1

        def shifted(x, p):
            hi, lo = PAIRS[p]
            return bass.AP(x, PAD - hi, [[PAD + T, 128], [hi - lo, 2], [1, T]])

        def stages(t):
            r = {}
            for s, lag in LAG.items():
                e = t - lag
                r[s] = None if isinstance(e, int) and not 0 <= e < B else e
            return r

        def passes(eng, one):
            for t in range(LOOP_FROM):
                one(t, t % 2, t)
            with eng.Fori(0, (LOOP_TO - LOOP_FROM) // 2) as r:
                for u in range(2):
                    one(r * 2 + (LOOP_FROM + u), (LOOP_FROM + u) % 2, LOOP_FROM + u)
            for t in range(LOOP_TO, B + LAST):
                one(t, t % 2, t)

        block = ctx.enter_context(nc.Block())

        @block.sync
        def _(sp):
            sp.dma_start(xT[:], A["xT"][:, 0:T]).then_inc(ld_xT, 16)
            for dst, name in consts:
                sp.dma_start(dst[:], A[name]).then_inc(ld_const, 16)
            sp.dma_start(identb[:].bitcast(U16), A["identb"]).then_inc(ld_const, 16)
            for tt in range(TT):
                for dst, name in ((bv0, "bv0"), (bo0, "bo0"), (boc, "boc")):
                    sp.dma_start(dst[:, tt, :], bass.AP(A[name].tensor, 0, [[0, 128], [1, 128]])).then_inc(ld_const, 16)
            for i in range(2):
                for s in range(2):
                    n = ROW_M + s - ROW_D
                    sp.dma_start(stack[i][ROW_D:ROW_D + n, s].bitcast(U16),
                                 A["rows"][0:n, s]).then_inc(ld_score, 16)
            for dst, name in score_consts:
                sp.dma_start(dst[:], A[name]).then_inc(ld_score, 16)

            def one(t, par, key):
                r = stages(t)
                for what, n in ORDER["sp"]:
                    if key == 1 and what == ORDER["sp"][0][0]:
                        for dst, name in expert_consts:
                            sp.dma_start(dst[:], A[name]).then_inc(ld_expert, 16)
                    if what == "X.xT" and (e := r["X"]) is not None:
                        sp.wait_ge(peA1.sem, peA1.count(e - 1, "v"))
                        sp.dma_start(xT[:], A["xT"][:, bass.ds(e * T, T)]).then_inc(ld_xT, 16)
                    if what == "A3.x":
                        if (e := r["A3"]) is not None:
                            sp.wait_ge(dveA3.sem, dveA3.count(e - 1, "res"))
                            sp.dma_start(x0[:], x_rows[:, bass.ds(e * TT, TT), :]).then_inc(ld_x, 16)
                    if what == "A1.part" and (e := r["A1"]) is not None:
                        if n == 0:
                            sp.wait_ge(ld_stack, dma_count(e - 1, N_STACK))
                            sp.wait_ge(actA1.sem, actA1.count(e, "hi", 1))
                        else:
                            sp.wait_ge(dveA1.sem, dveA1.count(e, ("mid", "lo")[n - 1]))
                        sp.dma_start(d_parts[:, n].rearrange("s p n -> p s n"), parts[:, :, n, :]).then_inc(st_part[n], 16)
                    if what == "A1.rows" and (e := r["A1"]) is not None:
                        sp.wait_ge(st_part[n], dma_count(e))
                        if n == 0:
                            sp.wait_ge(peA2.sem, peA2.count(e - 2, "ST", 15))
                        for qp in range(3):
                            sp.dma_start(stack[par][24 * n + 8 * qp:24 * n + 8 * qp + 8, 1].rearrange("p h n -> p (h n)"),
                                         bass.AP(d_parts.tensor, (3 + n) * 128 * T,
                                                 [[H * T, 8], [1, H * T]])).then_inc(ld_stack, 16)
                        if n == 2:
                            for kp in range(3):
                                sp.dma_start(stack[par][24 * kp:24 * kp + 24, 0].rearrange("p h n -> p (h n)"),
                                             bass.AP(d_parts.tensor, 0, [[H * T, 24], [1, H * T]])).then_inc(ld_stack, 16)
                    if what in ("B.cT", "D.cT", "B.cb", "D.cb"):
                        for st, dg, dr, st_s, ld_s, act, used in (("B", gB, d_cB, st_cB, ld_cB, actB, (dveB, "wu", 16)),
                                                                  ("D", gD, d_cD, st_cD, ld_cD, actD, (poolD, "xs", 3))):
                            if what == st + ".cT" and (e := r[st]) is not None:
                                sp.wait_ge(ld_s, dma_count(e - 1))
                                sp.wait_ge(act.sem, act.count(e, "cT"))
                                for tt in range(TT):
                                    sp.dma_start(dr[tt], dg["cT"][64 * tt:64 * tt + E, :]).then_inc(st_s, 16)
                        for st, dg, dr, st_s, ld_s, act, used in (("B", gB, d_cB, st_cB, ld_cB, actB, (dveB, "wu", 16)),
                                                                  ("D", gD, d_cD, st_cD, ld_cD, actD, (poolD, "xs", 3))):
                            if what == st + ".cb" and (e := r[st]) is not None:
                                sp.wait_ge(st_s, dma_count(e, TT))
                                sp.wait_ge(used[0].sem, used[0].count(e - 1, used[1], used[2]))
                                sp.dma_start(dg["cb"][:].rearrange("p a b n -> p (a b n)"),
                                             bass.AP(dr.tensor, 0, [[0, 128], [1, TT * E * 128]])).then_inc(ld_s, 16)
                    if what == "C1.w" and (e := r["C1"]) is not None:
                        sp.wait_ge(ld_w, dma_count(e - 1, N_W))
                        sp.wait_ge(actC1.sem, actC1.count(e, "wT"))
                        sp.dma_start(d_w.rearrange("s p n -> p s n"), wT[:]).then_inc(st_w, 16)
                        sp.wait_ge(st_w, dma_count(e))
                        sp.wait_ge(dveC2.sem, dveC2.count(e - 1, "gt"))
                        for d in range(HD):
                            sp.dma_start(wb[H * d:H * d + H].rearrange("p (s j) n -> p s j n", s=2),
                                         bass.AP(d_w.tensor, 0, [[T, H], [128 * T, 2], [H * T, NP], [1, T]])
                                         ).then_inc(ld_w, 16)
                    if what == "M.m" and (e := r["M"]) is not None:
                        sp.wait_ge(actM.sem, actM.count(e, "mT"))
                        sp.dma_start(stack[par][ROW_M:ROW_M + 1, 0], mT[:]).then_inc(ld_m, 16)
                    if what == "D2.out" and (e := r["D2"]) is not None:
                        sp.wait_ge(actND.sem, actND.count(e, "nm", 1))
                        sp.dma_start(out_rows[:, bass.ds(e * TT, TT), :], xout[:]).then_inc(st_out, 16)

            passes(sp, one)
            sp.wait_ge(st_out, dma_count(B - 1))

        @block.tensor
        def _(pe):
            mm = nc.tensor.matmul
            pe.wait_ge(ld_const, 16 * N_CONST)
            pe.wait_ge(setup_dve, SETUP_DVE)
            pe.wait_ge(setup_act, SETUP_ACT)
            last = {b: None for b in (0, 1, 2, 6, 7)}

            def take(bank_no, now, t):
                if last[bank_no]:
                    st, s, name, i, when = last[bank_no]
                    pe.wait_ge(s.sem, s.count(when - LAG[st], name, i))
                last[bank_no] = (*now, t)

            def one(t, par, key):
                if key == LOOP_FROM and not isinstance(t, int):
                    for b in last:
                        last[b] = (*last[b][:4], t - 1)
                if isinstance(t, int) and t == LOOP_TO:
                    for b in last:
                        last[b] = (*last[b][:4], LOOP_TO - 1)
                r = stages(t)
                odd = 1 - par
                for what, n in ORDER["pe"]:
                    if what == "A1.qk" and (e := r["A1"]) is not None:
                        take(6, ("A1", actA1, "hi", 1), t)
                        pe.wait_ge(ld_xT, dma_count(e))
                        mm(b6[:, 0:T], wqk0[:, 0, :], xT[:], start=True, stop=True)
                        mm(b6[:, T:2 * T], wqk0[:, 1, :], xT[:], start=True, stop=True).then_inc(peA1.done("qk"), 1)
                    if what == "A1.v" and (e := r["A1"]) is not None:
                        take(7, ("A1", dveA1, "v", 0), t)
                        for tt in range(TT):
                            i = mm(b7[:, tt * 128:tt * 128 + 128], xT[:, tt * 128:tt * 128 + 128], wv0[:],
                                   start=True, stop=True)
                        i.then_inc(peA1.done("v"), 1)
                    if what in ("B.xT", "C1.xT", "D.xT"):
                        for st, bk, bn, s, act, src, prev in (("B", b6, 6, peB, actB, x1, actNA),
                                                              ("C1", b7, 7, peC1, actC1, x2, actNB),
                                                              ("D", b6, 6, peD, actD, x3, actNC)):
                            if what == st + ".xT" and (e := r[st]) is not None:
                                take(bn, (st, act, "xT", 0), t)
                                pe.wait_ge(prev.sem, prev.count(e, "nm", 1))
                                for tt in range(TT):
                                    i = nc.tensor.transpose(bk[:, tt * 128:tt * 128 + 128], src[:, tt, :], ident[:])
                                i.then_inc(s.done("xT"), 1)
                    if what == "C1.qk" and (e := r["C1"]) is not None:
                        take(7, ("C1", actC1, "k", 0), t)
                        pe.wait_ge(actC1.sem, actC1.count(e, "xT"))
                        mm(b7[:, 0:T], wc[:, 0, :], x2T[:], start=True, stop=True)
                        mm(b7[:, T:2 * T], wc[:, 1, :], x2T[:], start=True, stop=True).then_inc(peC1.done("qk"), 1)
                    if what in ("B.lg", "D.lg"):
                        for st, bk, bn, s, act, xt, gw, dg in (("B", b6, 6, peB, actB, x1T, gw0, dveBg),
                                                               ("D", b6, 6, peD, actD, x3T, gw1, dveDg)):
                            if what == st + ".lg" and (e := r[st]) is not None:
                                take(bn, (st, dg, "cp", 0), t)
                                pe.wait_ge(act.sem, act.count(e, "xT"))
                                for tt in range(TT):
                                    i = mm(bk[:, tt * E:tt * E + E], xt[:, tt * 128:tt * 128 + 128], gw[:],
                                           start=True, stop=True)
                                i.then_inc(s.done("lg"), 1)
                    if what == "C2.out" and (e := r["C2"]) is not None:
                        take(7, ("C2", dveC2n, "res", 0), t)
                        pe.wait_ge(dveC2.sem, dveC2.count(e, "gt"))
                        for tt in range(TT):
                            i = mm(b7[:, tt * 128:tt * 128 + 128], gat[:, tt * 128:tt * 128 + 128], woc[:],
                                   start=True, stop=True)
                        i.then_inc(peC2.done("out"), 1)
                    if what == "C1.vg" and (e := r["C1"]) is not None:
                        take(7, ("C1", actC1, "g", 0), t)
                        mm(b7[:, 0:T], wc[:, 2, :], x2T[:], start=True, stop=True)
                        mm(b7[:, T:2 * T], wc[:, 3, :], x2T[:], start=True, stop=True).then_inc(peC1.done("vg"), 1)
                    if what in ("B.cT", "D.cT"):
                        for st, bk, bn, s, act, dg, gb in (("B", b6, 6, peB, actB, dveBg, gB),
                                                           ("D", b7, 7, peD, actD, dveDg, gD)):
                            if what == st + ".cT" and (e := r[st]) is not None:
                                take(bn, (st, act, "cT", 0), t)
                                pe.wait_ge(dg.sem, dg.count(e, "c"))
                                nc.tensor.transpose(bk[:, 0:128], gb["c"][:].rearrange("p a b -> p (a b)"),
                                                    ident[:]).then_inc(s.done("cT"), 1)
                    if what == "A2.ST" and (e := r["A2"]) is not None:
                        k = n
                        h = head(k)
                        if k == 0:
                            pe.wait_ge(ld_m, dma_count(e))
                        take(turn_bank("ST", k), ("A2", actA2, "exp", k), t)
                        o = bTU[turn_bank("ST", k)]
                        for kt in range(TT):
                            q = slice(kt * T, kt * T + T)
                            c = slice(kt * T + kt * 128, kt * T + kt * 128 + 128)
                            mm(o[:, q], stack[odd][0:ROW_M + 1, 1, h, kt * 128:kt * 128 + 128],
                               stack[odd][0:ROW_M + 1, 0, h, :], start=True, stop=False)
                            last_part = h % 2 == 0
                            i = mm(o[:, c], identh[:], dist[:, h, 0, :], start=False, stop=last_part)
                            if not last_part:
                                i = mm(o[:, c], identh[:], dist[:, h, 1, :], start=False, stop=True)
                        i.then_inc(peA2.done("ST", k), 1)
                    if what == "A2.PV" and (e := r["A2"]) is not None:
                        rr = n
                        pe.wait_ge(actA2.sem, actA2.count(e, "exp", 4 * rr + 3))
                        if rr == 0:
                            pe.wait_ge(actA3.sem, actA3.count(e - 1, "cp"))
                            if (b2_ := r["B2"]) is not None:
                                pe.wait_ge(dveBn.sem, dveBn.count(b2_, "res"))
                            pe.wait_ge(dveA1.sem, dveA1.count(e, "v"))
                        half = rr // 2
                        for kt in range(TT):
                            for j in range(4):
                                i = mm(bPV[32 * j:32 * j + 32, half * T:half * T + T], Vz[odd][:, kt, 4 * j + rr, :],
                                       P[(4 * rr + j) % 8][:, kt, :], start=(rr == 0 and kt == 0),
                                       stop=(rr % 2 == 1 and kt == 1), skip_group_check=True)
                        i.then_inc(pePV.done("PV", rr), 1)
                    if what == "D2.y" and (e := r["D2"]) is not None:
                        tt = n
                        if tt == 0:
                            take(6, ("D2", dveDn, "res", 0), t)
                        for x in range(E):
                            if tt == 0 and x % 2 == 0:
                                pe.wait_ge(poolD.sem, poolD.count(e, "xs", x // 2))
                            i = mm(b6[:, tt * 128:tt * 128 + 128], xs[:, x, tt * 128:tt * 128 + 128], ew[:, x, :],
                                   start=(x == 0), stop=(x == E - 1))
                        i.then_inc(peD.done("y", tt), 1)
                    if what in ("B.z", "B2.z") and (e := r[what[:-2]]) is not None:
                        if what == "B.z":
                            if (a3 := r["A3"]) is not None:
                                pe.wait_ge(actA3.sem, actA3.count(a3, "cp"))
                            pe.wait_ge(dveBn.sem, dveBn.count(e - 1, "res"))
                            pe.wait_ge(actB.sem, actB.count(e, "cT"))
                            for tt in range(TT):
                                mm(bPV[:, tt * 128:tt * 128 + 128], gB["cT"][:], b2[:, tt, :], start=(tt == 0), stop=False,
                                   skip_group_check=True)
                        for x in range(E + 1):
                            if (x < Z_FIRST) == (what == "B.z"):
                                pe.wait_ge(poolB.sem, poolB.count(e, "h", x))
                                for tt in range(TT):
                                    i = mm(bPV[:, tt * 128:tt * 128 + 128], h9[:, x, tt * 128:tt * 128 + 128],
                                           w2[:, expert(x), :], start=False, stop=(x == E), skip_group_check=True)
                        i.then_inc(peZ.done("z", 0 if what == "B.z" else 1), 1)
                    if what == "A1.S" and (e := r["A1"]) is not None:
                        k = n
                        if key == 0 and k == 0:
                            pe.wait_ge(ld_score, 16 * N_SCORE)
                        if k == 0:
                            pe.wait_ge(ld_stack, dma_count(e, N_STACK))
                        if k >= 2:
                            pe.wait_ge(dveA1.sem, dveA1.count(e, "max", k - 2))
                        else:
                            pe.wait_ge(dveA1.sem, dveA1.count(e - 1, "max", k + 14))
                        o = bS[k % 2]
                        h = k
                        for qt in range(TT):
                            mm(o[:, qt * T:qt * T + T], stack[par][0:ROW_M, 0, h, qt * 128:qt * 128 + 128],
                               stack[par][0:ROW_M, 1, h, :], start=True, stop=False)
                            c = slice(qt * T + qt * 128, qt * T + qt * 128 + 128)
                            i = mm(o[:, c], identh[:], dist[:, h, 0, :], start=False, stop=True)
                        i.then_inc(peA1.done("S", k), 1)
                    if what == "B.ab" and (e := r["B"]) is not None:
                        if key == LAG["B"] and n == 0:
                            pe.wait_ge(ld_expert, 16 * N_EXPERT)
                        x = expert(n)
                        take(turn_bank("ab", n), ("B", dveB, "wu", 2 * n), t)
                        bAB = bTU[turn_bank("ab", n)]
                        mm(bAB[:, 0:T], w13[:, x, 0, :], x1T[:], start=True, stop=True)
                        mm(bAB[:, T:2 * T], w13[:, x, 1, :], x1T[:], start=True, stop=True).then_inc(peB.done("ab", n), 1)
                    if what == "C1.sc" and (e := r["C1"]) is not None:
                        take(7, ("C1", actC1, "sc", 1), t)
                        pe.wait_ge(poolC1.sem, poolC1.count(e, "prod", 7))
                        for s in range(2):
                            for o2 in range(2):
                                for j in range(4):
                                    i = mm(b7[32 * j:32 * j + 32, s * T:s * T + T], hsum[:, o2, :],
                                           prod[:, 2 * (4 * s + j) + o2, :], start=(s == 0 and o2 == 0), stop=o2 == 1,
                                           skip_group_check=True)
                        i.then_inc(peC1.done("sc"), 1)
                    if what == "C1.scT" and (e := r["C1"]) is not None:
                        take(7, ("C1", dveC1, "sub", 0), t)
                        for tt in range(TT):
                            for s in range(2):
                                i = nc.tensor.transpose(b7[:, tt * T + s * 128:tt * T + s * 128 + 128],
                                                        scs[:, s, tt * 128:tt * 128 + 128], ident[:])
                        i.then_inc(peC1.done("scT"), 1)
                    if what == "A3.pT" and (e := r["A3"]) is not None:
                        take(6, ("A3", dveA3, "num", 1), t)
                        pe.wait_ge(actA3.sem, actA3.count(e, "cp"))
                        for tt in range(TT):
                            for a in range(2):
                                c = 128 * (2 * tt + a)
                                i = nc.tensor.transpose(b6[:, c:c + 128], sums[:, a, tt * 128:tt * 128 + 128], ident[:])
                        i.then_inc(peA3.done("pT"), 1)
                    if what == "A3.aT" and (e := r["A3"]) is not None:
                        take(6, ("A3", actA3, "aT", 0), t)
                        pe.wait_ge(dveA3.sem, dveA3.count(e, "num", 1))
                        for tt in range(TT):
                            i = nc.tensor.transpose(b6[:, tt * 128:tt * 128 + 128], attn[:, tt, :], ident[:])
                        i.then_inc(peA3.done("aT"), 1)
                    if what == "A3.out":
                        if (e := r["A3"]) is not None:
                            take(6, ("A3", dveA3, "res", 0), t)
                            pe.wait_ge(actA3.sem, actA3.count(e, "aT"))
                            for tt in range(TT):
                                i = mm(b6[:, tt * 128:tt * 128 + 128], attnT[:, tt * 128:tt * 128 + 128], wo0[:],
                                       start=True, stop=True)
                            i.then_inc(peA3.done("out"), 1)
                    if what == "C1.wT" and (e := r["C1"]) is not None:
                        take(7, ("C1", actC1, "wT", 0), t)
                        pe.wait_ge(dveC1.sem, dveC1.count(e, "w"))
                        wv = wn[:].rearrange("p t a h -> p t (a h)")
                        for s in range(2):
                            for tt in range(TT):
                                i = nc.tensor.transpose(b7[:, s * T + tt * 128:s * T + tt * 128 + 128],
                                                        wv[:, tt, s * 128:s * 128 + 128], ident[:])
                        i.then_inc(peC1.done("wT"), 1)
                    if what == "M.mT" and (e := r["M"]) is not None:
                        take(7, ("M", actM, "mT", 0), t)
                        pe.wait_ge(dveM.sem, dveM.count(e, "neg"))
                        o = b7[:].bitcast(BF)
                        for tt in range(TT):
                            i = nc.tensor.transpose(o[0:H, tt * 128:tt * 128 + 128], mneg[:, tt, :], identb[:])
                        i.then_inc(peM.done("mT"), 1)

            passes(pe, one)

        @block.scalar
        def _(act):
            act.wait_ge(ld_const, 16 * N_CONST)
            q_scale = HD ** -0.5
            nc.scalar.mul(bqk0[:, 0:1], bqk0[:, 0:1], q_scale).then_inc(setup_act, 1)
            nc.scalar.mul(b3[:], b3[:], 0.5).then_inc(setup_act, 1)
            nc.scalar.mul(bc[:, 0:1], bc[:, 0:1], q_scale).then_inc(setup_act, 1)
            nc.scalar.mul(bc[:, 3:4], bc[:, 3:4], 0.5).then_inc(setup_act, 1)
            nc.scalar.mul(woc[:], woc[:], 0.5).then_inc(setup_act, 1)
            act.wait_ge(setup_dve, 15)
            nc.scalar.activation(posd[:], posd[:], ACT.Exp).then_inc(setup_act, 1)
            nc.scalar.activation(oobd[:], oobd[:], ACT.Exp).then_inc(setup_act, 1)
            act.wait_ge(setup_dve, 17)
            nc.scalar.activation(posE[:], poss[:], ACT.Ln).then_inc(setup_act, 1)
            nc.scalar.activation(oobE[:], oobs[:], ACT.Ln).then_inc(setup_act, 1)
            act.wait_ge(setup_act, SETUP_ACT)
            act.wait_ge(setup_dve, SETUP_DVE)

            def one(t, par, key):
                r = stages(t)
                odd = 1 - par
                act_f = nc.scalar.activation
                for what, n in ORDER["act"]:
                    if what == "A1.qk" and (e := r["A1"]) is not None:
                        act.wait_ge(peA1.sem, peA1.count(e, "qk"))
                        act.wait_ge(dveA1.sem, dveA1.count(e - 1, "lo"))
                        act_f(qk[:, 0, :], b6[:, 0:T], ACT.Identity, bias=bqk0[:, 0:1],
                              scale=q_scale).then_inc(actA1.done("q"), 1)
                        act_f(qk[:, 1, :], b6[:, T:2 * T], ACT.Identity, bias=bqk0[:, 1:2]).then_inc(actA1.done("k"), 1)
                        act.wait_ge(st_part[0], dma_count(e - 1))
                        act_f(parts[:, 0, 0, :], b6[:, 0:T], ACT.Identity, bias=bqk0[:, 0:1],
                              scale=q_scale).then_inc(actA1.done("hi", 0), 1)
                        act_f(parts[:, 1, 0, :], b6[:, T:2 * T], ACT.Identity,
                              bias=bqk0[:, 1:2]).then_inc(actA1.done("hi", 1), 1)
                    if what == "B.xT" and (e := r["B"]) is not None:
                        act.wait_ge(peB.sem, peB.count(e, "xT"))
                        act.wait_ge(peB.sem, peB.count(e - 1, "ab", 8))
                        nc.scalar.copy(x1T[:], b6[:, 0:T]).then_inc(actB.done("xT"), 1)
                    if what == "C1.xT" and (e := r["C1"]) is not None:
                        act.wait_ge(peC1.sem, peC1.count(e, "xT"))
                        nc.scalar.copy(x2T[:], b7[:, 0:T]).then_inc(actC1.done("xT"), 1)
                    if what == "C1.qk" and (e := r["C1"]) is not None:
                        act.wait_ge(peC1.sem, peC1.count(e, "qk"))
                        act.wait_ge(poolC1.sem, poolC1.count(e - 1, "prod", 7))
                        act_f(qC[:], b7[:, 0:T], ACT.Identity, bias=bc[:, 0:1], scale=q_scale).then_inc(actC1.done("q"), 1)
                        act_f(kC[:, PAD:], b7[:, T:2 * T], ACT.Identity, bias=bc[:, 1:2]).then_inc(actC1.done("k"), 1)
                    if what == "D.xT" and (e := r["D"]) is not None:
                        act.wait_ge(peD.sem, peD.count(e, "xT"))
                        act.wait_ge(poolD.sem, poolD.count(e - 1, "xs", 3))
                        nc.scalar.copy(x3T[:], b6[:, 0:T]).then_inc(actD.done("xT"), 1)
                    if what == "C1.vg" and (e := r["C1"]) is not None:
                        act.wait_ge(peC1.sem, peC1.count(e, "vg"))
                        act.wait_ge(dveC2.sem, dveC2.count(e - 1, "pv", 7))
                        act.wait_ge(dveC2.sem, dveC2.count(e - 1, "gt"))
                        act_f(vC[:, PAD:], b7[:, 0:T], ACT.Identity, bias=bc[:, 2:3]).then_inc(actC1.done("v"), 1)
                        act_f(tg[:], b7[:, T:2 * T], ACT.Tanh, bias=bc[:, 3:4], scale=0.5).then_inc(actC1.done("g"), 1)
                    if what in ("B.ge", "D.ge"):
                        for st, s, dg, gb in (("B", actB, dveBg, gB), ("D", actD, dveDg, gD)):
                            if what == st + ".ge" and (e := r[st]) is not None:
                                act.wait_ge(dg.sem, dg.count(e, "sub"))
                                act.wait_ge(dg.sem, dg.count(e - 1, "sum"))
                                act_f(gb["ge"][:], gb["dl"][:], ACT.Exp).then_inc(s.done("ge"), 1)
                    if what in ("B.cT", "D.cT"):
                        for st, s, p, gb, bk, used in (("B", actB, peB, gB, b6, (peZ, "z")), ("D", actD, peD, gD, b7, None)):
                            if what == st + ".cT" and (e := r[st]) is not None:
                                act.wait_ge(p.sem, p.count(e, "cT"))
                                act.wait_ge(st_cB if st == "B" else st_cD, dma_count(e - 1, TT))
                                if used:
                                    act.wait_ge(used[0].sem, used[0].count(e - 1, used[1], 1))
                                nc.scalar.copy(gb["cT"][:], bk[:, 0:128]).then_inc(s.done("cT"), 1)
                    if what == "A2.exp" and (e := r["A2"]) is not None:
                        k = n
                        act.wait_ge(peA2.sem, peA2.count(e, "ST", k))
                        if k >= 8:
                            act.wait_ge(pePV.sem, pePV.count(e, "PV", (k - 8) // 4))
                        else:
                            act.wait_ge(pePV.sem, pePV.count(e - 1, "PV", (k + 8) // 4))
                        act_f(P[k % 8][:].rearrange("p a b -> p (a b)"), bTU[turn_bank("ST", k)][:], ACT.Exp).then_inc(actA2.done("exp", k), 1)
                    if what == "B.ab" and (e := r["B"]) is not None:
                        x = expert(n)
                        act.wait_ge(peB.sem, peB.count(e, "ab", n))
                        if n >= 2:
                            act.wait_ge(dveB.sem, dveB.count(e, "wu", 2 * n - 3))
                        else:
                            act.wait_ge(dveB.sem, dveB.count(e - 1, "wu", 17))
                        bAB = bTU[turn_bank("ab", n)]
                        act_f(th[n % 2][:], bAB[:, 0:T], ACT.Tanh, bias=b1h[:, x:x + 1], scale=0.5).then_inc(actB.done("ab", 2 * n), 1)
                        act_f(bb[n % 2][:], bAB[:, T:2 * T], ACT.Identity, bias=b3[:, x:x + 1],
                              scale=0.5).then_inc(actB.done("ab", 2 * n + 1), 1)
                    if what == "A3.cp" and (e := r["A3"]) is not None:
                        act.wait_ge(pePV.sem, pePV.count(e, "PV", 3))
                        act.wait_ge(peA3.sem, peA3.count(e - 1, "pT"))
                        nc.scalar.copy(sums[:].rearrange("p a b -> p (a b)"), bPV[:]).then_inc(actA3.done("cp"), 1)
                    if what == "A3.aT" and (e := r["A3"]) is not None:
                        act.wait_ge(peA3.sem, peA3.count(e, "aT"))
                        act.wait_ge(peA3.sem, peA3.count(e - 1, "out"))
                        nc.scalar.copy(attnT[:], b6[:, 0:T]).then_inc(actA3.done("aT"), 1)
                    if what == "C1.sc" and (e := r["C1"]) is not None:
                        act.wait_ge(peC1.sem, peC1.count(e, "sc"))
                        act.wait_ge(peC1.sem, peC1.count(e - 1, "scT"))
                        for s in range(2):
                            act_f(scs[:, s, :], b7[:, s * T:s * T + T], ACT.Identity,
                                  bias=posE[:, s:s + 1]).then_inc(actC1.done("sc", s), 1)
                    for row, (st, y, x, s) in enumerate((("A3n", nA, x1, actNA), ("B2", nB, x2, actNB),
                                                         ("C2n", nC, x3, actNC), ("D2", nD, xout, actND))):
                        if what == st + ".nm" and (e := r[st]) is not None:
                            act.wait_ge(dveN.sem, dveN.count(t - LAG["A3n"], "nb"))
                            if st == "A3n":
                                act.wait_ge(peB.sem, peB.count(e - 1, "xT"))
                            if st == "B2":
                                act.wait_ge(poolC2.sem, poolC2.count(e - 1, "xb"))
                                act.wait_ge(peC1.sem, peC1.count(e - 1, "xT"))
                            if st == "C2n":
                                act.wait_ge(peD.sem, peD.count(e - 1, "xT"))
                            if st == "D2":
                                act.wait_ge(st_out, dma_count(e - 1))
                            for tt in range(TT):
                                act_f(x[:, tt, :], y["y"][:, tt, :], ACT.Identity, bias=n_b[:, row, tt:tt + 1],
                                      scale=n_r[:, row, tt:tt + 1]).then_inc(s.done("nm", tt), 1)
                    if what == "C1.exp" and (e := r["C1"]) is not None:
                        act.wait_ge(dveC1.sem, dveC1.count(e, "subo"))
                        act_f(es[:], ds[:], ACT.Exp).then_inc(actC1.done("exp"), 1)
                    if what == "C1.wT" and (e := r["C1"]) is not None:
                        act.wait_ge(peC1.sem, peC1.count(e, "wT"))
                        act.wait_ge(st_w, dma_count(e - 1))
                        nc.scalar.copy(wT[:].rearrange("p a b -> p (a b)"), b7[:]).then_inc(actC1.done("wT"), 1)
                    if what == "M.mT" and (e := r["M"]) is not None:
                        act.wait_ge(peM.sem, peM.count(e, "mT"))
                        act.wait_ge(ld_m, dma_count(e - 1))
                        nc.scalar.copy(mT[:], b7[:].bitcast(BF)[0:H, 0:T]).then_inc(actM.done("mT"), 1)

            passes(act, one)

        @block.vector
        def _(dve):
            v = nc.vector
            for i in range(2):
                v.memset(Vz[i][:], 0.0).then_inc(setup_dve, 1)
            dve.wait_ge(setup_dve, 2)
            for i in range(2):
                v.memset(bass.AP(Vz[i], 16, [[TT * H * 32, 128], [64, TT * H // 2], [33, 2]]), 1.0).then_inc(setup_dve, 1)
            for z in (kC[:, 0:PAD], vC[:, 0:PAD]):
                v.memset(z, 0.0).then_inc(setup_dve, 1)
            for gb in (gB, gD):
                v.memset(gb["c"][:, :, E + 1:], 0.0).then_inc(setup_dve, 1)
                v.memset(gb["c"][:, :, E:E + 1], 1.0).then_inc(setup_dve, 1)
            dve.wait_ge(ld_const, 16 * N_CONST)
            v.tensor_scalar(b1h[:], b1[:], 0.5, None, ALU.mult).then_inc(setup_dve, 1)
            v.tensor_reduce(posm[:], posd[:], op=ALU.max, axis=AX.X).then_inc(setup_dve, 1)
            v.tensor_reduce(oobm[:], oobd[:], op=ALU.max, axis=AX.X).then_inc(setup_dve, 1)
            dve.wait_ge(setup_dve, 13)
            v.tensor_tensor(posd[:], posd[:], posm[:].unsqueeze(2).to_broadcast([128, 2, DUP]),
                            ALU.subtract).then_inc(setup_dve, 1)
            v.tensor_tensor(oobd[:], oobd[:], oobm[:].unsqueeze(2).to_broadcast([128, H, len(OOB)]),
                            ALU.subtract).then_inc(setup_dve, 1)
            dve.wait_ge(setup_act, 7)
            v.tensor_reduce(poss[:], posd[:], op=ALU.add, axis=AX.X).then_inc(setup_dve, 1)
            v.tensor_reduce(oobs[:], oobd[:], op=ALU.add, axis=AX.X).then_inc(setup_dve, 1)
            dve.wait_ge(setup_act, 9)
            v.tensor_tensor(posE[:], posE[:], posm[:], ALU.add).then_inc(setup_dve, 1)
            v.tensor_tensor(oobE[:], oobE[:], oobm[:], ALU.add).then_inc(setup_dve, 1)
            dve.wait_ge(setup_dve, SETUP_DVE)

            def moments(s, e, nb):
                dve.wait_ge(s.sem, s.count(e, "res"))
                for tt in range(TT):
                    v.bn_stats(nb["st"][:, tt, :], nb["y"][:, tt, :]).then_inc(s.done("bn", tt), 1)
                for tt in range(TT):
                    dve.wait_ge(s.sem, s.count(e, "bn", tt))
                    v.memset(nb["tick"][:, tt:tt + 1], 0.0)
                    v.bn_aggr(n_mv[:, nb["row"], tt, :], nb["st"][:, tt, :]).then_inc(s.done("ag", tt), 1)

            def inverse_roots(e, rows, parts):
                nv, ni, nr, ns = n_v[:, rows, :], n_i[:, rows, :], n_r[:, rows, :], n_s[:, rows, :]
                if 0 in parts:
                    v.tensor_scalar(nv, n_mv[:, rows, :, 1], EPS, None, ALU.add).then_inc(dveN.done("ve"), 1)
                    dve.wait_ge(dveN.sem, dveN.count(e, "ve"))
                    v.tensor_scalar(ni, nv.bitcast(I32), 1, None, ALU.logical_shift_right).then_inc(dveN.done("sh"), 1)
                    dve.wait_ge(dveN.sem, dveN.count(e, "sh"))
                    v.tensor_scalar(nr.bitcast(I32), ni, -1.0, float(0x5F3759DF), ALU.mult,
                                    ALU.add).then_inc(dveN.done("mg"), 1)
                for n in range(3):
                    if n + 1 in parts:
                        dve.wait_ge(dveN.sem, dveN.count(e, "nt", 3 * n - 1) if n else dveN.count(e, "mg"))
                        v.tensor_tensor(ns, nr, nr, ALU.mult).then_inc(dveN.done("nt", 3 * n), 1)
                        dve.wait_ge(dveN.sem, dveN.count(e, "nt", 3 * n))
                        v.scalar_tensor_tensor(ns, ns, -0.5, nv, ALU.mult, ALU.mult).then_inc(dveN.done("nt", 3 * n + 1), 1)
                        dve.wait_ge(dveN.sem, dveN.count(e, "nt", 3 * n + 1))
                        v.scalar_tensor_tensor(nr, ns, 1.5, nr, ALU.add, ALU.mult).then_inc(dveN.done("nt", 3 * n + 2), 1)
                if 3 in parts:
                    dve.wait_ge(dveN.sem, dveN.count(e, "nt", 8))
                    v.scalar_tensor_tensor(n_b[:, rows, :], n_mv[:, rows, :, 0], -1.0, nr, ALU.mult,
                                           ALU.mult).then_inc(dveN.done("nb"), 1)

            def gates_rank(both):
                for s, e, gb, bk, p in both:
                    dve.wait_ge(p.sem, p.count(e, "lg"))
                    dve.wait_ge(s.sem, s.count(e - 1, "c"))
                    v.tensor_copy(gb["L"][:].rearrange("p t x -> p (t x)"), bk[:, 0:TT * E]).then_inc(s.done("cp"), 1)
                for s, e, gb, bk, p in both:
                    dve.wait_ge(s.sem, s.count(e, "cp"))
                    v.tensor_reduce(gb["mx"][:], gb["L"][:], op=ALU.max, axis=AX.X).then_inc(s.done("gmx"), 1)
                for s, e, gb, bk, p in both:
                    dve.wait_ge(s.sem, s.count(e, "gmx"))
                    v.tensor_tensor(gb["dl"][:], gb["L"][:], gb["mx"][:].unsqueeze(2).to_broadcast([128, TT, E]),
                                    ALU.subtract).then_inc(s.done("sub"), 1)
                for s, e, gb, bk, p in both:
                    lj = gb["L"][:].unsqueeze(2).to_broadcast([128, TT, E, E])
                    li = gb["L"][:].unsqueeze(3).to_broadcast([128, TT, E, E])
                    o = [gb[x][:].rearrange("p (t i j) -> p t i j", t=TT, i=E) for x in ("gt", "eq")]
                    v.tensor_tensor(o[0], lj, li, ALU.is_gt).then_inc(s.done("gt"), 1)
                    v.tensor_tensor(o[1], lj, li, ALU.is_equal).then_inc(s.done("eq"), 1)
                for s, e, gb, bk, p in both:
                    dve.wait_ge(s.sem, s.count(e, "eq"))
                    v.tensor_tensor(gb["eq"][:], gb["eq"][:], tri[:], ALU.mult).then_inc(s.done("eqt"), 1)
                for s, e, gb, bk, p in both:
                    dve.wait_ge(s.sem, s.count(e, "eqt"))
                    v.tensor_tensor(gb["gt"][:], gb["gt"][:], gb["eq"][:], ALU.add).then_inc(s.done("add"), 1)
                for s, e, gb, bk, p in both:
                    dve.wait_ge(s.sem, s.count(e, "add"))
                    v.tensor_reduce(gb["rank"][:].rearrange("p t x -> p (t x)"),
                                    gb["gt"][:].rearrange("p (a j) -> p a j", j=E), op=ALU.add,
                                    axis=AX.X).then_inc(s.done("rank"), 1)

            def gates_weigh(both):
                for s, e, gb, acts, peS, over in both:
                    dve.wait_ge(acts.sem, acts.count(e, "ge"))
                    dve.wait_ge(s.sem, s.count(e, "rank"))
                    v.scalar_tensor_tensor(gb["sel"][:], gb["rank"][:], 1.5, gb["ge"][:], ALU.is_lt,
                                           ALU.mult).then_inc(s.done("sel"), 1)
                for s, e, gb, acts, peS, over in both:
                    dve.wait_ge(s.sem, s.count(e, "sel"))
                    v.tensor_reduce(gb["sum"][:], gb[over][:], op=ALU.add, axis=AX.X).then_inc(s.done("sum"), 1)
                for s, e, gb, acts, peS, over in both:
                    dve.wait_ge(s.sem, s.count(e, "sum"))
                    v.reciprocal(gb["rec"][:], gb["sum"][:]).then_inc(s.done("rec"), 1)
                for s, e, gb, acts, peS, over in both:
                    dve.wait_ge(s.sem, s.count(e, "rec"))
                    dve.wait_ge(peS.sem, peS.count(e - 1, "cT"))
                    v.tensor_tensor(gb["c"][:, :, 0:E], gb["sel"][:], gb["rec"][:].unsqueeze(2).to_broadcast([128, TT, E]),
                                    ALU.mult).then_inc(s.done("c"), 1)

            def one(t, par, key):
                r = stages(t)
                odd = 1 - par
                present = [n for n, st in enumerate(NORMS) if r[st] is not None]
                rows = slice(present[0], present[-1] + 1) if present else None
                eN = t - LAG["A3n"]
                for what, n in ORDER["dve"]:
                    if what == "A1.rest" and (e := r["A1"]) is not None:
                        dve.wait_ge(actA1.sem, actA1.count(e, "hi", 1))
                        v.tensor_tensor(rest[:], qk[:], parts[:, :, 0, :], ALU.subtract).then_inc(dveA1.done("rest"), 1)
                    if what == "A1.v" and (e := r["A1"]) is not None:
                        dve.wait_ge(peA1.sem, peA1.count(e, "v"))
                        dve.wait_ge(pePV.sem, pePV.count(e - 2, "PV", 3))
                        o = bass.AP(Vz[par], 0, [[TT * H * 32, 128], [64, TT * H // 2], [40, 2], [1, HD]])
                        v.tensor_tensor(o, b7[:, 0:T].rearrange("p (a r d) -> p a r d", r=2, d=HD),
                                        bv0[:].rearrange("p t c -> p (t c)").rearrange("p (a r d) -> p a r d", r=2, d=HD),
                                        ALU.add).then_inc(dveA1.done("v"), 1)
                    if what == "A1.mid" and (e := r["A1"]) is not None:
                        dve.wait_ge(st_part[1], dma_count(e - 1))
                        dve.wait_ge(dveA1.sem, dveA1.count(e, "rest"))
                        v.tensor_copy(parts[:, :, 1, :], rest[:]).then_inc(dveA1.done("mid"), 1)
                    if what == "A1.lo" and (e := r["A1"]) is not None:
                        dve.wait_ge(st_part[2], dma_count(e - 1))
                        dve.wait_ge(dveA1.sem, dveA1.count(e, "mid"))
                        v.tensor_tensor(parts[:, :, 2, :], rest[:], parts[:, :, 1, :],
                                        ALU.subtract).then_inc(dveA1.done("lo"), 1)
                    if what == "C2.pv" and (e := r["C2"]) is not None:
                        if n == 0:
                            dve.wait_ge(ld_w, dma_count(e, N_W))
                            dve.wait_ge(actC1.sem, actC1.count(e, "v"))
                        p = PV_ORDER[n]
                        v.tensor_tensor(pv[:, 2 * p:2 * p + 2, :], wb[:, 2 * p:2 * p + 2, :], shifted(vC, p),
                                        ALU.mult).then_inc(dveC2.done("pv", n), 1)
                    if what == "A3.rec" and (e := r["A3"]) is not None:
                        dve.wait_ge(peA3.sem, peA3.count(e, "pT"))
                        dve.wait_ge(dveA3.sem, dveA3.count(e - 1, "num", 1))
                        s_ = b6[:].rearrange("p (q j c) -> p q j c", q=2 * TT, j=4)
                        v.reciprocal(rden[:], s_[:, :, :, 16:18]).then_inc(dveA3.done("rec"), 1)
                    if what == "A3.num" and (e := r["A3"]) is not None:
                        dve.wait_ge(dveA3.sem, dveA3.count(e, "rec"))
                        dve.wait_ge(peA3.sem, peA3.count(e - 1, "aT"))
                        s_ = b6[:].rearrange("p (q j c) -> p q j c", q=2 * TT, j=4)
                        o = attn[:].rearrange("p t (a j r d) -> p (t a) j r d", a=2, j=4, r=2)
                        for i in range(2):
                            v.tensor_tensor(o[:, :, :, i, :], s_[:, :, :, 8 * i:8 * i + 8],
                                            rden[:, :, :, i].unsqueeze(3).to_broadcast([128, 2 * TT, 4, HD]),
                                            ALU.mult).then_inc(dveA3.done("num", i), 1)
                    if what == "A3.res" and (e := r["A3"]) is not None:
                        dve.wait_ge(peA3.sem, peA3.count(e, "out"))
                        dve.wait_ge(poolA3.sem, poolA3.count(e, "xbo"))
                        dve.wait_ge(actNA.sem, actNA.count(e - 1, "nm", 1))
                        v.tensor_tensor(nA["y"][:].rearrange("p t c -> p (t c)"), b6[:, 0:T],
                                        x0b[:].rearrange("p t c -> p (t c)"), ALU.add).then_inc(dveA3.done("res"), 1)
                        moments(dveA3, e, nA)
                    if what == "D2.res" and (e := r["D2"]) is not None:
                        dve.wait_ge(peD.sem, peD.count(e, "y", 1))
                        dve.wait_ge(actND.sem, actND.count(e - 1, "nm", 1))
                        v.tensor_tensor(nD["y"][:].rearrange("p t c -> p (t c)"), b6[:, 0:T],
                                        x3[:].rearrange("p t c -> p (t c)"), ALU.add).then_inc(dveDn.done("res"), 1)
                        moments(dveDn, e, nD)
                    if what == "B2.res" and (e := r["B2"]) is not None:
                        dve.wait_ge(peZ.sem, peZ.count(e, "z", 1))
                        dve.wait_ge(actNB.sem, actNB.count(e - 1, "nm", 1))
                        v.tensor_tensor(nB["y"][:].rearrange("p t c -> p (t c)"), bPV[:, 0:T],
                                        x1[:].rearrange("p t c -> p (t c)"), ALU.add).then_inc(dveBn.done("res"), 1)
                        moments(dveBn, e, nB)
                    if what == "N.root" and n == 0 and present:
                        for m, (s, actN) in enumerate(((dveA3, actNA), (dveBn, actNB), (dveC2n, actNC), (dveDn, actND))):
                            if m in present:
                                dve.wait_ge(s.sem, s.count(r[NORMS[m]], "ag", 1))
                                dve.wait_ge(actN.sem, actN.count(r[NORMS[m]] - 1, "nm", 1))
                        inverse_roots(eN, rows, (0,))
                    if what == "C2.add" and n == 0 and (e := r["C2"]) is not None:
                        dve.wait_ge(poolC2.sem, poolC2.count(e, "add", 1))
                        v.tensor_tensor(pv[:, 0:4, :], pv[:, 0:4, :], pv[:, 4:8, :], ALU.add).then_inc(dveC2.done("add", 0), 1)
                    if what == "N.root" and n == 1 and present:
                        inverse_roots(eN, rows, (1,))
                    if what == "C2.add" and n == 1 and (e := r["C2"]) is not None:
                        dve.wait_ge(dveC2.sem, dveC2.count(e, "add", 0))
                        v.tensor_tensor(pv[:, 0:2, :], pv[:, 0:2, :], pv[:, 2:4, :], ALU.add).then_inc(dveC2.done("add", 1), 1)
                    if what == "N.root" and n == 2 and present:
                        inverse_roots(eN, rows, (2,))
                    if what == "N.root" and n == 3 and present:
                        inverse_roots(eN, rows, (3,))
                    if what == "C2.add" and n == 2 and (e := r["C2"]) is not None:
                        dve.wait_ge(dveC2.sem, dveC2.count(e, "add", 1))
                        v.tensor_tensor(pv[:, 0, :], pv[:, 0, :], pv[:, 1, :], ALU.add).then_inc(dveC2.done("add", 2), 1)
                    if what == "C2.gt" and (e := r["C2"]) is not None:
                        dve.wait_ge(dveC2.sem, dveC2.count(e, "add", 2))
                        dve.wait_ge(actC1.sem, actC1.count(e, "g"))
                        dve.wait_ge(peC2.sem, peC2.count(e - 1, "out"))
                        v.scalar_tensor_tensor(gat[:], tg[:], 1.0, pv[:, 0, :], ALU.add,
                                               ALU.mult).then_inc(dveC2.done("gt"), 1)
                    if what == "C2.res" and (e := r["C2"]) is not None:
                        dve.wait_ge(peC2.sem, peC2.count(e, "out"))
                        dve.wait_ge(poolC2.sem, poolC2.count(e, "xb"))
                        dve.wait_ge(actNC.sem, actNC.count(e - 1, "nm", 1))
                        v.tensor_tensor(nC["y"][:].rearrange("p t c -> p (t c)"), b7[:, 0:T],
                                        x2b[:].rearrange("p t c -> p (t c)"), ALU.add).then_inc(dveC2n.done("res"), 1)
                        moments(dveC2n, e, nC)
                    if what == "G.rank":
                        both = [(s, r[st], gb, bk, p) for st, s, gb, bk, p in
                                (("B", dveBg, gB, b6, peB), ("D", dveDg, gD, b6, peD)) if r[st] is not None]
                        gates_rank(both)
                    if what == "G.weigh":
                        both = [(s, r[st], gb, a, p, over) for st, s, gb, a, p, over in
                                (("B", dveBg, gB, actB, peB, "ge"), ("D", dveDg, gD, actD, peD, "sel"))
                                if r[st] is not None]
                        gates_weigh(both)
                    if what == "A1.max" and (e := r["A1"]) is not None:
                        k = n
                        dve.wait_ge(peA1.sem, peA1.count(e, "S", k))
                        if k == 0:
                            dve.wait_ge(dveM.sem, dveM.count(e - 1, "neg"))
                        v.tensor_reduce(mx[:, :, k], bS[k % 2][:].rearrange("p (a b) -> p a b", a=TT), op=ALU.max,
                                        axis=AX.X).then_inc(dveA1.done("max", k), 1)
                    if what == "B.wu" and (e := r["B"]) is not None:
                        x = expert(n)
                        dve.wait_ge(actB.sem, actB.count(e, "ab", 2 * n + 1))
                        if n >= 2:
                            dve.wait_ge(poolB.sem, poolB.count(e, "h", n - 2))
                        else:
                            dve.wait_ge(poolB.sem, poolB.count(e - 1, "h", n + 7))
                        bAB = bTU[turn_bank("ab", n)]
                        if n == 1:
                            dve.wait_ge(ld_cB, dma_count(e))
                        if n == 0:
                            i = v.tensor_scalar(wa[0][:], bAB[:, 0:T], b1[:, x:x + 1], None, ALU.add)
                        else:
                            i = v.scalar_tensor_tensor(wa[n % 2][:].rearrange("p (t n) -> p t n", t=TT),
                                                       bAB[:, 0:T].rearrange("p (t n) -> p t n", t=TT), b1[:, x:x + 1],
                                                       gB["cb"][:, :, x, :], ALU.add, ALU.mult)
                        i.then_inc(dveB.done("wu", 2 * n), 1)
                        v.scalar_tensor_tensor(ub[n % 2][:], th[n % 2][:], 1.0, bb[n % 2][:], ALU.add,
                                               ALU.mult).then_inc(dveB.done("wu", 2 * n + 1), 1)
                    if what == "C1.mx" and (e := r["C1"]) is not None:
                        dve.wait_ge(peC1.sem, peC1.count(e, "scT"))
                        sc_ = b7[:].rearrange("p (t a h) -> p t a h", t=TT, h=H)
                        v.tensor_reduce(mC[:], sc_.rearrange("p t a h -> p t h a"), op=ALU.max,
                                        axis=AX.X).then_inc(dveC1.done("mx"), 1)
                        dve.wait_ge(dveC1.sem, dveC1.count(e, "mx"))
                        ob = oobE[:].unsqueeze(1).to_broadcast([128, TT, H])
                        v.tensor_tensor(mC2[:], mC[:], ob, ALU.max).then_inc(dveC1.done("m2"), 1)
                        dve.wait_ge(dveC1.sem, dveC1.count(e, "m2"))
                        dve.wait_ge(actC1.sem, actC1.count(e - 1, "exp"))
                        v.tensor_tensor(ds[:, :, 0:NS, :], sc_, mC2[:].unsqueeze(2).to_broadcast([128, TT, NS, H]),
                                        ALU.subtract).then_inc(dveC1.done("sub"), 1)
                        v.tensor_tensor(ds[:, :, NS, :], ob, mC2[:], ALU.subtract).then_inc(dveC1.done("subo"), 1)
                    if what == "C1.sum" and (e := r["C1"]) is not None:
                        dve.wait_ge(actC1.sem, actC1.count(e, "exp"))
                        v.tensor_reduce(sC[:], es[:].rearrange("p t a h -> p t h a"), op=ALU.add,
                                        axis=AX.X).then_inc(dveC1.done("sum"), 1)
                        dve.wait_ge(dveC1.sem, dveC1.count(e, "sum"))
                        v.reciprocal(rC[:], sC[:]).then_inc(dveC1.done("rec"), 1)
                        dve.wait_ge(dveC1.sem, dveC1.count(e, "rec"))
                        dve.wait_ge(peC1.sem, peC1.count(e - 1, "wT"))
                        v.tensor_tensor(wn[:], es[:, :, 0:NS, :], rC[:].unsqueeze(2).to_broadcast([128, TT, NS, H]),
                                        ALU.mult).then_inc(dveC1.done("w"), 1)
                    if what == "M.neg" and (e := r["M"]) is not None:
                        dve.wait_ge(dveA1.sem, dveA1.count(e, "max", 15))
                        dve.wait_ge(peM.sem, peM.count(e - 1, "mT"))
                        v.tensor_scalar(mneg[:], mx[:], -1.0, None, ALU.mult).then_inc(dveM.done("neg"), 1)

            passes(dve, one)

        @block.gpsimd
        def _(pool):
            tt_ = nc.gpsimd.tensor_tensor
            pool.wait_ge(ld_const, 16 * N_CONST)
            pool.wait_ge(setup_dve, SETUP_DVE)

            def one(t, par, key):
                r = stages(t)
                odd = 1 - par
                for what, n in ORDER["pool"]:
                    if what == "A3.xbo":
                        if (e := r["A3"]) is not None:
                            pool.wait_ge(ld_x, dma_count(e))
                            pool.wait_ge(dveA3.sem, dveA3.count(e - 1, "res"))
                            tt_(x0b[:], x0[:], bo0[:], ALU.add).then_inc(poolA3.done("xbo"), 1)
                    if what == "C2.add" and (e := r["C2"]) is not None:
                        pool.wait_ge(dveC2.sem, dveC2.count(e, "pv", 4 * n + 3))
                        tt_(pv[:, 4 * n:4 * n + 4, :], pv[:, 4 * n:4 * n + 4, :], pv[:, 4 * n + 8:4 * n + 12, :],
                            ALU.add).then_inc(poolC2.done("add", n), 1)
                    if what == "C1.prod" and (e := r["C1"]) is not None:
                        if n == 0:
                            pool.wait_ge(actC1.sem, actC1.count(e, "k"))
                            pool.wait_ge(peC1.sem, peC1.count(e - 1, "sc"))
                            pool.wait_ge(peD.sem, peD.count(e + LAG["C1"] - LAG["D2"], "y"))
                        p = n
                        tt_(prod[:, 2 * p:2 * p + 2, :], shifted(kC, p), qC[:].unsqueeze(1).to_broadcast([128, 2, T]),
                            ALU.mult).then_inc(poolC1.done("prod", p), 1)
                    if what == "C2.xb" and (e := r["C1"]) is not None:
                        pool.wait_ge(dveC2n.sem, dveC2n.count(e - 1, "res"))
                        pool.wait_ge(actNB.sem, actNB.count(e, "nm", 1))
                        tt_(x2b[:], x2[:], boc[:], ALU.add).then_inc(poolC2.done("xb"), 1)
                    if what == "D.xs" and (e := r["D"]) is not None:
                        i = n
                        if i == 0:
                            pool.wait_ge(ld_cD, dma_count(e))
                            pool.wait_ge(actD.sem, actD.count(e, "xT"))
                            pool.wait_ge(peD.sem, peD.count(e - 1, "y", 1))
                            if (c1 := r["C1"]) is not None:
                                pool.wait_ge(peC1.sem, peC1.count(c1, "sc"))
                        tt_(xs[:, 2 * i:2 * i + 2, :].rearrange("p x (t n) -> p x t n", t=TT),
                            gD["cb"][:, :, 2 * i:2 * i + 2, :].rearrange("p t x n -> p x t n"),
                            x3T[:].rearrange("p (t n) -> p t n", t=TT).unsqueeze(1).to_broadcast([128, 2, TT, 128]),
                            ALU.mult).then_inc(poolD.done("xs", i), 1)
                    if what == "B.h" and (e := r["B"]) is not None:
                        pool.wait_ge(dveB.sem, dveB.count(e, "wu", 2 * n + 1))
                        if n == 0:
                            pool.wait_ge(peZ.sem, peZ.count(e - 1, "z", 1))
                        tt_(h9[:, n, :], wa[n % 2][:], ub[n % 2][:], ALU.mult).then_inc(poolB.done("h", n), 1)

            passes(pool, one)


def distance_tables():
    slopes = np.power(np.float32(2.0), np.float32(8.0) * np.arange(0, -H, -1, dtype=np.float32) / np.float32(H))
    i = np.arange(128)
    d = -slopes[:, None, None].astype(np.float64) * np.abs(i[:, None] - i[None, :])
    hi = d.astype(np.float16)
    lo = (d - hi.astype(np.float64)).astype(np.float16)
    dist = np.stack([hi, lo], 1).transpose(2, 0, 1, 3)

    def bf16(a):
        u = np.asarray(a, np.float32).view(np.uint32)
        u = ((u + 0x7FFF + ((u >> 16) & 1)) >> 16).astype(np.uint32)
        return u.astype(np.uint16), (u << 16).view(np.float32)

    def three(a):
        out, left = [], np.asarray(a, np.float64)
        for _ in range(3):
            bits, val = bf16(left.astype(np.float32))
            out.append(bits)
            left = left - val
        return out

    one = bf16(np.ones(1))[0][0]
    t = np.arange(T)
    first, second = t < 128, t >= 128
    rows = np.zeros((ROW_M + 1 - ROW_D, 2, H, T), np.uint16)
    far = slopes[:, None].astype(np.float64) * np.abs(t - 128)
    for n, part in enumerate(three(-far)):
        rows[n, 0] = np.where(first, one, 0)
        rows[n, 1] = np.where(second, part, 0)
        rows[3 + n, 0] = np.where(first, part, 0)
        rows[3 + n, 1] = np.where(second, one, 0)
        rows[6 + n, 0] = np.where(second, one, 0)
        rows[6 + n, 1] = np.where(first, part, 0)
        rows[9 + n, 0] = np.where(second, part, 0)
        rows[9 + n, 1] = np.where(first, one, 0)
    rows[ROW_M - ROW_D, 1] = one
    identb = np.zeros((128, 128), np.uint16)
    identb[i, i] = one
    return np.ascontiguousarray(dist), rows, identb


def kernel(**inputs):
    from concourse import bacc
    from concourse.bass_utils import run_bass_kernel_spmd

    a = {k: np.asarray(v) for k, v in inputs.items()}
    dh = np.arange(D).reshape(H, HD).T.reshape(-1)
    ajrd = np.arange(D).reshape(4, 2, 2, HD).transpose(1, 0, 2, 3).reshape(-1)
    w, b = a["L0_attn_W_qkv"], a["L0_attn_b_qkv"]
    cw, cb = a["L1_attn_w_qkv"], a["L1_attn_b_qkv"]
    pos = a["L1_attn_pos_bias"]
    posd = np.full((128, 2, DUP), -1e30, pos.dtype)
    for p, pair in enumerate(PAIRS):
        for o2, shift in enumerate(pair):
            for n, i in enumerate(i for i, o in enumerate(OFFSETS) if o == shift):
                row = 32 * (p % 4) + 16 * o2
                posd[row:row + H, p // 4, n] = pos[i]
    dist, rows, identb = distance_tables()
    hsum = np.zeros((128, 2, 32), np.float32)
    for o2 in range(2):
        for p in range(128):
            hsum[p, o2, 16 * o2 + p % H] = 1
    b2 = np.zeros((128, TT, D), np.float32)
    for tt in range(TT):
        b2[64 * tt:64 * tt + E, tt] = a["L0_ffn_b2"]
        b2[64 * tt + E, tt] = a["L0_ffn_sb2"]
    ii = np.arange(E)
    arrays = {
        "x": a["L0_attn_x"],
        "xT": a["L0_attn_x"].reshape(B * T, D).T,
        "wqk0": np.stack([w[:D][dh].T, w[D:2 * D][dh].T], 1),
        "wv0": w[2 * D:].T,
        "wo0": a["L0_attn_W_out"].T[ajrd],
        "bqk0": np.stack([b[:D][dh], b[D:2 * D][dh]], 1),
        "bv0": b[None, 2 * D:],
        "bo0": a["L0_attn_b_out"][None],
        "gw0": a["L0_ffn_gate_w"].T,
        "w13": np.stack([np.concatenate([a["L0_ffn_w1"], a["L0_ffn_sw1"][None]]),
                         np.concatenate([a["L0_ffn_w3"], a["L0_ffn_sw3"][None]])], 1).transpose(2, 0, 1, 3),
        "w2": np.concatenate([a["L0_ffn_w2"], a["L0_ffn_sw2"][None]]).transpose(1, 0, 2),
        "b1": np.concatenate([a["L0_ffn_b1"], a["L0_ffn_sb1"][None]]).T,
        "b3": np.concatenate([a["L0_ffn_b3"], a["L0_ffn_sb3"][None]]).T,
        "b2": b2,
        "wc": np.stack([cw[:, :D][:, dh], cw[:, D:2 * D][:, dh], cw[:, 2 * D:][:, dh],
                        a["L1_attn_w_gate"][:, dh]], 1),
        "bc": np.stack([cb[:D][dh], cb[D:2 * D][dh], cb[2 * D:][dh], a["L1_attn_b_gate"][dh]], 1),
        "woc": a["L1_attn_w_out"][dh],
        "boc": a["L1_attn_b_out"][None],
        "gw1": a["L1_ffn_gate_w"].T,
        "ew": a["L1_ffn_expert_w"].transpose(2, 0, 1),
        "posd": posd,
        "oobd": np.broadcast_to(pos[OOB].T, (128, H, len(OOB))),
        "ident": np.eye(128, dtype=np.float32),
        "identh": np.eye(128, dtype=np.float16),
        "identb": identb,
        "dist": dist,
        "rows": rows,
        "hsum": hsum,
        "tri": np.broadcast_to((ii[None, :] < ii[:, None]).astype(np.float32).reshape(1, 1, -1),
                               (128, TT, E * E)).reshape(128, -1),
    }
    nc = bacc.Bacc("TRN2", target_bir_lowering=False, num_devices=1)
    feeds, aps = {}, {}
    for name, x in arrays.items():
        x = np.ascontiguousarray(x)
        feeds[f"in_{name}"] = x
        aps[name] = nc.dram_tensor(f"in_{name}", x.shape, mybir.dt.from_np(x.dtype), kind="ExternalInput").ap()
    out = nc.dram_tensor("out_x", (B, T, D), mybir.dt.float32, kind="ExternalOutput").ap()
    network(nc, aps, out)
    return run_bass_kernel_spmd(nc, [feeds], core_ids=[0]).results[0]["out_x"]
```
